# Optimizing a Trainium2 kernel written in Bass

```python
import numpy as np
import jax
import jax.numpy as jnp

def _softmax(x, axis=-1):
    return jax.nn.softmax(x, axis=axis)

def _gelu(x):
    return jax.nn.gelu(x, approximate=True)

def _silu(x):
    return jax.nn.silu(x)

def _sigmoid(x):
    return jax.nn.sigmoid(x)

def _layernorm(x, axis=-1, eps=1e-05):
    m = jnp.mean(x, axis=axis, keepdims=True)
    v = jnp.var(x, axis=axis, keepdims=True)
    return (x - m) / jnp.sqrt(v + eps)

def _scatter_add(tgt, idx, src, axis=0):
    return tgt.at[idx].add(src)

def _segment_sum(src, seg, n):
    return jax.ops.segment_sum(src, seg, n)
kernel_name = 'mk_sandwich_d2_jaxref_r4_745088'

def setup_inputs(seed: int=0):
    np.random.seed(seed)
    _w = jnp.asarray

    def _L0_attn_setup():
        import jax, jax.numpy as jnp
        import numpy as np
        EMBED_DIM = 256
        NUM_HEADS = 16
        HEAD_DIM = EMBED_DIM // NUM_HEADS
        key = jax.random.key(seed)
        k1, k2, k3 = jax.random.split(key, 3)
        inputs = jax.random.normal(k1, (4, 512, EMBED_DIM), dtype=jnp.float32)
        rotation_params = jax.random.normal(k2, (NUM_HEADS, HEAD_DIM), dtype=jnp.float32)
        entangle_params = jax.random.normal(k3, (NUM_HEADS, HEAD_DIM), dtype=jnp.float32)
        return {'inputs': inputs, 'rotation_params': rotation_params, 'entangle_params': entangle_params}
    _L0_attn_in = _L0_attn_setup()

    def _L0_ffn_setup():
        import jax, jax.numpy as jnp
        import numpy as np
        DIM = 256

        def _reference_tuple_inner(x, W_r, W_k, W_v, mu_r, mu_k):
            B, T, C = x.shape
            x_prev = jnp.concatenate([jnp.zeros((B, 1, C), x.dtype), x[:, :-1, :]], axis=1)
            xr = mu_r * x + (1.0 - mu_r) * x_prev
            xk = mu_k * x + (1.0 - mu_k) * x_prev
            r = jax.nn.sigmoid(jnp.einsum('btc,dc->btd', xr, W_r))
            k = jnp.einsum('btc,dc->btd', xk, W_k)
            k_act = jnp.square(jax.nn.relu(k))
            out = r * jnp.einsum('btc,dc->btd', k_act, W_v)
            new_state = x[:, -1, :]
            return (out, new_state)
        key = jax.random.key(seed)
        ks = jax.random.split(key, 6)
        B, T, C = (8, 512, DIM)
        x = jax.random.normal(ks[0], (B, T, C), dtype=jnp.float32)
        s = 1.0 / np.sqrt(C)
        W_r = jax.random.uniform(ks[1], (C, C), jnp.float32, -s, s)
        W_k = jax.random.uniform(ks[2], (C, C), jnp.float32, -s, s)
        W_v = jax.random.uniform(ks[3], (C, C), jnp.float32, -s, s)
        mu_r = jax.random.uniform(ks[4], (C,), jnp.float32)
        mu_k = jax.random.uniform(ks[5], (C,), jnp.float32)
        return {'x': x, 'W_r': W_r, 'W_k': W_k, 'W_v': W_v, 'mu_r': mu_r, 'mu_k': mu_k}
    _L0_ffn_in = _L0_ffn_setup()

    def _L1_attn_setup():
        import jax, jax.numpy as jnp
        import numpy as np
        D_MODEL = 256
        NHEAD = 8
        HEAD_DIM = D_MODEL // NHEAD
        D_FF = 1024
        EPS_ATTN = 1e-06
        EPS_LN = 1e-05

        def _layernorm(x, g, b):
            mu = jnp.mean(x, axis=-1, keepdims=True)
            var = jnp.var(x, axis=-1, keepdims=True)
            return (x - mu) * jax.lax.rsqrt(var + EPS_LN) * g + b

        def _linear_attention(q, k, v):
            Q = jax.nn.elu(q) + 1.0
            K = jax.nn.elu(k) + 1.0
            v_length = v.shape[1]
            v = v / v_length
            KV = jnp.einsum('nshd,nshv->nhdv', K, v)
            Z = 1.0 / (jnp.einsum('nlhd,nhd->nlh', Q, K.sum(axis=1)) + EPS_ATTN)
            out = jnp.einsum('nlhd,nhdv,nlh->nlhv', Q, KV, Z) * v_length
            return out
        key = jax.random.key(seed)
        ks = jax.random.split(key, 12)
        s = 1.0 / np.sqrt(D_MODEL)
        sf = 1.0 / np.sqrt(D_FF)
        return {'x': jax.random.normal(ks[0], (2, 1024, D_MODEL), jnp.float32), 'wq': jax.random.normal(ks[1], (D_MODEL, D_MODEL), jnp.float32) * s, 'wk': jax.random.normal(ks[2], (D_MODEL, D_MODEL), jnp.float32) * s, 'wv': jax.random.normal(ks[3], (D_MODEL, D_MODEL), jnp.float32) * s, 'w1': jax.random.normal(ks[4], (D_FF, D_MODEL), jnp.float32) * s, 'b1': jnp.zeros((D_FF,), jnp.float32), 'w2': jax.random.normal(ks[5], (D_MODEL, D_FF), jnp.float32) * sf, 'b2': jnp.zeros((D_MODEL,), jnp.float32), 'g1': jnp.ones((D_MODEL,), jnp.float32), 'be1': jnp.zeros((D_MODEL,), jnp.float32), 'g2': jnp.ones((D_MODEL,), jnp.float32), 'be2': jnp.zeros((D_MODEL,), jnp.float32)}
    _L1_attn_in = _L1_attn_setup()

    def _L1_ffn_setup():
        import jax, jax.numpy as jnp
        import numpy as np
        DIM = 256
        HIDDEN = 768
        SCALE = 1.0 / 127.0

        def _dequant(w_int, dtype):
            return w_int.astype(dtype) * jnp.asarray(SCALE, dtype)
        key = jax.random.key(seed)
        k_x, k_g, k_u, k_d = jax.random.split(key, 4)
        x = jax.random.normal(k_x, (4, 512, DIM), dtype=jnp.float32)
        w_gate = jax.random.randint(k_g, (HIDDEN, DIM), -127, 128, dtype=jnp.int32)
        w_up = jax.random.randint(k_u, (HIDDEN, DIM), -127, 128, dtype=jnp.int32)
        w_down = jax.random.randint(k_d, (DIM, HIDDEN), -127, 128, dtype=jnp.int32)
        return {'x': x, 'w_gate': w_gate, 'w_up': w_up, 'w_down': w_down}
    _L1_ffn_in = _L1_ffn_setup()
    _d = {'L0_attn_inputs': _L0_attn_in['inputs'], 'L0_attn_rotation_params': _L0_attn_in['rotation_params'], 'L0_attn_entangle_params': _L0_attn_in['entangle_params'], 'L0_ffn_W_r': _L0_ffn_in['W_r'], 'L0_ffn_W_k': _L0_ffn_in['W_k'], 'L0_ffn_W_v': _L0_ffn_in['W_v'], 'L0_ffn_mu_r': _L0_ffn_in['mu_r'], 'L0_ffn_mu_k': _L0_ffn_in['mu_k'], 'L1_attn_wq': _L1_attn_in['wq'], 'L1_attn_wk': _L1_attn_in['wk'], 'L1_attn_wv': _L1_attn_in['wv'], 'L1_attn_w1': _L1_attn_in['w1'], 'L1_attn_b1': _L1_attn_in['b1'], 'L1_attn_w2': _L1_attn_in['w2'], 'L1_attn_b2': _L1_attn_in['b2'], 'L1_attn_g1': _L1_attn_in['g1'], 'L1_attn_be1': _L1_attn_in['be1'], 'L1_attn_g2': _L1_attn_in['g2'], 'L1_attn_be2': _L1_attn_in['be2'], 'L1_ffn_w_gate': _L1_ffn_in['w_gate'], 'L1_ffn_w_up': _L1_ffn_in['w_up'], 'L1_ffn_w_down': _L1_ffn_in['w_down']}
    _x0 = _d['L0_attn_inputs']
    _d['L0_attn_inputs'] = jax.random.normal(jax.random.fold_in(jax.random.key(seed), 1), (4, 2048, 256), dtype=_x0.dtype)
    del _x0
    return _d

def reference(L0_attn_inputs, L0_attn_rotation_params, L0_attn_entangle_params, L0_ffn_W_r, L0_ffn_W_k, L0_ffn_W_v, L0_ffn_mu_r, L0_ffn_mu_k, L1_attn_wq, L1_attn_wk, L1_attn_wv, L1_attn_w1, L1_attn_b1, L1_attn_w2, L1_attn_b2, L1_attn_g1, L1_attn_be1, L1_attn_g2, L1_attn_be2, L1_ffn_w_gate, L1_ffn_w_up, L1_ffn_w_down):

    def _L0_attn_ref(inputs, rotation_params, entangle_params):
        import jax, jax.numpy as jnp
        import numpy as np
        EMBED_DIM = 256
        NUM_HEADS = 16
        HEAD_DIM = EMBED_DIM // NUM_HEADS
        B, T, _ = inputs.shape
        x = inputs.reshape(B, T, NUM_HEADS, HEAD_DIM).transpose(0, 2, 1, 3)
        q = x * rotation_params[None, :, None, :]
        k = x * entangle_params[None, :, None, :]
        v = x
        scale = 1.0 / np.sqrt(HEAD_DIM).astype(np.float32)
        attn_scores = jnp.einsum('bhid,bhjd->bhij', q, k) * scale
        attn_weights = jax.nn.softmax(attn_scores, axis=-1)
        out = jnp.einsum('bhij,bhjd->bhid', attn_weights, v)
        out = out.transpose(0, 2, 1, 3).reshape(B, T, EMBED_DIM)
        return out

    def _L0_ffn_ref(x, W_r, W_k, W_v, mu_r, mu_k):
        import jax, jax.numpy as jnp
        import numpy as np
        DIM = 256

        def _reference_tuple_inner(x, W_r, W_k, W_v, mu_r, mu_k):
            B, T, C = x.shape
            x_prev = jnp.concatenate([jnp.zeros((B, 1, C), x.dtype), x[:, :-1, :]], axis=1)
            xr = mu_r * x + (1.0 - mu_r) * x_prev
            xk = mu_k * x + (1.0 - mu_k) * x_prev
            r = jax.nn.sigmoid(jnp.einsum('btc,dc->btd', xr, W_r))
            k = jnp.einsum('btc,dc->btd', xk, W_k)
            k_act = jnp.square(jax.nn.relu(k))
            out = r * jnp.einsum('btc,dc->btd', k_act, W_v)
            new_state = x[:, -1, :]
            return (out, new_state)
        return _reference_tuple_inner(x, W_r, W_k, W_v, mu_r, mu_k)[0]

    def _L1_attn_ref(x, wq, wk, wv, w1, b1, w2, b2, g1, be1, g2, be2):
        import jax, jax.numpy as jnp
        import numpy as np
        D_MODEL = 256
        NHEAD = 8
        HEAD_DIM = D_MODEL // NHEAD
        D_FF = 1024
        EPS_ATTN = 1e-06
        EPS_LN = 1e-05

        def _layernorm(x, g, b):
            mu = jnp.mean(x, axis=-1, keepdims=True)
            var = jnp.var(x, axis=-1, keepdims=True)
            return (x - mu) * jax.lax.rsqrt(var + EPS_LN) * g + b

        def _linear_attention(q, k, v):
            Q = jax.nn.elu(q) + 1.0
            K = jax.nn.elu(k) + 1.0
            v_length = v.shape[1]
            v = v / v_length
            KV = jnp.einsum('nshd,nshv->nhdv', K, v)
            Z = 1.0 / (jnp.einsum('nlhd,nhd->nlh', Q, K.sum(axis=1)) + EPS_ATTN)
            out = jnp.einsum('nlhd,nhdv,nlh->nlhv', Q, KV, Z) * v_length
            return out
        N, L, C = x.shape
        x2 = _layernorm(x, g1, be1)
        q = (x2 @ wq.T).reshape(N, L, NHEAD, HEAD_DIM)
        k = (x2 @ wk.T).reshape(N, L, NHEAD, HEAD_DIM)
        v = (x2 @ wv.T).reshape(N, L, NHEAD, HEAD_DIM)
        msg = _linear_attention(q, k, v).reshape(N, L, C)
        x = x + msg
        x2 = _layernorm(x, g2, be2)
        h = jax.nn.gelu(x2 @ w1.T + b1, approximate=False)
        x = x + (h @ w2.T + b2)
        return x

    def _L1_ffn_ref(x, w_gate, w_up, w_down):
        import jax, jax.numpy as jnp
        import numpy as np
        DIM = 256
        HIDDEN = 768
        SCALE = 1.0 / 127.0

        def _dequant(w_int, dtype):
            return w_int.astype(dtype) * jnp.asarray(SCALE, dtype)
        wg = _dequant(w_gate, x.dtype)
        wu = _dequant(w_up, x.dtype)
        wd = _dequant(w_down, x.dtype)
        gate = jnp.einsum('bsd,hd->bsh', x, wg)
        up = jnp.einsum('bsd,hd->bsh', x, wu)
        h = jax.nn.silu(gate) * up
        return jnp.einsum('bsh,dh->bsd', h, wd)
    x = L0_attn_inputs
    x = x + _layernorm(_L0_attn_ref(_layernorm(x, axis=-1), L0_attn_rotation_params, L0_attn_entangle_params), axis=-1)
    x = x + _layernorm(_L0_ffn_ref(_layernorm(x, axis=-1), L0_ffn_W_r, L0_ffn_W_k, L0_ffn_W_v, L0_ffn_mu_r, L0_ffn_mu_k), axis=-1)
    x = x + _layernorm(_L1_attn_ref(_layernorm(x, axis=-1), L1_attn_wq, L1_attn_wk, L1_attn_wv, L1_attn_w1, L1_attn_b1, L1_attn_w2, L1_attn_b2, L1_attn_g1, L1_attn_be1, L1_attn_g2, L1_attn_be2), axis=-1)
    x = x + _layernorm(_L1_ffn_ref(_layernorm(x, axis=-1), L1_ffn_w_gate, L1_ffn_w_up, L1_ffn_w_down), axis=-1)
    return x

_drawn_inputs = setup_inputs


def setup_inputs(seed=0):
    import zlib

    import numpy as np

    out = dict(_drawn_inputs(seed))
    spreads = {'L1_attn_b1': (0.0, 0.34),
     'L1_attn_b2': (0.0, 0.1),
     'L1_attn_g1': (1.0, 0.6),
     'L1_attn_be1': (0.0, 0.1),
     'L1_attn_g2': (1.0, 0.2),
     'L1_attn_be2': (0.0, 0.348)}
    factors = {'L1_attn_wq': 8.0, 'L1_attn_wk': 8.0}
    for name, (base, spread) in spreads.items():
        noise = np.random.default_rng([zlib.crc32(name.encode()), seed]).standard_normal(out[name].shape)
        drawn = base * np.exp(spread * noise) if base else spread * noise
        out[name] = jnp.asarray(drawn.astype(out[name].dtype))
    for name, factor in factors.items():
        out[name] = (out[name] * factor).astype(out[name].dtype)
    return out
```

```python
import concourse.bass as bass
from concourse import mybir
from concourse.alu_op_type import AluOpType as ALU
from contextlib import ExitStack

F32, BF16, I32 = mybir.dt.float32, mybir.dt.bfloat16, mybir.dt.int32
ACT = mybir.ActivationFunctionType
AX = mybir.AxisListType

P = 128
B, T, C = 4, 2048, 256
EPS = 1e-5

H, D = 16, 16
NHD = B * H
BB = T // P
NB = B * BB
BANK = 512
QC = T // BANK
HALVES = 2 * BB
ROUNDS = 4
PARTS = 6
BIAS = PARTS * D
SAFE = 75.0
PROBS = 4

N = 512
NC = B * T // N
CB = T // N
K4 = N // P
KC = C // P
F1, F2 = 1024, 768
M1, M2 = F1 // P, F2 // P
HG, DG = 4, 32
KVW = HG * DG + 2
MSGW = HG * DG + HG
EPS_ATTN = 1e-6
DEQUANT = 1.0 / 127.0

FLOAT_WEIGHTS = (("wr", KC, C), ("wk", KC, C), ("wv", KC, C), ("aq", KC, C), ("akv", KC, 2 * C), ("w1", KC, F1), ("w2", M1, C),
                 ("mu_r", 1, KC), ("mu_k", 1, KC), ("b1", 1, M1))
INT_WEIGHTS = (("wg", KC, F2), ("wu", KC, F2), ("wd", M2, C))
ROWS = ("b2", "g1", "be1", "g2", "be2")
FLOAT_COLS = sum(k * n for _, k, n in FLOAT_WEIGHTS)
INT_COLS = sum(k * n for _, k, n in INT_WEIGHTS)


class Chain:

    def __init__(self, eng, sem, base=0):
        self.eng, self.sem, self.base, self.n = eng, sem, base, 0

    def done(self, ins):
        ins.then_inc(self.sem, 1)
        self.n += 1

    def wait(self):
        self.eng.wait_ge(self.sem, self.base + self.n)

    def link(self, ins):
        self.done(ins)
        self.wait()


def softmax_attention(nc, x_in, rot, ent, floats, ints, rows, stage_mem, row_mem, ident, heads_out):
    with ExitStack() as ctx:
        sb = lambda n, s, d=F32: ctx.enter_context(nc.sbuf_tensor(n, s, d))
        sem = lambda n: ctx.enter_context(nc.semaphore(n))

        heads = sb("heads", [P, NHD, BB, D])
        xs = stage_mem[:, :].rearrange("p (k c) -> p k c", c=C)
        slots = xs.shape[1] // BB
        identb = sb("identb", [P, P], BF16)
        neghalf = sb("neghalf", [P, BB])
        rot_row, ent_row = sb("rot_row", [P, C]), sb("ent_row", [P, C])
        rot_heads, ent_heads = sb("rot_heads", [P, NHD, D]), sb("ent_heads", [P, NHD, D])
        stats, mv, ve, rstd = sb("stats", [P, NB, 6]), sb("mv", [P, NB, 2]), sb("ve", [P, NB]), sb("rstd", [P, NB])
        bound, widest = sb("bound", [P, BB]), sb("widest", [P, 2])
        flag = sb("flag", [P, 1], I32)
        probs = sb("probs", [P, PROBS, T])
        q_split, k_split = sb("q_split", [P, BB, P], BF16), sb("k_split", [P, BB, P], BF16)
        qT = [sb(f"qT{i}", [P, T], BF16) for i in range(2)]
        kT = [sb(f"kT{i}", [P, T], BF16) for i in range(2)]
        vals = [sb(f"vals{i}", [P, BB, 32]) for i in range(2)]
        qf, kf, qk, q_rest, k_rest = (sb(n, [P, BB, D]) for n in ("qf", "kf", "qk", "q_rest", "k_rest"))
        sums = sb("sums", [P, BANK])
        recip = sb("recip", [P, QC, QC])
        chunk_max, neg_max = sb("chunk_max", [P, BB, QC]), sb("neg_max", [P, BB, 2])

        ps = ctx.enter_context(nc.psum_tensor("ps", [P, 8, BANK], F32))
        SCORES = [ps[:, 2 * s:2 * s + 2, :].rearrange("p a n -> p (a n)") for s in range(3)]
        ACC = ps[:, 6, :]
        TURN = ps[:, 7, :]
        TURNB = TURN.bitcast(BF16)

        rot_loaded, weights_loaded, weights_ready = sem("rot_loaded"), sem("weights_loaded"), sem("weights_ready")
        x_loaded = [sem(f"x_loaded{b}") for b in range(B)]
        pool_init, consts, static_ready = sem("pool_init"), sem("consts"), sem("static_ready")
        var_ready, rstd_ready, normed, norm_step = sem("var_ready"), sem("rstd_ready"), sem("normed"), sem("norm_step")
        prep_step, split_ready, operands_ready = sem("prep_step"), sem("split_ready"), sem("operands_ready")
        bound_ready, widest_ready, flag_ready, flag_read = sem("bound_ready"), sem("widest_ready"), sem("flag_ready"), sem("flag_read")
        turn_full, turn_free = sem("turn_full"), sem("turn_free")
        scores_ready, exps_done, probs_free = sem("scores_ready"), sem("exps_done"), sem("probs_free")
        acc_free, sums_ready, recip_ready = sem("acc_free"), sem("sums_ready"), sem("recip_ready")
        qk_turned, max_full, max_free, max_ready, max_step = sem("qk_turned"), sem("max_full"), sem("max_free"), sem("max_ready"), sem("max_step")
        heads_stored = sem("heads_stored")
        waited = sem("waited")

        USES = ROUNDS + 1
        rounds_of = lambda head: (head - 1) * USES + ROUNDS
        result_of = lambda head: head * USES + 2 * ROUNDS
        LAST_RESULT = (NHD - 1) * USES + ROUNDS
        MAX_USES = BB * QC + 2

        block = ctx.enter_context(nc.Block())

        @block.sync
        def _(sp):
            sp.dma_start(rot_row[:, :], rot.rearrange("h d -> (h d)").partition_broadcast(P)).then_inc(rot_loaded, 16)
            sp.dma_start(ent_row[:, :], ent.rearrange("h d -> (h d)").partition_broadcast(P)).then_inc(rot_loaded, 16)
            for b in range(B):
                if b >= slots:
                    sp.wait_ge(normed, b - slots + 1)
                sp.dma_start(xs[:, (b % slots) * BB:(b % slots + 1) * BB, :], x_in[b].rearrange("(k p) c -> p k c", p=P)).then_inc(x_loaded[b], 16)
            sp.dma_start(row_mem[:, :, :].rearrange("p a c -> p (a c)"), rows.partition_broadcast(P)).then_inc(weights_loaded, 16)
            sp.wait_ge(normed, B)
            sp.dma_start(stage_mem[:, 0:FLOAT_COLS], floats).then_inc(weights_loaded, 16)
            sp.dma_start(stage_mem[:, FLOAT_COLS:FLOAT_COLS + INT_COLS].bitcast(I32), ints).then_inc(weights_loaded, 16)
            with sp.Fori(0, NHD - 1) as head:
                sp.wait_ge(turn_free, result_of(head) + 2)
                sp.dma_start(heads_out[bass.ds(head, 1)].rearrange("a p n -> p (a n)"),
                             heads[:, bass.ds(head, 1), :, :].rearrange("p a k d -> p (a k d)")).then_inc(heads_stored, 16)
            sp.wait_ge(turn_free, LAST_RESULT + 2)
            sp.dma_start(heads_out[NHD - 1], heads[:, NHD - 1, :, :].rearrange("p k d -> p (k d)")).then_inc(heads_stored, 16)
            sp.wait_ge(heads_stored, 16 * NHD)

        @block.gpsimd
        def _(pool):
            pool.memset(neghalf[:, :], -0.5).then_inc(pool_init, 1)
            for m in (ident, identb):
                pool.memset(m[:, :], 0.0).then_inc(pool_init, 1)
            pool.wait_ge(pool_init, 3)
            for m in (ident, identb):
                pool.affine_select(out=m[:, :], in_=m[:, :], compare_op=ALU.not_equal, fill=1.0, base=0,
                                   pattern=[[-1, P]], channel_multiplier=1).then_inc(consts, 1)

            def inverse_std(b):
                blks = slice(b * BB, (b + 1) * BB)
                pool.wait_ge(var_ready, b + 1)
                pool.tensor_tensor(rstd[:, blks], ve[:, blks], neghalf[:, :], ALU.pow).then_inc(rstd_ready, 1)

            def widest_of(head):
                pool.wait_ge(bound_ready, head + 1)
                pool.sem_inc(waited, 1)
                pool.partition_all_reduce(widest[:, 1:2], widest[:, 0:1], P, bass.bass_isa.ReduceOp.max).then_inc(widest_ready, 1)

            inverse_std(0)
            widest_of(0)
            for b in range(1, B):
                widest_of(b)
                inverse_std(b)
            with pool.Fori(B, NHD) as head:
                widest_of(head)

        @block.tensor
        def _(pe):
            pe.wait_ge(consts, 2)
            pe.sem_inc(probs_free, PROBS)
            pe.sem_inc(turn_free, 1)
            pe.sem_inc(acc_free, 1)
            pe.sem_inc(max_free, 1)

            def turn_round(r, full):
                src = q_split if r < 2 else k_split
                for k in range(8):
                    last = nc.tensor.transpose(TURNB[:, k * P:(k + 1) * P], src[:, (r % 2) * 8 + k, :], identb[:, :])
                last.then_inc(full, 1)

            def half_scores(i, buf):
                j, half = i // 2, i % 2
                for n in range(2):
                    q0 = half * T // 2 + n * BANK
                    last = nc.tensor.matmul(SCORES[i % 3][:, n * BANK:(n + 1) * BANK], kT[buf][:, j * P:(j + 1) * P],
                                            qT[buf][:, q0:q0 + BANK], start=True, stop=True)
                last.then_inc(scores_ready, 1)

            def general_scores(head, buf):
                pe.wait_ge(flag_ready, head + 1)
                pe.sem_inc(waited, 1)
                general = pe.value_load(flag[0:1, 0:1], min_val=0, max_val=1)
                with pe.If(general > 0):
                    pe.wait_ge(qk_turned, head + 1)
                    pe.sem_inc(waited, 1)
                    with pe.Fori(0, BB) as k:
                        for c in range(QC):
                            pe.wait_ge(max_free, head * MAX_USES + k * QC + c + 1)
                            nc.tensor.matmul(TURN, qT[buf][:, bass.ds(k * P, P)], kT[buf][:, c * BANK:(c + 1) * BANK],
                                             start=True, stop=True).then_inc(max_full, 1)
                    pe.wait_ge(max_ready, head + 1)
                    for r in range(2):
                        pe.wait_ge(max_free, head * MAX_USES + BB * QC + r + 1)
                        turn_round(r, max_full)
                    pe.wait_ge(max_free, (head + 1) * MAX_USES + 1)
                with pe.Else():
                    pe.sem_inc(max_full, MAX_USES)
                pe.sem_inc(flag_read, 1)

            pe.wait_ge(split_ready, 1)
            for r in range(ROUNDS):
                pe.wait_ge(turn_free, r + 1)
                turn_round(r, turn_full)
            general_scores(0, 0)
            pe.wait_ge(operands_ready, 1)
            for i in range(4):
                if i == 3:
                    pe.wait_ge(exps_done, 1)
                half_scores(i, 0)

            def head_sums(head, buf, last):
                for j in range(BB):
                    if j in (3, 5, 7, 9) and not last:
                        r = (j - 3) // 2
                        if r == 0:
                            pe.wait_ge(split_ready, head + 2)
                        pe.wait_ge(turn_free, rounds_of(head + 1) + r + 1)
                        turn_round(r, turn_full)
                        if r == ROUNDS - 1:
                            general_scores(head + 1, 1 - buf)
                    if j + 2 < BB or not last:
                        for i in (2 * (j + 2), 2 * (j + 2) + 1):
                            if i < HALVES:
                                pe.wait_ge(exps_done, head * HALVES + i - 2)
                                half_scores(i, buf)
                            else:
                                if i == HALVES:
                                    pe.wait_ge(operands_ready, head + 2)
                                pe.wait_ge(exps_done, head * HALVES + {0: 31, 1: 32, 2: 30, 3: 33}[i - HALVES])
                                half_scores(i - HALVES, 1 - buf)
                    pe.wait_ge(exps_done, head * HALVES + 2 * j + 2)
                    if j == 0:
                        pe.wait_ge(acc_free, head + 1)
                    for c in range(QC):
                        mm = nc.tensor.matmul(ACC[32 * c:32 * c + 32, :], vals[buf][:, j, :], probs[:, j % PROBS, c * BANK:(c + 1) * BANK],
                                              start=(j == 0), stop=(j == BB - 1), tile_position=(0, 32 * c))
                    mm.then_inc(probs_free, 1)
                pe.wait_ge(sums_ready, head + 1)
                pe.wait_ge(turn_free, (LAST_RESULT if last else result_of(head)) + 1)
                for t in range(QC):
                    mm = nc.tensor.transpose(TURN[:, t * P:(t + 1) * P], sums[:, t * P:(t + 1) * P], ident[:, :])
                mm.then_inc(turn_full, 1)

            with pe.Fori(0, NHD // 2 - 1) as pair:
                for e in range(2):
                    head_sums(pair * 2 + e, e, False)
            head_sums(NHD - 2, 0, False)
            head_sums(NHD - 1, 1, True)

        @block.scalar
        def _(act):
            GROUP = 4
            with act.Fori(0, NHD // GROUP) as group:
                for g in range(GROUP):
                    head = group * GROUP + g
                    for i in range(HALVES):
                        if i % 2 == 0:
                            act.wait_ge(probs_free, head * BB + i // 2 + 1)
                        act.wait_ge(scores_ready, head * HALVES + i + 1)
                        nc.scalar.activation(probs[:, i // 2 % PROBS, i % 2 * T // 2:(i % 2 + 1) * T // 2], SCORES[i % 3], ACT.Exp).then_inc(exps_done, 1)

        @block.vector
        def _(dve):
            V = nc.vector
            setup = Chain(dve, prep_step)
            dve.wait_ge(rot_loaded, 32)
            for b in range(B):
                setup.done(V.tensor_scalar(rot_heads[:, b * H:(b + 1) * H, :].rearrange("p h d -> p (h d)"), rot_row[:, :], D ** -0.5, None, ALU.mult))
                setup.done(V.tensor_copy(ent_heads[:, b * H:(b + 1) * H, :].rearrange("p h d -> p (h d)"), ent_row[:, :]))
            setup.wait()

            def norm(b):
                ch = Chain(dve, norm_step, b * 2)
                blks = range(b * BB, (b + 1) * BB)
                here = slice(b * BB, (b + 1) * BB)
                dve.wait_ge(x_loaded[b], 16)
                for k in blks:
                    ins = V.bn_stats(stats[:, k, :], xs[:, k % (slots * BB), :])
                ch.link(ins)
                for k in blks:
                    ins = V.bn_aggr(mv[:, k, :], stats[:, k, :])
                ch.link(ins)
                V.tensor_scalar(ve[:, here], mv[:, here, 1], EPS, None, ALU.add).then_inc(var_ready, 1)
                dve.wait_ge(rstd_ready, b + 1)
                for k in blks:
                    ins = V.tensor_scalar(heads[:, b * H:(b + 1) * H, k % BB, :], xs[:, k % (slots * BB), :].rearrange("p (h d) -> p h d", h=H),
                                          mv[:, k, 0:1], rstd[:, k:k + 1], ALU.subtract, ALU.mult)
                ins.then_inc(normed, 1)
                dve.wait_ge(normed, b + 1)

            norm(0)
            static = Chain(dve, static_ready)
            for t in (q_split, k_split, *vals):
                static.done(V.memset(t[:, :, :], 0.0))
            static.wait()
            static.done(V.memset(k_split[:, :, BIAS:BIAS + 3], 1.0))
            for t in vals:
                static.done(V.memset(t[:, :, D:D + 1], 1.0))
            static.wait()

            SETUP_STEPS, PREP_STEPS, MAX_STEPS = setup.n, 12, 6

            def prep(head, buf, uses):
                ch = Chain(dve, prep_step, SETUP_STEPS + head * PREP_STEPS)
                x = heads[:, bass.ds(head, 1), :, :].rearrange("p a k d -> p (a k) d")
                factor = lambda t: t[:, bass.ds(head, 1), :].broadcast_to([P, BB, D])
                qs = q_split[:, :, 0:BIAS].rearrange("p k (s d) -> p k s d", s=PARTS)
                ks = k_split[:, :, 0:BIAS].rearrange("p k (s d) -> p k s d", s=PARTS)
                copies = lambda t, n: t[:, :, :].unsqueeze(2).broadcast_to([P, BB, n, D])
                ch.done(V.tensor_tensor(qf[:, :, :], x, factor(rot_heads), ALU.mult))
                ch.link(V.tensor_tensor(kf[:, :, :], x, factor(ent_heads), ALU.mult))
                ch.done(V.tensor_copy(qs[:, :, 0:3, :], copies(qf, 3)))
                ch.done(V.tensor_copy(vals[buf][:, :, 0:D], x))
                ch.done(V.tensor_copy(ks[:, :, 0:4:3, :], copies(kf, 2)))
                ch.link(V.tensor_copy(ks[:, :, 5, :], kf[:, :, :]))
                V.tensor_tensor(q_rest[:, :, :], qf[:, :, :], qs[:, :, 0, :], ALU.subtract)
                ch.link(V.tensor_tensor(k_rest[:, :, :], kf[:, :, :], ks[:, :, 0, :], ALU.subtract))
                V.tensor_copy(qs[:, :, 3:5, :], copies(q_rest, 2))
                ch.link(V.tensor_copy(ks[:, :, 1:5:3, :], copies(k_rest, 2)))
                ch.done(V.tensor_tensor(qs[:, :, 5, :], q_rest[:, :, :], qs[:, :, 3, :], ALU.subtract))
                V.tensor_tensor(ks[:, :, 2, :], k_rest[:, :, :], ks[:, :, 1, :], ALU.subtract).then_inc(split_ready, 1)

                dve.wait_ge(flag_read, head)
                ch.link(V.tensor_tensor(qk[:, :, :], qf[:, :, :], kf[:, :, :], ALU.mult))
                ch.link(V.tensor_reduce(bound[:, :], qk[:, :, :], AX.X, ALU.add, apply_absolute_value=True))
                V.tensor_reduce(widest[:, 0:1], bound[:, :], AX.X, ALU.max).then_inc(bound_ready, 1)
                dve.wait_ge(widest_ready, head + 1)
                ch.link(V.tensor_scalar(flag[:, :], widest[:, 1:2], SAFE, None, ALU.is_gt))
                dve.sem_inc(flag_ready, 1)
                general = dve.value_load(flag[0:1, 0:1], min_val=0, max_val=1)
                assert ch.n == PREP_STEPS

                for r in range(ROUNDS):
                    dve.wait_ge(turn_full, uses + r + 1)
                    dst = (qT if r < 2 else kT)[buf]
                    V.tensor_copy(dst[:, (r % 2) * T // 2:(r % 2 + 1) * T // 2], TURNB).then_inc(turn_free, 1)
                with dve.If(general > 0):
                    dve.wait_ge(turn_free, uses + ROUNDS + 1)
                    dve.sem_inc(qk_turned, 1)
                    with dve.Fori(0, BB) as k:
                        for c in range(QC):
                            dve.wait_ge(max_full, head * MAX_USES + k * QC + c + 1)
                            V.tensor_reduce(chunk_max[:, bass.ds(k, 1), c], TURN, AX.X, ALU.max).then_inc(max_free, 1)
                    dve.wait_ge(max_free, head * MAX_USES + BB * QC + 1)
                    g = Chain(dve, max_step, head * MAX_STEPS)
                    rest, rest2, parts = neg_max[:, :, 0], neg_max[:, :, 1], q_split[:, :, BIAS:BIAS + 3]
                    g.link(V.tensor_reduce(rest, chunk_max[:, :, :], AX.X, ALU.max, negate=True))
                    g.link(V.tensor_copy(parts[:, :, 0], rest))
                    g.link(V.tensor_tensor(rest2, rest, parts[:, :, 0], ALU.subtract))
                    g.link(V.tensor_copy(parts[:, :, 1], rest2))
                    V.tensor_tensor(parts[:, :, 2], rest2, parts[:, :, 1], ALU.subtract).then_inc(max_ready, 1)
                    for r in range(2):
                        dve.wait_ge(max_full, head * MAX_USES + BB * QC + r + 1)
                        V.tensor_copy(qT[buf][:, r * T // 2:(r + 1) * T // 2], TURNB).then_inc(max_free, 1)
                    g.done(V.memset(parts, 0.0))
                    dve.wait_ge(max_free, (head + 1) * MAX_USES + 1)
                    g.wait()
                    dve.sem_inc(max_step, MAX_STEPS - g.n)
                with dve.Else():
                    dve.sem_inc(qk_turned, 1)
                    dve.sem_inc(max_free, MAX_USES)
                    dve.sem_inc(max_ready, 1)
                    dve.sem_inc(max_step, MAX_STEPS)
                dve.wait_ge(turn_free, uses + ROUNDS + 1)
                dve.sem_inc(operands_ready, 1)

            def finish(head, uses):
                dve.wait_ge(probs_free, head * BB + BB + PROBS)
                V.tensor_copy(sums[:, :], ACC).then_inc(sums_ready, 1)
                dve.wait_ge(sums_ready, head + 1)
                dve.sem_inc(acc_free, 1)
                dve.wait_ge(turn_full, uses + 1)
                turned = TURN.rearrange("p (t c d) -> p t c d", t=QC, c=QC)
                V.reciprocal(recip[:, :, :], turned[:, :, :, D]).then_inc(recip_ready, 1)
                dve.wait_ge(recip_ready, head + 1)
                dst = heads[:, bass.ds(head, 1), :, :].rearrange("p a (c t) d -> p (a t) c d", c=QC)
                V.tensor_tensor(dst, turned[:, :, :, 0:D], recip[:, :, :].unsqueeze(3).broadcast_to([P, QC, QC, D]), ALU.mult).then_inc(turn_free, 1)

            prep(0, 0, 0)
            for head in range(B):
                prep(head + 1, 1 - head % 2, rounds_of(head + 1))
                if head + 1 < B:
                    norm(head + 1)
                finish(head, result_of(head))
            with dve.Fori(B // 2, NHD // 2 - 1) as pair:
                for e in range(2):
                    head = pair * 2 + e
                    prep(head + 1, 1 - e, rounds_of(head + 1))
                    finish(head, result_of(head))
            prep(NHD - 1, 1, rounds_of(NHD - 1))
            dve.wait_ge(weights_loaded, 48)
            ints_here = stage_mem[:, FLOAT_COLS:FLOAT_COLS + INT_COLS]
            V.tensor_scalar(ints_here, ints_here.bitcast(I32), DEQUANT, None, ALU.mult).then_inc(weights_ready, 1)
            finish(NHD - 2, result_of(NHD - 2))
            finish(NHD - 1, LAST_RESULT)
            dve.wait_ge(weights_ready, 1)


SHIFT = {"l": CB, "0": 0, "1": 1, "a": CB + 1, "b": CB + 2}
ORDER = [("load_in", "0"), ("msg", "a"), ("load_msg", "l"), ("load_x2", "a"), ("up0", "b"), ("y", "a"), ("up1", "b"), ("up2", "b"), ("mix", "1"),
         ("up3", "b"), ("yT", "a"), ("up4", "b"), ("up5", "b"), ("rk", "1"), ("fc0", "a"), ("val", "1"), ("fc1", "a"), ("proj0", "a"),
         ("uT", "1"), ("proj1", "a"), ("qkv", "1"), ("in0", "0"), ("in1", "0"), ("down", "b"), ("in2", "0"), ("kv", "1"), ("nT", "a"), ("end", "b")]
STREAM = dict(ORDER)
PLACE = {stage: i for i, (stage, _) in enumerate(ORDER)}
LOOPS = [(0, 1, "0"), (1, 2, "01"), (2, CB + 1, "01"), (CB + 1, CB + 2, "01a"), (CB + 2, CB + 3, "01ab"), (CB + 3, NC, "01ab"), (NC, NC + 1, "1ab"), (NC + 1, NC + CB + 1, "ab"), (NC + CB + 1, NC + CB + 2, "b")]
SP_LOOPS = [(0, 1, "0"), (1, 2, "01"), (2, CB, "01"), (CB, CB + 1, "01l"), (CB + 1, CB + 2, "01la"), (CB + 2, CB + 3, "01lab"), (CB + 3, NC, "01lab"), (NC, NC + 1, "1lab"),
            (NC + 1, NC + CB, "lab"), (NC + CB, NC + CB + 1, "ab"), (NC + CB + 1, NC + CB + 2, "b")]


def run(eng, stages, loops=LOOPS):
    def once(it, first, end, streams):
        def counter(here):
            def chunks_past(there):
                shift = SHIFT[STREAM[there]]
                if first < shift:
                    return 0
                if first >= shift + NC:
                    return NC
                return it - shift + (PLACE[there] < PLACE[here])
            return chunks_past

        for stage, stream in ORDER:
            if stream in streams and stage in stages:
                stages[stage](it - SHIFT[stream], counter(stage))

    for first, end, streams in loops:
        if end - first == 1:
            once(first, first, end, streams)
        else:
            with eng.Fori(first, end) as it:
                once(it, first, end, streams)


def later_layers(nc, heads_in, x_in, W, ident, out):
    with ExitStack() as ctx:
        sb = lambda n, s, d=F32: ctx.enter_context(nc.sbuf_tensor(n, s, d))
        dram = lambda n: nc.dram_tensor(n, [NC, P, K4 * C], F32, kind="Internal").ap()
        sems = {}

        def sem(n):
            if n not in sems:
                sems[n] = ctx.enter_context(nc.semaphore(n))
            return sems[n]

        x2_dram, n2_dram, q_dram = dram("x2_dram"), dram("n2_dram"), dram("q_dram")

        tok = lambda n: sb(n, [P, K4, C])
        chan = lambda n: sb(n, [P, KC, N])
        flat = lambda t: t[:, :, :].rearrange("p a b -> p (a b)")
        attn = sb("attn", [P, H, K4, D])
        x0, x1, t1, n1, f, x2, r_gate = (tok(n) for n in ("x0", "x1", "t1", "n1", "f", "x2", "r_gate"))
        n1T = sb("n1T", [P, KC, N + 1])
        xr, xk, k_act, uT, q = (chan(n) for n in ("xr", "xk", "k_act", "uT", "q"))
        k_relu = chan("k_relu")
        q_exp, k_exp = xr, r_gate
        k_feat = tok("k_feat")
        v_ones = sb("v_ones", [P, K4, KC, KVW])
        kv_sums = sb("kv_sums", [P, B, KC * KVW])
        kv_diag = sb("kv_diag", [P, KC, MSGW])
        q_in = chan("q_in")
        n2_in, x3, x3_b2, t2, x2_in, x4, x4_kept, y_out = (tok(n) for n in ("n2_in", "x3", "x3_b2", "t2", "x2_in", "x4", "x4_kept", "y_out"))
        o = f
        yT, n4T = chan("yT"), chan("n4T")
        denom = sb("denom", [P, K4, KC, HG])
        hT = sb("hT", [P, M1, N])
        gate = sb("gate", [P, 2, N])
        gated = sb("gated", [P, M2, N])
        norms = ("attn", "x1", "f", "x2", "x3", "o", "x4", "ffn")
        stats = {l: sb(f"stats_{l}", [P, K4, 6]) for l in norms}
        mv = {l: sb(f"mv_{l}", [P, K4, 2]) for l in norms}
        ve = {l: sb(f"ve_{l}", [P, K4]) for l in norms}
        rstd = {l: sb(f"rstd_{l}", [P, K4]) for l in norms}
        ve_n2, rstd_n2 = sb("ve_n2", [P, K4]), sb("rstd_n2", [P, K4])
        keep = sb("keep", [P, NC + 1])
        neghalf = sb("neghalf_k4", [P, K4])
        one_minus_mu = sb("one_minus_mu", [P, 2, KC])
        ps = ctx.enter_context(nc.psum_tensor("layers_ps", [P, 8, BANK], F32))
        banks = lambda a, n: ps[:, a:a + n, :]
        wide = lambda a, n: ps[:, a:a + n, :].rearrange("p a n -> p (a n)")
        blocks = lambda a: ps[:, a:a + 2, :].rearrange("p a (b n) -> p (a b) n", b=2)
        MSG_BANKS = (2, 3, 6, 7)
        up_bank = lambda m: (4, 2)[m % 2]

        block = ctx.enter_context(nc.Block())

        @block.sync
        def _(sp):
            heads_v = heads_in.rearrange("(b h) p (q n) -> b q p h n", b=B, q=CB)
            x_v = x_in.rearrange("b (q k p) c -> (b q) p k c", q=CB, p=P)
            out_v = out.rearrange("b (q k p) c -> (b q) p k c", q=CB, p=P)
            slab = lambda d, c: d[bass.ds(c, 1)].rearrange("a p n -> p (a n)")

            def load_in(c, past):
                sp.wait_ge(sem("attn_used"), c)
                sp.dma_start(attn[:, :, :, :].rearrange("p h k d -> p h (k d)"),
                             heads_v[bass.ds(c // CB, 1), bass.ds(c % CB, 1)].rearrange("a b p h n -> p (a b h) n")).then_inc(sem("attn_loaded"), 16)
                sp.wait_ge(sem("x1_done"), c)
                sp.dma_start(x0[:, :, :], x_v[bass.ds(c, 1)].rearrange("a p k c -> p (a k) c")).then_inc(sem("x0_loaded"), 16)

            def load_msg(c, past):
                sp.wait_ge(sem("msg_mm"), c * K4)
                sp.wait_ge(sem("q_stored"), c * 16 + 16)
                sp.dma_start(flat(q_in), slab(q_dram, c)).then_inc(sem("q_loaded"), 16)
                sp.wait_ge(sem("x3_done"), c)
                sp.wait_ge(sem("n2_stored"), c * 16 + 16)
                sp.dma_start(flat(n2_in), slab(n2_dram, c)).then_inc(sem("n2_loaded"), 16)

            def load_x2(c, past):
                sp.wait_ge(sem("x4_done"), c)
                sp.wait_ge(sem("x2_stored"), c * 16 + 16)
                sp.dma_start(flat(x2_in), slab(x2_dram, c)).then_inc(sem("x2_loaded"), 16)

            def store_x2_n2(c, past):
                sp.wait_ge(sem("x2_done"), c + 1)
                sp.dma_start(slab(x2_dram, c), flat(x2)).then_inc(sem("x2_stored"), 16)
                sp.wait_ge(sem("n2_done"), c + 1)
                sp.dma_start(slab(n2_dram, c), flat(n1)).then_inc(sem("n2_stored"), 16)

            def store_q(c, past):
                sp.wait_ge(sem("q_done"), c + 1)
                sp.dma_start(slab(q_dram, c), flat(q)).then_inc(sem("q_stored"), 16)

            def store_out(c, past):
                sp.wait_ge(sem("y_done"), c + 1)
                sp.dma_start(out_v[bass.ds(c, 1)].rearrange("a p k c -> p (a k) c"), y_out[:, :, :]).then_inc(sem("stored"), 16)

            run(sp, {"load_in": load_in, "load_msg": load_msg, "load_x2": load_x2, "uT": store_x2_n2, "kv": store_q, "end": store_out}, SP_LOOPS)
            for name in ("stored", "x2_stored", "n2_stored", "q_stored"):
                sp.wait_ge(sem(name), 16 * NC)

        @block.gpsimd
        def _(pool):
            pool.memset(neghalf[:, :], -0.5).then_inc(sem("pool_ready"), 1)
            pool.wait_ge(sem("pool_ready"), 1)

            def inverse_std(l):
                def f(c, past):
                    pool.wait_ge(sem("ve_" + l), c + 1)
                    pool.tensor_tensor(rstd[l][:, :], ve[l][:, :], neghalf[:, :], ALU.pow).then_inc(sem("rstd_" + l), 1)
                return f

            def val(c, past):
                inverse_std("f")(c, past)
                inverse_std("x2")(c, past)
                pool.wait_ge(sem("ve_n2"), c + 1)
                pool.tensor_tensor(rstd_n2[:, :], ve_n2[:, :], neghalf[:, :], ALU.pow).then_inc(sem("rstd_n2"), 1)

            def msg(c, past):
                inverse_std("x3")(c, past)
                pool.wait_ge(sem("o_done"), c)
                pool.tensor_tensor(x3_b2[:, :, :], x3[:, :, :], W["b2"].unsqueeze(1).broadcast_to([P, K4, C]), ALU.add).then_inc(sem("x3_b2_done"), 1)

            def proj1(c, past):
                inverse_std("o")(c, past)
                inverse_std("x4")(c, past)

            run(pool, {"in0": inverse_std("attn"), "in1": inverse_std("x1"), "val": val, "msg": msg, "proj1": proj1, "end": inverse_std("ffn")})

        @block.tensor
        def _(pe):
            def turn(src, done):
                for k in range(K4):
                    for h in range(KC):
                        last = nc.tensor.transpose(ps[:, h, k * P:(k + 1) * P], src[:, k, h * P:(h + 1) * P], ident[:, :])
                last.then_inc(sem(done), 1)

            def chan_out(dst, w, i, x, kk=KC):
                for k in range(kk):
                    last = nc.tensor.matmul(dst, w[:, k, i * P:(i + 1) * P], x[:, k, :], start=(k == 0), stop=(k == kk - 1))
                return last

            def tok_out(dst, x, blk, w, kk=KC):
                for k in range(kk):
                    last = nc.tensor.matmul(dst, x[:, k, blk * P:(blk + 1) * P], w[:, k, :], start=(k == 0), stop=(k == kk - 1))
                return last

            def mix(c, past):
                pe.wait_ge(sem("n1_done"), c + 1)
                pe.wait_ge(sem("q_done"), c)
                pe.wait_ge(sem("n4T_done"), past("nT"))
                turn(n1, "mix_mm")

            def rk(c, past):
                pe.wait_ge(sem("mixed"), c + 1)
                pe.wait_ge(sem("kv_done"), c)
                pe.wait_ge(sem("msg_read"), past("msg"))
                pe.wait_ge(sem("gated_done"), past("up5") * M2)
                for i in range(KC):
                    last = chan_out(ps[:, 2 + i, :], W["wk"], i, xk)
                last.then_inc(sem("k_mm"), 1)
                pe.wait_ge(sem("v_read"), c)
                pe.wait_ge(sem("ffn_read"), past("end"))
                for k in range(K4):
                    last = tok_out(blocks(4)[:, k, :], xr, k, W["wr"])
                last.then_inc(sem("r_mm"), 1)

            def val(c, past):
                pe.wait_ge(sem("k_act_done"), c + 1)
                for k in range(K4):
                    last = tok_out(blocks(2)[:, k, :], k_act, k, W["wv"])
                last.then_inc(sem("val_mm"), 1)

            def turn_u(c, past):
                pe.wait_ge(sem("u_done"), c + 1)
                pe.wait_ge(sem("yT_done"), past("yT"))
                turn(t1, "uT_mm")

            def qkv(c, past):
                pe.wait_ge(sem("uT_done"), c + 1)
                for i, name in enumerate(("k2_mm", "v2_mm")):
                    for k in range(K4):
                        last = tok_out(blocks(2 + 2 * i)[:, k, :], uT, k, W["akv"][:, :, i * C:(i + 1) * C])
                    last.then_inc(sem(name), 1)
                for i in range(KC):
                    last = chan_out(ps[:, i, :], W["aq"], i, uT)
                last.then_inc(sem("q_mm"), 1)

            def kv(c, past):
                pe.wait_ge(sem("k_feat_done"), c + 1)
                pe.wait_ge(sem("v_read"), c + 1)
                for g in range(KC):
                    for k in range(K4):
                        last = nc.tensor.matmul(ps[:, 2, g * KVW:(g + 1) * KVW], k_feat[:, k, g * P:(g + 1) * P], v_ones[:, k, g, :],
                                                start=(k == 0), stop=(k == K4 - 1))
                last.then_inc(sem("kv_mm"), 1)

            def msg(c, past):
                pe.wait_ge(sem("q_loaded"), c * 16 + 16)
                pe.wait_ge(sem("kv_diag_done"), c + 1)
                pe.wait_ge(sem("kv_done"), past("kv"))
                pe.wait_ge(sem("k_feat_done"), past("qkv"))
                pe.wait_ge(sem("gated_done"), past("up5") * M2)
                pe.wait_ge(sem("o_done"), c)
                for k in range(K4):
                    for g in range(KC):
                        last = nc.tensor.matmul(ps[:, MSG_BANKS[k], g * MSGW:(g + 1) * MSGW], q_in[:, g, k * P:(k + 1) * P], kv_diag[:, g, :], start=True, stop=True)
                    last.then_inc(sem("msg_mm"), 1)

            def turn_y(c, past):
                pe.wait_ge(sem("y_in_done"), c + 1)
                pe.wait_ge(sem("n1T_done"), past("mix"))
                pe.wait_ge(sem("n4T_done"), c)
                turn(t2, "yT_mm")

            def fc(half):
                def f(c, past):
                    if half == 0:
                        pe.wait_ge(sem("yT_done"), c + 1)
                        pe.wait_ge(sem("msg_read"), c + 1)
                    for i in range(half * M1 // 2, (half + 1) * M1 // 2):
                        if i >= 2:
                            pe.wait_ge(sem("gelu_done"), c * M1 + i - 1)
                        chan_out(ps[:, 6 + i % 2, :], W["w1"], i, yT).then_inc(sem("fc_mm"), 1)
                return f

            def proj(half):
                def f(c, past):
                    pe.wait_ge(sem("gelu_done"), c * M1 + M1)
                    for k in (2 * half, 2 * half + 1):
                        last = tok_out(blocks(6)[:, k, :], hT, k, W["w2"], M1)
                    last.then_inc(sem("proj_mm"), 1)
                return f

            def turn_n4(c, past):
                pe.wait_ge(sem("n4_done"), c + 1)
                pe.wait_ge(sem("q_done"), past("qkv"))
                turn(t2, "nT_mm")

            def up(m):
                def f(c, past):
                    if m == 0:
                        pe.wait_ge(sem("n4T_done"), c + 1)
                        pe.wait_ge(sem("ffn_read"), c)
                        pe.wait_ge(sem("v_read"), past("qkv"))
                    elif m == 1:
                        pe.wait_ge(sem("msg_read"), past("msg"))
                    else:
                        pe.wait_ge(sem("gated_done"), c * M2 + m - 1)
                    a = up_bank(m)
                    chan_out(ps[:, a, :], W["wg"], m, n4T).then_inc(sem("gate_mm"), 1)
                    chan_out(ps[:, a + 1, :], W["wu"], m, n4T).then_inc(sem("up_mm"), 1)
                return f

            def down(c, past):
                pe.wait_ge(sem("gated_done"), c * M2 + M2)
                pe.wait_ge(sem("v_read"), past("qkv"))
                for k in range(K4):
                    last = tok_out(blocks(4)[:, k, :], gated, k, W["wd"], M2)
                last.then_inc(sem("down_mm"), 1)

            run(pe, {"mix": mix, "rk": rk, "val": val, "uT": turn_u, "qkv": qkv, "kv": kv, "msg": msg, "yT": turn_y, "fc0": fc(0), "fc1": fc(1),
                     "proj0": proj(0), "proj1": proj(1), "nT": turn_n4, "down": down, **{f"up{m}": up(m) for m in range(M2)}})

        @block.scalar
        def _(act):
            A = nc.scalar.activation

            def mix(c, past):
                act.wait_ge(sem("mix_mm"), c + 1)
                act.wait_ge(sem("carried"), c + 1)
                A(n1T[:, :, 1:N + 1], banks(0, 2), ACT.Copy).then_inc(sem("n1T_done"), 1)

            def rk(c, past):
                act.wait_ge(sem("k_mm"), c + 1)
                act.wait_ge(sem("k_act_done"), c)
                A(k_relu[:, :, :], banks(2, 2), ACT.Relu).then_inc(sem("k_read"), 1)
                act.wait_ge(sem("r_mm"), c + 1)
                act.wait_ge(sem("k_feat_done"), c)
                A(flat(r_gate), wide(4, 2), ACT.Sigmoid).then_inc(sem("r_read"), 1)

            def turn_u(c, past):
                act.wait_ge(sem("uT_mm"), c + 1)
                act.wait_ge(sem("q_mm"), c)
                A(uT[:, :, :], banks(0, 2), ACT.Copy).then_inc(sem("uT_done"), 1)

            def qkv(c, past):
                act.wait_ge(sem("v2_mm"), c + 1)
                act.wait_ge(sem("kv_mm"), c)
                A(v_ones[:, :, :, 0:P], blocks(4).rearrange("p k (g n) -> p k g n", g=KC), ACT.Copy).then_inc(sem("v_read"), 1)
                act.wait_ge(sem("k_low"), c + 1)
                A(k_exp[:, :, :], k_exp[:, :, :], ACT.Exp).then_inc(sem("k_exp_done"), 1)
                act.wait_ge(sem("q_low"), c + 1)
                A(q_exp[:, :, :], q_exp[:, :, :], ACT.Exp).then_inc(sem("q_exp_done"), 1)

            def turn_y(c, past):
                act.wait_ge(sem("yT_mm"), c + 1)
                act.wait_ge(sem("fc_mm"), c * M1)
                A(yT[:, :, :], banks(0, 2), ACT.Copy).then_inc(sem("yT_done"), 1)

            def fc(half):
                def f(c, past):
                    if half == 0:
                        act.wait_ge(sem("proj_mm"), c * 2)
                    for i in range(half * M1 // 2, (half + 1) * M1 // 2):
                        act.wait_ge(sem("fc_mm"), c * M1 + i + 1)
                        A(hT[:, i, :], ps[:, 6 + i % 2, :], ACT.Gelu, bias=W["b1"][:, 0, i:i + 1]).then_inc(sem("gelu_done"), 1)
                return f

            def turn_n4(c, past):
                act.wait_ge(sem("nT_mm"), c + 1)
                act.wait_ge(sem("up_mm"), c * M2)
                A(n4T[:, :, :], banks(0, 2), ACT.Copy).then_inc(sem("n4T_done"), 1)

            def up(m):
                def f(c, past):
                    if m == 0:
                        act.wait_ge(sem("x4_done"), c + 1)
                        act.wait_ge(sem("y_done"), c)
                        A(x4_kept[:, :, :], x4[:, :, :], ACT.Copy).then_inc(sem("x4_kept"), 1)
                    act.wait_ge(sem("gate_mm"), c * M2 + m + 1)
                    act.wait_ge(sem("gated_done"), c * M2 + max(m - 1, 0))
                    A(gate[:, m % 2, :], ps[:, up_bank(m), :], ACT.Silu).then_inc(sem("silu_done"), 1)
                return f

            run(act, {"mix": mix, "rk": rk, "uT": turn_u, "qkv": qkv, "yT": turn_y, "fc0": fc(0), "fc1": fc(1), "nT": turn_n4,
                      **{f"up{m}": up(m) for m in range(M2)}})

        @block.vector
        def _(dve):
            V = nc.vector
            setup = Chain(dve, sem("setup"))
            setup.done(V.memset(n1T[:, :, :], 0.0))
            setup.done(V.memset(kv_sums[:, :, :], 0.0))
            setup.done(V.memset(kv_diag[:, :, :], 0.0))
            setup.done(V.memset(keep[:, :], 1.0))
            setup.done(V.memset(v_ones[:, :, :, P:P + 1], 1.0))
            setup.done(V.memset(v_ones[:, :, :, P + 1:P + 2], 0.0))
            for i, mu in enumerate(("mu_r", "mu_k")):
                setup.done(V.tensor_scalar(one_minus_mu[:, i, :], W[mu][:, 0, :], -1.0, 1.0, ALU.mult, ALU.add))
            setup.wait()
            setup.link(V.memset(keep[:, 0:NC:CB], 0.0))
            V.memset(keep[:, NC:NC + 1], 0.0).then_inc(sem("carried"), 1)

            def norm_stats(l, src, c):
                ch = Chain(dve, sem("stats_" + l), c * 2)
                for k in range(K4):
                    ins = V.bn_stats(stats[l][:, k, :], src(k))
                ch.link(ins)
                dve.sem_inc(sem("waited"), 1)
                for k in range(K4):
                    ins = V.bn_aggr(mv[l][:, k, :], stats[l][:, k, :])
                ch.link(ins)
                V.tensor_scalar(ve[l][:, :], mv[l][:, :, 1], EPS, None, ALU.add).then_inc(sem("ve_" + l), 1)

            def norm_apply(l, dst, src, c):
                dve.wait_ge(sem("rstd_" + l), c + 1)
                for k in range(K4):
                    ins = V.tensor_scalar(dst(k), src(k), mv[l][:, k, 0:1], rstd[l][:, k:k + 1], ALU.subtract, ALU.mult)
                return ins

            blk = lambda t: (lambda k: t[:, k, :])
            attn_blk = lambda k: attn[:, :, k, :]

            def in0(c, past):
                dve.wait_ge(sem("attn_loaded"), c * 16 + 16)
                norm_stats("attn", attn_blk, c)

            def in1(c, past):
                dve.wait_ge(sem("uT_mm"), c)
                norm_apply("attn", lambda k: t1[:, k, :].rearrange("p (h d) -> p h d", h=H), attn_blk, c).then_inc(sem("attn_used"), 1)
                dve.wait_ge(sem("attn_used"), c + 1)
                dve.wait_ge(sem("x0_loaded"), c * 16 + 16)
                V.tensor_tensor(x1[:, :, :], x0[:, :, :], t1[:, :, :], ALU.add).then_inc(sem("x1_done"), 1)
                dve.wait_ge(sem("x1_done"), c + 1)
                norm_stats("x1", blk(x1), c)

            def in2(c, past):
                dve.wait_ge(sem("n2_stored"), c * 16)
                norm_apply("x1", blk(n1), blk(x1), c).then_inc(sem("n1_done"), 1)

            def mix(c, past):
                ch = Chain(dve, sem("mix_step"), c * 2 * KC)
                dve.wait_ge(sem("n1T_done"), c + 1)
                dve.wait_ge(sem("r_mm"), c)
                dve.wait_ge(sem("q_done"), c)
                pairs = ((xk, "mu_k", 1), (xr, "mu_r", 0))
                for dst, mu, i in pairs:
                    for h in range(KC):
                        ch.done(V.tensor_scalar(dst[:, h, :], n1T[:, h, 0:N], one_minus_mu[:, i, h:h + 1], None, ALU.mult))
                ch.wait()
                for dst, mu, i in pairs:
                    for h in range(KC):
                        ins = V.scalar_tensor_tensor(dst[:, h, :], n1T[:, h, 1:N + 1], W[mu][:, 0, h:h + 1], dst[:, h, :], ALU.mult, ALU.add)
                ins.then_inc(sem("mixed"), 1)
                dve.wait_ge(sem("mixed"), c + 1)
                V.tensor_scalar(n1T[:, :, 0:1], n1T[:, :, N:N + 1], keep[:, bass.ds(c + 1, 1)], None, ALU.mult).then_inc(sem("carried"), 1)

            def rk(c, past):
                dve.wait_ge(sem("k_read"), c + 1)
                dve.wait_ge(sem("val_mm"), c)
                V.tensor_tensor(k_act[:, :, :], k_relu[:, :, :], k_relu[:, :, :], ALU.mult).then_inc(sem("k_act_done"), 1)

            def val(c, past):
                ch = Chain(dve, sem("val_step"), c * 4)
                dve.wait_ge(sem("val_mm"), c + 1)
                dve.wait_ge(sem("r_read"), c + 1)
                V.tensor_tensor(flat(f), wide(2, 2), flat(r_gate), ALU.mult).then_inc(sem("f_done"), 1)
                dve.wait_ge(sem("f_done"), c + 1)
                norm_stats("f", blk(f), c)
                ch.link(norm_apply("f", blk(t1), blk(f), c))
                dve.wait_ge(sem("x2_stored"), c * 16)
                V.tensor_tensor(x2[:, :, :], x1[:, :, :], t1[:, :, :], ALU.add).then_inc(sem("x2_done"), 1)
                dve.wait_ge(sem("x2_done"), c + 1)
                norm_stats("x2", blk(x2), c)
                norm_apply("x2", blk(n1), blk(x2), c).then_inc(sem("n2_done"), 1)
                ch.link(V.tensor_tensor(ve_n2[:, :], rstd["x2"][:, :], rstd["x2"][:, :], ALU.mult))
                ch.link(V.tensor_tensor(ve_n2[:, :], ve_n2[:, :], mv["x2"][:, :, 1], ALU.mult))
                V.tensor_scalar(ve_n2[:, :], ve_n2[:, :], EPS, None, ALU.add).then_inc(sem("ve_n2"), 1)
                dve.wait_ge(sem("n2_done"), c + 1)
                dve.wait_ge(sem("rstd_n2"), c + 1)
                for k in range(K4):
                    ins = V.scalar_tensor_tensor(t1[:, k, :], n1[:, k, :], rstd_n2[:, k:k + 1], W["g1"], ALU.mult, ALU.mult)
                ch.link(ins)
                V.tensor_tensor(t1[:, :, :], t1[:, :, :], W["be1"].unsqueeze(1).broadcast_to([P, K4, C]), ALU.add).then_inc(sem("u_done"), 1)

            def qkv(c, past):
                dve.wait_ge(sem("k2_mm"), c + 1)
                V.tensor_scalar(flat(k_exp), wide(2, 2), 0.0, None, ALU.min).then_inc(sem("k_low"), 1)
                dve.wait_ge(sem("q_mm"), c + 1)
                V.tensor_scalar(flat(q_exp), wide(0, 2), 0.0, None, ALU.min).then_inc(sem("q_low"), 1)
                dve.wait_ge(sem("k_exp_done"), c + 1)
                V.scalar_tensor_tensor(flat(k_feat), wide(2, 2), 0.0, flat(k_exp), ALU.max, ALU.add).then_inc(sem("k_feat_done"), 1)
                dve.wait_ge(sem("q_exp_done"), c + 1)
                dve.wait_ge(sem("q_stored"), c * 16)
                V.scalar_tensor_tensor(flat(q), wide(0, 2), 0.0, flat(q_exp), ALU.max, ALU.add).then_inc(sem("q_done"), 1)

            def kv(c, past):
                dve.wait_ge(sem("kv_mm"), c + 1)
                slot = kv_sums[:, bass.ds(c // CB, 1), :].rearrange("p a n -> p (a n)")
                V.scalar_tensor_tensor(slot, slot, keep[:, bass.ds(c, 1)], ps[:, 2, 0:KC * KVW], ALU.mult, ALU.add).then_inc(sem("kv_done"), 1)
                dve.wait_ge(sem("kv_done"), c + 1)

            def msg(c, past):
                ch = Chain(dve, sem("msg_step"), c * K4)
                dve.wait_ge(sem("msg_mm"), c * K4)
                for h in range(HG):
                    rows = slice(h * DG, (h + 1) * DG)
                    src = kv_sums[rows, bass.ds(c // CB, 1), :].rearrange("p a (g n) -> p (a g) n", g=KC)
                    V.tensor_copy(kv_diag[rows, :, h * DG:(h + 1) * DG], src[:, :, h * DG:(h + 1) * DG])
                    ins = V.tensor_copy(kv_diag[rows, :, HG * DG + h:HG * DG + h + 1], src[:, :, P:P + 1])
                ins.then_inc(sem("kv_diag_done"), 1)
                dve.wait_ge(sem("msg_mm"), c * K4 + K4)
                for k in range(0, K4, 2):
                    both = ps[:, MSG_BANKS[k]:MSG_BANKS[k] + 2, 0:KC * MSGW].rearrange("p k (g n) -> p k g n", g=KC)
                    ch.link(V.tensor_scalar(denom[:, k:k + 2, :, :], both[:, :, :, HG * DG:MSGW], EPS_ATTN, None, ALU.add))
                    ch.link(V.reciprocal(denom[:, k:k + 2, :, :], denom[:, k:k + 2, :, :]))
                    for i in range(2):
                        ins = V.tensor_tensor(t2[:, k + i, :].rearrange("p (g h d) -> p g h d", g=KC, h=HG),
                                              both[:, i, :, 0:HG * DG].rearrange("p g (h d) -> p g h d", h=HG),
                                              denom[:, k + i, :, :].unsqueeze(3).broadcast_to([P, KC, HG, DG]), ALU.mult)
                ins.then_inc(sem("msg_read"), 1)
                dve.wait_ge(sem("msg_read"), c + 1)
                dve.wait_ge(sem("n2_loaded"), c * 16 + 16)
                dve.wait_ge(sem("x3_b2_done"), c)
                V.tensor_tensor(x3[:, :, :], n2_in[:, :, :], t2[:, :, :], ALU.add).then_inc(sem("x3_done"), 1)
                dve.wait_ge(sem("x3_done"), c + 1)
                norm_stats("x3", blk(x3), c)

            def y_in(c, past):
                ch = Chain(dve, sem("y_step"), c)
                dve.wait_ge(sem("rstd_x3"), c + 1)
                for k in range(K4):
                    ins = V.scalar_tensor_tensor(t2[:, k, :], x3[:, k, :], mv["x3"][:, k, 0:1], W["g2"], ALU.subtract, ALU.mult)
                ch.link(ins)
                for k in range(K4):
                    ins = V.scalar_tensor_tensor(t2[:, k, :], t2[:, k, :], rstd["x3"][:, k:k + 1], W["be2"], ALU.mult, ALU.add)
                ins.then_inc(sem("y_in_done"), 1)

            def proj1(c, past):
                ch = Chain(dve, sem("proj_step"), c)
                dve.wait_ge(sem("proj_mm"), c * 2 + 2)
                dve.wait_ge(sem("x3_b2_done"), c + 1)
                V.tensor_tensor(flat(o), wide(6, 2), flat(x3_b2), ALU.add).then_inc(sem("o_done"), 1)
                dve.wait_ge(sem("o_done"), c + 1)
                norm_stats("o", blk(o), c)
                dve.wait_ge(sem("yT_mm"), c + 1)
                ch.link(norm_apply("o", blk(t2), blk(o), c))
                dve.wait_ge(sem("x2_loaded"), c * 16 + 16)
                dve.wait_ge(sem("x4_kept"), c)
                V.tensor_tensor(x4[:, :, :], x2_in[:, :, :], t2[:, :, :], ALU.add).then_inc(sem("x4_done"), 1)
                dve.wait_ge(sem("x4_done"), c + 1)
                norm_stats("x4", blk(x4), c)
                norm_apply("x4", blk(t2), blk(x4), c).then_inc(sem("n4_done"), 1)

            def up(m):
                def f(c, past):
                    dve.wait_ge(sem("silu_done"), c * M2 + m + 1)
                    dve.wait_ge(sem("up_mm"), c * M2 + m + 1)
                    if m == 0:
                        dve.wait_ge(sem("down_mm"), c)
                    V.tensor_tensor(gated[:, m, :], ps[:, up_bank(m) + 1, :], gate[:, m % 2, :], ALU.mult).then_inc(sem("gated_done"), 1)
                return f

            def end(c, past):
                dve.wait_ge(sem("down_mm"), c + 1)
                ffn_blk = lambda k: blocks(4)[:, k, :]
                norm_stats("ffn", ffn_blk, c)
                dve.wait_ge(sem("stored"), c * 16)
                norm_apply("ffn", blk(y_out), ffn_blk, c).then_inc(sem("ffn_read"), 1)
                dve.wait_ge(sem("ffn_read"), c + 1)
                dve.wait_ge(sem("x4_kept"), c + 1)
                V.tensor_tensor(y_out[:, :, :], y_out[:, :, :], x4_kept[:, :, :], ALU.add).then_inc(sem("y_done"), 1)

            run(dve, {"in0": in0, "in1": in1, "in2": in2, "mix": mix, "rk": rk, "val": val, "qkv": qkv, "kv": kv, "msg": msg, "y": y_in, "proj1": proj1,
                      "end": end, **{f"up{m}": up(m) for m in range(M2)}})


def transformer(nc, x, rot, ent, floats, ints, rows, out):
    with ExitStack() as ctx:
        sb = lambda n, s: ctx.enter_context(nc.sbuf_tensor(n, s, F32))
        stage_mem = sb("stage_mem", [P, max(3 * BB * C, FLOAT_COLS + INT_COLS)])
        row_mem = sb("row_mem", [P, len(ROWS), C])
        ident = sb("ident", [P, P])
        heads_dram = nc.dram_tensor("heads_dram", [NHD, P, BB * D], F32, kind="Internal").ap()
        W, at = {}, 0
        for name, k, n in FLOAT_WEIGHTS + INT_WEIGHTS:
            W[name] = stage_mem[:, at:at + k * n].rearrange("p (k n) -> p k n", k=k)
            at += k * n
        for i, name in enumerate(ROWS):
            W[name] = row_mem[:, i, :]
        softmax_attention(nc, x, rot, ent, floats, ints, rows, stage_mem, row_mem, ident, heads_dram)
        later_layers(nc, heads_dram, x, W, ident, out)


def kernel(**inputs):
    import numpy as np
    import concourse.bacc as bacc
    from concourse.bass_utils import run_bass_kernel_spmd

    def on_partitions(w):
        k = w.shape[0] // P
        return w.reshape(k, P, -1).transpose(1, 0, 2).reshape(P, -1)

    a = {name: np.asarray(v) for name, v in inputs.items()}
    vec = lambda name: a[name].reshape(-1, P).T
    mat = lambda *names: on_partitions(np.concatenate([a[n].T for n in names], axis=1))
    arrays = {
        "in_x_dram": a["L0_attn_inputs"],
        "in_rot_dram": a["L0_attn_rotation_params"],
        "in_ent_dram": a["L0_attn_entangle_params"],
        "in_floats_dram": np.concatenate([mat("L0_ffn_W_r"), mat("L0_ffn_W_k"), mat("L0_ffn_W_v"), mat("L1_attn_wq"), mat("L1_attn_wk", "L1_attn_wv"),
                                          mat("L1_attn_w1"), mat("L1_attn_w2"), vec("L0_ffn_mu_r"), vec("L0_ffn_mu_k"), vec("L1_attn_b1")], axis=1),
        "in_ints_dram": np.concatenate([mat("L1_ffn_w_gate"), mat("L1_ffn_w_up"), mat("L1_ffn_w_down")], axis=1),
        "in_rows_dram": np.concatenate([a["L1_attn_" + n] for n in ROWS]),
    }
    arrays = {n: np.ascontiguousarray(v) for n, v in arrays.items()}
    nc = bacc.Bacc("TRN2", target_bir_lowering=False, num_devices=1)
    args = [nc.dram_tensor(n, v.shape, mybir.dt.from_np(v.dtype), kind="ExternalInput").ap() for n, v in arrays.items()]
    out = nc.dram_tensor("out_0_dram", (B, T, C), F32, kind="ExternalOutput").ap()
    transformer(nc, *args, out)
    r = run_bass_kernel_spmd(nc, [arrays], core_ids=[0])
    return r.results[0]["out_0_dram"]
```

```python
import concourse.bass as bass
from concourse import mybir
from concourse.alu_op_type import AluOpType as ALU
from contextlib import ExitStack

F32, BF16, I32 = mybir.dt.float32, mybir.dt.bfloat16, mybir.dt.int32
ACT = mybir.ActivationFunctionType
AX = mybir.AxisListType

P = 128
B, T, C = 4, 2048, 256
EPS = 1e-5

H, D = 16, 16
NHD = B * H
BB = T // P
NB = B * BB
BANK = 512
QC = T // BANK
GH = P // D
GROUPS = NHD // GH
HALVES = 2 * BB
SLOTS = 3
AHEAD = 3
ROUNDS = QC
ROUND_AT, GENERAL_AT = 4, 8
PARTS = 3
PRODUCTS = 6
BIAS = PRODUCTS * D
ROWS_QK = BIAS + PARTS
SAFE = 75.0
PROBS = 4

N = 512
NC = B * T // N
CB = T // N
K4 = N // P
KC = C // P
F1, F2 = 1024, 768
M1, M2 = F1 // P, F2 // P
HG, DG = 4, 32
KVW = HG * DG + 2
MSGW = HG * DG + HG
EPS_ATTN = 1e-6
DEQUANT = 1.0 / 127.0

FLOAT_WEIGHTS = (("wr", KC, C), ("wk", KC, C), ("wv", KC, C), ("aq", KC, C), ("akv", KC, 2 * C), ("w1", KC, F1), ("w2", M1, C),
                 ("mu_r", 1, KC), ("mu_k", 1, KC), ("b1", 1, M1))
INT_WEIGHTS = (("wg", KC, F2), ("wu", KC, F2), ("wd", M2, C))
ROWS = ("b2", "g1", "be1", "g2", "be2")
FLOAT_COLS = sum(k * n for _, k, n in FLOAT_WEIGHTS)
INT_COLS = sum(k * n for _, k, n in INT_WEIGHTS)


class Chain:

    def __init__(self, eng, sem, base=0):
        self.eng, self.sem, self.base, self.n = eng, sem, base, 0

    def done(self, ins):
        ins.then_inc(self.sem, 1)
        self.n += 1

    def wait(self):
        self.eng.wait_ge(self.sem, self.base + self.n)

    def link(self, ins):
        self.done(ins)
        self.wait()


def slot_of(at):
    at %= GH * HALVES
    return 1 if at == GH * HALVES - 1 else at % SLOTS


def last_use(at):
    return max(g for g in range(at) if slot_of(g) == slot_of(at))


def softmax_attention(nc, x_in, rot, ent, floats, ints, rows, weight_mem, row_mem, ident, heads_out):
    with ExitStack() as ctx:
        sb = lambda n, s, d=F32: ctx.enter_context(nc.sbuf_tensor(n, s, d))
        sem = lambda n: ctx.enter_context(nc.semaphore(n))

        xs = sb("xs", [P, B * BB, C])
        result = sb("result", [P, 2, BB, D])
        identb = sb("identb", [P, P], BF16)
        neghalf = sb("neghalf", [P, BB])
        rot_row, ent_row = sb("rot_row", [P, C]), sb("ent_row", [P, C])
        rot_col, ent_col = sb("rot_col", [P, KC]), sb("ent_col", [P, KC])
        q_factor, k_factor = sb("q_factor", [P, GROUPS]), sb("k_factor", [P, GROUPS])
        stats, mv, ve, rstd = sb("stats", [P, BB, 6]), sb("mv", [P, BB, 2]), sb("ve", [P, BB]), sb("rstd", [P, BB])
        weighted = sb("weighted", [P, GH, BB, D])
        bound, widest = sb("bound", [P, GH, BB]), sb("widest", [P, 2, GH])
        flags = sb("flags", [P, NHD], I32)
        probs = sb("probs", [P, PROBS, T])
        staged = sb("staged", [P, QC, P])
        qk = sb("qk", [P, 2, BANK])
        parts = [sb(f"parts{i}", [P, 2 * PARTS, BANK], BF16) for i in range(2)]
        qT = [sb(f"qT{i}", [P, T], BF16) for i in range(2)]
        kT = [sb(f"kT{i}", [P, T], BF16) for i in range(2)]
        vals = [sb(f"vals{i}", [P, BB, 32]) for i in range(2)]
        sums = sb("sums", [P, BANK])
        recip = sb("recip", [P, QC, QC])
        chunk_max, neg_max = sb("chunk_max", [P, BB, QC]), sb("neg_max", [P, BB, 2])
        max_split = sb("max_split", [P, BB, P], BF16)

        split_dram = nc.dram_tensor("split_dram", [GROUPS, 2 * PARTS, P, T], BF16, kind="Internal").ap()

        ps = ctx.enter_context(nc.psum_tensor("ps", [P, 8, BANK], F32))
        SCORES = [ps[:, 2 * s:2 * s + 2, :].rearrange("p a n -> p (a n)") for s in range(SLOTS)]
        ACC = ps[:, 6, :]
        TURN = ps[:, 7, :]
        TURNB = TURN.bitcast(BF16)

        rot_loaded, weights_loaded, weights_ready = sem("rot_loaded"), sem("weights_loaded"), sem("weights_ready")
        x_loaded = [sem(f"x_loaded{b}") for b in range(B)]
        pool_init, consts, setup_step = sem("pool_init"), sem("consts"), sem("setup_step")
        var_ready, rstd_ready, normed, norm_step = sem("var_ready"), sem("rstd_ready"), sem("normed"), sem("norm_step")
        round_staged, round_full, round_read, split_step, parts_ready = (sem(n) for n in ("round_staged", "round_full", "round_read", "split_step", "parts_ready"))
        split_stored = [sem(f"split_stored{i}") for i in range(2)]
        bound_step, bound_ready, widest_ready, flags_ready = sem("bound_step"), sem("bound_ready"), sem("widest_ready"), sem("flags_ready")
        qk_loaded = [sem(f"qk_loaded{i}") for i in range(2)]
        bias_clear, vals_ready, operands_ready = sem("bias_clear"), sem("vals_ready"), sem("operands_ready")
        scores_ready, exps_done, probs_free = sem("scores_ready"), sem("exps_done"), sem("probs_free")
        acc_free, sums_ready, result_full, recip_ready, result_read = (sem(n) for n in ("acc_free", "sums_ready", "result_full", "recip_ready", "result_read"))
        max_full, max_free, max_ready, max_step = sem("max_full"), sem("max_free"), sem("max_ready"), sem("max_step")
        heads_stored = [sem(f"heads_stored{i}") for i in range(2)]
        waited = sem("waited")

        MAX_USES = BB * QC + 2
        MAX_STEPS = 5
        SPLIT_STEPS = 4
        LOADS = 6 * 16

        block = ctx.enter_context(nc.Block())

        @block.sync
        def _(sp):
            for dst, src in ((rot_row, rot), (ent_row, ent)):
                sp.dma_start(dst[:, :], src.rearrange("h d -> (h d)").partition_broadcast(P)).then_inc(rot_loaded, 16)
            for dst, src in ((rot_col, rot), (ent_col, ent)):
                for half in range(KC):
                    sp.dma_start(dst[:, half:half + 1], src[half * GH:(half + 1) * GH, :].rearrange("h d -> (h d)").unsqueeze(1)).then_inc(rot_loaded, 16)

            def load_x(b):
                sp.dma_start(xs[:, b * BB:(b + 1) * BB, :], x_in[b].rearrange("(k p) c -> p k c", p=P)).then_inc(x_loaded[b], 16)

            def store_round(group, r):
                sp.wait_ge(parts_ready, group * ROUNDS + r + 1)
                sp.dma_start(split_dram[bass.ds(group, 1), :, :, r * BANK:(r + 1) * BANK].rearrange("g s p t -> p (g s) t"),
                             parts[r % 2][:, :, :]).then_inc(split_stored[r % 2], 16)

            def load_operands(head, group, e):
                buf = e % 2
                if e == 0:
                    for stored in split_stored:
                        sp.wait_ge(stored, (group + 1) * (ROUNDS // 2 * 16))
                        sp.sem_inc(waited, 1)
                if not (isinstance(head, int) and head < 2):
                    sp.wait_ge(scores_ready, (head - 1) * HALVES)
                src = split_dram[bass.ds(group, 1), :, e * D:(e + 1) * D, :].rearrange("g s p t -> (g s) p t")
                at = 0
                for i in range(PARTS):
                    n = PARTS - i
                    q_src = src[i:i + 1].broadcast_to([n, D, T])
                    sp.dma_start(qT[buf][at:at + n * D, :], q_src).then_inc(qk_loaded[buf], 16)
                    sp.dma_start(kT[buf][at:at + n * D, :], src[PARTS:PARTS + n]).then_inc(qk_loaded[buf], 16)
                    at += n * D

            def store_result(head, buf):
                sp.wait_ge(result_read, head + 2)
                sp.dma_start(heads_out[bass.ds(head, 1)].rearrange("a p n -> p (a n)"),
                             result[:, buf, :, :].rearrange("p k d -> p (k d)")).then_inc(heads_stored[buf], 16)

            for b in range(B):
                load_x(b)
            for r in range(ROUNDS):
                store_round(0, r)
            load_operands(0, 0, 0)
            sp.dma_start(weight_mem[:, 0:FLOAT_COLS], floats).then_inc(weights_loaded, 16)
            sp.dma_start(weight_mem[:, FLOAT_COLS:].bitcast(I32), ints).then_inc(weights_loaded, 16)
            sp.dma_start(row_mem[:, :, :].rearrange("p a c -> p (a c)"), rows.partition_broadcast(P)).then_inc(weights_loaded, 16)

            def group_of_heads(group, last):
                for e in range(GH):
                    head = group * GH + e
                    if e + 1 < GH:
                        load_operands(head + 1, group, e + 1)
                    elif not last:
                        load_operands(head + 1, group + 1, 0)
                    if not (isinstance(head, int) and head == 0):
                        store_result(head - 1, (e + 1) % 2)
                    if e < ROUNDS and not last:
                        store_round(group + 1, e)

            group_of_heads(0, False)
            with sp.Fori(1, GROUPS - 1) as group:
                group_of_heads(group, False)
            group_of_heads(GROUPS - 1, True)
            store_result(NHD - 1, (GH - 1) % 2)
            for stored in heads_stored:
                sp.wait_ge(stored, 16 * NHD // 2)

        @block.gpsimd
        def _(pool):
            pool.memset(neghalf[:, :], -0.5).then_inc(pool_init, 1)
            for m in (ident, identb):
                pool.memset(m[:, :], 0.0).then_inc(pool_init, 1)
            pool.wait_ge(pool_init, 3)
            for m in (ident, identb):
                pool.affine_select(out=m[:, :], in_=m[:, :], compare_op=ALU.not_equal, fill=1.0, base=0,
                                   pattern=[[-1, P]], channel_multiplier=1).then_inc(consts, 1)

            def inverse_std(b):
                pool.wait_ge(var_ready, b + 1)
                pool.tensor_tensor(rstd[:, :], ve[:, :], neghalf[:, :], ALU.pow).then_inc(rstd_ready, 1)

            def widest_of(group):
                pool.wait_ge(bound_ready, group + 1)
                pool.partition_all_reduce(widest[:, 1, :], widest[:, 0, :], P, bass.bass_isa.ReduceOp.max).then_inc(widest_ready, 1)

            inverse_std(0)
            widest_of(0)
            widest_of(1)
            for b in range(1, B):
                inverse_std(b)
            for group in range(2, GROUPS):
                widest_of(group)

        @block.tensor
        def _(pe):
            pe.wait_ge(consts, 2)
            pe.sem_inc(probs_free, PROBS)
            pe.sem_inc(acc_free, 1)
            pe.sem_inc(max_free, 1)
            pe.sem_inc(result_read, 1)

            def turn_round(group, r):
                pe.wait_ge(round_staged, group * ROUNDS + r + 1)
                for k in range(QC):
                    last = nc.tensor.transpose(TURN[:, k * P:(k + 1) * P], staged[:, k, :], ident[:, :])
                last.then_inc(round_full, 1)

            def half_scores(i, slot, buf):
                j, half = i // 2, i % 2
                for n in range(2):
                    q0 = half * T // 2 + n * BANK
                    last = nc.tensor.matmul(SCORES[slot][:, n * BANK:(n + 1) * BANK], kT[buf][0:ROWS_QK, j * P:(j + 1) * P],
                                            qT[buf][0:ROWS_QK, q0:q0 + BANK], start=True, stop=True)
                last.then_inc(scores_ready, 1)

            def general_scores(head, group, e):
                buf = e % 2
                if e == 0:
                    pe.wait_ge(flags_ready, group + 1)
                pe.sem_inc(waited, 1)
                general = pe.value_load(flags[0:1, bass.ds(head, 1)], min_val=0, max_val=1)
                with pe.If(general > 0):
                    pe.wait_ge(qk_loaded[buf], (group * (GH // 2) + e // 2 + 1) * LOADS)
                    pe.wait_ge(bias_clear, head + 1)
                    pe.sem_inc(waited, 1)
                    with pe.Fori(0, BB) as k:
                        for c in range(QC):
                            pe.wait_ge(max_free, head * MAX_USES + k * QC + c + 1)
                            nc.tensor.matmul(TURN, qT[buf][0:ROWS_QK, bass.ds(k * P, P)], kT[buf][0:ROWS_QK, c * BANK:(c + 1) * BANK],
                                             start=True, stop=True).then_inc(max_full, 1)
                    pe.wait_ge(max_ready, head + 1)
                    for r in range(2):
                        pe.wait_ge(max_free, head * MAX_USES + BB * QC + r + 1)
                        for k in range(BB // 2):
                            last = nc.tensor.transpose(TURNB[:, k * P:(k + 1) * P], max_split[:, r * BB // 2 + k, :], identb[:, :])
                        last.then_inc(max_full, 1)
                    pe.wait_ge(max_free, (head + 1) * MAX_USES + 1)
                with pe.Else():
                    pe.sem_inc(max_full, MAX_USES)

            def operands(head, group, e):
                pe.wait_ge(operands_ready, head + 1)
                pe.wait_ge(qk_loaded[e % 2], (group * (GH // 2) + e // 2 + 1) * LOADS)

            for r in range(ROUNDS):
                if r > 0:
                    pe.wait_ge(round_read, r)
                turn_round(0, r)
            pe.wait_ge(round_read, ROUNDS)
            general_scores(0, 0, 0)
            operands(0, 0, 0)
            for i in range(2 * AHEAD):
                if i >= SLOTS:
                    pe.wait_ge(exps_done, i - SLOTS + 1)
                half_scores(i, slot_of(i), 0)

            def group_of_heads(group, last_group):
                first = group * GH * HALVES
                for e in range(GH):
                    head, buf, last = group * GH + e, e % 2, last_group and e == GH - 1
                    nxt, nxt_group, nxt_e = head + 1, group + (e + 1) // GH, (e + 1) % GH
                    for j in range(BB):
                        pe.wait_ge(exps_done, head * HALVES + 2 * j + 2)
                        if j == 0:
                            pe.wait_ge(acc_free, head + 1)
                        for c in range(QC):
                            mm = nc.tensor.matmul(ACC[32 * c:32 * c + 32, :], vals[buf][:, j, :], probs[:, j % PROBS, c * BANK:(c + 1) * BANK],
                                                  start=(j == 0), stop=(j == BB - 1), tile_position=(0, 32 * c))
                        mm.then_inc(probs_free, 1)
                        if j == ROUND_AT and e < ROUNDS and not last_group:
                            pe.wait_ge(result_read, head + 1)
                            turn_round(group + 1, e)
                        if j == GENERAL_AT and not last:
                            rounds = group * ROUNDS + ROUNDS + (0 if last_group else min(e + 1, ROUNDS))
                            pe.wait_ge(round_read, rounds)
                            pe.wait_ge(result_read, head + 1)
                            general_scores(nxt, nxt_group, nxt_e)
                        if j + AHEAD == BB and not last:
                            operands(nxt, nxt_group, nxt_e)
                        for half in range(2):
                            i = 2 * (j + AHEAD) + half
                            if i >= HALVES and last:
                                continue
                            at = e * HALVES + i
                            pe.wait_ge(exps_done, first + last_use(at) + 1)
                            half_scores(i % HALVES, slot_of(at), buf if i < HALVES else 1 - buf)
                    pe.wait_ge(sums_ready, head + 1)
                    if last:
                        pe.wait_ge(result_read, head + 1)
                    for t in range(QC):
                        mm = nc.tensor.transpose(TURN[:, t * P:(t + 1) * P], sums[:, t * P:(t + 1) * P], ident[:, :])
                    mm.then_inc(result_full, 1)

            with pe.Fori(0, GROUPS - 1) as group:
                group_of_heads(group, False)
            group_of_heads(GROUPS - 1, True)

        @block.scalar
        def _(act):
            with act.Fori(0, GROUPS) as group:
                for at in range(GH * HALVES):
                    j, half = at // 2, at % 2
                    if half == 0:
                        act.wait_ge(probs_free, group * GH * BB + j + 1)
                    act.wait_ge(scores_ready, group * GH * HALVES + at + 1)
                    nc.scalar.activation(probs[:, j % PROBS, half * T // 2:(half + 1) * T // 2], SCORES[slot_of(at)], ACT.Exp).then_inc(exps_done, 1)

        @block.vector
        def _(dve):
            V = nc.vector
            setup = Chain(dve, setup_step)
            setup.done(V.memset(max_split[:, :, :], 0.0))
            for t in kT:
                setup.done(V.memset(t[BIAS:BIAS + PARTS, :], 1.0))
            for t in vals:
                setup.done(V.memset(t[:, :, :], 0.0))
            setup.wait()
            for t in vals:
                setup.done(V.memset(t[:, :, D:D + 1], 1.0))
            dve.wait_ge(rot_loaded, 16 * (2 + 2 * KC))
            for half in range(KC):
                setup.done(V.tensor_scalar(q_factor[:, half:GROUPS:KC], rot_col[:, half:half + 1].broadcast_to([P, B]), D ** -0.5, None, ALU.mult))
                setup.done(V.tensor_copy(k_factor[:, half:GROUPS:KC], ent_col[:, half:half + 1].broadcast_to([P, B])))
            setup.done(V.scalar_tensor_tensor(rot_row[:, :], rot_row[:, :], D ** -0.5, ent_row[:, :], ALU.mult, ALU.mult))
            setup.wait()

            def norm(b):
                ch = Chain(dve, norm_step, b * 2)
                x = lambda k: xs[:, b * BB + k, :]
                dve.wait_ge(x_loaded[b], 16)
                for k in range(BB):
                    ins = V.bn_stats(stats[:, k, :], x(k))
                ch.link(ins)
                for k in range(BB):
                    ins = V.bn_aggr(mv[:, k, :], stats[:, k, :])
                ch.link(ins)
                V.tensor_scalar(ve[:, :], mv[:, :, 1], EPS, None, ALU.add).then_inc(var_ready, 1)
                dve.wait_ge(rstd_ready, b + 1)
                for k in range(BB):
                    ins = V.tensor_scalar(x(k), x(k), mv[:, k, 0:1], rstd[:, k:k + 1], ALU.subtract, ALU.mult)
                ins.then_inc(normed, 1)
                dve.wait_ge(normed, b + 1)

            def split_round(group, r):
                ch = Chain(dve, split_step, (group * ROUNDS + r) * SPLIT_STEPS)
                cut = lambda i: parts[r % 2][:, i:2 * PARTS:PARTS, :]
                V.tensor_copy(staged[:, :, :], xs[:, bass.ds(group // KC * BB + r * QC, QC), bass.ds(group % KC * P, P)]).then_inc(round_staged, 1)
                dve.wait_ge(round_full, group * ROUNDS + r + 1)
                if not (isinstance(group, int) and group * ROUNDS + r < 2):
                    dve.wait_ge(split_stored[r % 2], (group * (ROUNDS // 2) + r // 2) * 16)
                V.tensor_scalar(qk[:, 0, :], TURN, q_factor[:, bass.ds(group, 1)], None, ALU.mult)
                V.tensor_scalar(qk[:, 1, :], TURN, k_factor[:, bass.ds(group, 1)], None, ALU.mult).then_inc(round_read, 1)
                dve.wait_ge(round_read, group * ROUNDS + r + 1)
                ch.link(V.tensor_copy(cut(0), qk[:, :, :]))
                ch.link(V.tensor_tensor(qk[:, :, :], qk[:, :, :], cut(0), ALU.subtract))
                ch.link(V.tensor_copy(cut(1), qk[:, :, :]))
                ch.link(V.tensor_tensor(cut(2), qk[:, :, :], cut(1), ALU.subtract))
                dve.sem_inc(parts_ready, 1)

            def bounds(group):
                ch = Chain(dve, bound_step, group * 4)
                x = xs[:, bass.ds(group // KC * BB, BB), bass.ds(group % KC * P, P)].rearrange("p k (h d) -> p h k d", h=GH)
                w = weights_of_group(group)
                ch.link(V.tensor_tensor(weighted[:, :, :, :], x, x, ALU.mult))
                ch.link(V.tensor_tensor(weighted[:, :, :, :], weighted[:, :, :, :], w, ALU.mult))
                ch.link(V.tensor_reduce(bound[:, :, :], weighted[:, :, :, :], AX.X, ALU.add, apply_absolute_value=True))
                V.tensor_reduce(widest[:, 0, :], bound[:, :, :], AX.X, ALU.max).then_inc(bound_ready, 1)
                dve.wait_ge(widest_ready, group + 1)
                ch.link(V.tensor_scalar(flags[:, bass.ds(group * GH, GH)], widest[:, 1, :], SAFE, None, ALU.is_gt))
                dve.sem_inc(flags_ready, 1)

            def weights_of_group(group):
                half = group % KC
                w = rot_row[:, half * GH * D:(half + 1) * GH * D] if isinstance(half, int) else rot_row[:, bass.ds(half * GH * D, GH * D)]
                return w.rearrange("p (h d) -> p h d", h=GH).unsqueeze(2).broadcast_to([P, GH, BB, D])

            def prepare(head, group, e):
                buf = e % 2
                if not (isinstance(head, int) and head < 2):
                    dve.wait_ge(scores_ready, (head - 1) * HALVES)
                V.memset(qT[buf][BIAS:BIAS + PARTS, :], 0.0).then_inc(bias_clear, 1)
                V.tensor_copy(vals[buf][:, :, 0:D], xs[:, bass.ds(group // KC * BB, BB), bass.ds(group % KC * P + e * D, D)]).then_inc(vals_ready, 1)
                general = dve.value_load(flags[0:1, bass.ds(head, 1)], min_val=0, max_val=1)
                with dve.If(general > 0):
                    with dve.Fori(0, BB) as k:
                        for c in range(QC):
                            dve.wait_ge(max_full, head * MAX_USES + k * QC + c + 1)
                            V.tensor_reduce(chunk_max[:, bass.ds(k, 1), c], TURN, AX.X, ALU.max).then_inc(max_free, 1)
                    dve.wait_ge(max_free, head * MAX_USES + BB * QC + 1)
                    ch = Chain(dve, max_step, head * MAX_STEPS)
                    rest, rest2, cut = neg_max[:, :, 0], neg_max[:, :, 1], max_split[:, :, BIAS:BIAS + PARTS]
                    ch.link(V.tensor_reduce(rest, chunk_max[:, :, :], AX.X, ALU.max, negate=True))
                    ch.link(V.tensor_copy(cut[:, :, 0], rest))
                    ch.link(V.tensor_tensor(rest2, rest, cut[:, :, 0], ALU.subtract))
                    ch.link(V.tensor_copy(cut[:, :, 1], rest2))
                    ch.link(V.tensor_tensor(cut[:, :, 2], rest2, cut[:, :, 1], ALU.subtract))
                    dve.sem_inc(max_ready, 1)
                    dve.wait_ge(bias_clear, head + 1)
                    for r in range(2):
                        dve.wait_ge(max_full, head * MAX_USES + BB * QC + r + 1)
                        V.tensor_copy(qT[buf][BIAS:BIAS + PARTS, r * T // 2:(r + 1) * T // 2], TURNB[BIAS:BIAS + PARTS, :]).then_inc(max_free, 1)
                    dve.wait_ge(max_free, (head + 1) * MAX_USES + 1)
                    dve.sem_inc(waited, 1)
                with dve.Else():
                    dve.sem_inc(max_free, MAX_USES)
                    dve.sem_inc(max_ready, 1)
                    dve.sem_inc(max_step, MAX_STEPS)
                dve.wait_ge(bias_clear, head + 1)
                dve.wait_ge(vals_ready, head + 1)
                dve.sem_inc(operands_ready, 1)

            def finish(head, group, e):
                dve.wait_ge(probs_free, head * BB + BB + PROBS)
                V.tensor_copy(sums[:, :], ACC).then_inc(sums_ready, 1)
                dve.wait_ge(sums_ready, head + 1)
                dve.sem_inc(acc_free, 1)
                dve.wait_ge(result_full, head + 1)
                turned = TURN.rearrange("p (t c d) -> p t c d", t=QC, c=QC)
                V.reciprocal(recip[:, :, :], turned[:, :, :, D]).then_inc(recip_ready, 1)
                dve.wait_ge(recip_ready, head + 1)
                dst = result[:, e % 2, :, :].rearrange("p (c t) d -> p t c d", c=QC)
                if not (isinstance(head, int) and head < 2):
                    dve.wait_ge(heads_stored[e % 2], (group * (GH // 2) + e // 2) * 16)
                V.tensor_tensor(dst, turned[:, :, :, 0:D], recip[:, :, :].unsqueeze(3).broadcast_to([P, QC, QC, D]), ALU.mult).then_inc(result_read, 1)

            norm(0)
            for r in range(ROUNDS):
                split_round(0, r)
            bounds(0)
            prepare(0, 0, 0)

            def group_of_heads(group, last_group):
                for e in range(GH):
                    head = group * GH + e
                    if e < ROUNDS and not last_group:
                        split_round(group + 1, e)
                    if isinstance(group, int) and group == 0 and ROUNDS < e < ROUNDS + B:
                        norm(e - ROUNDS)
                    if last_group and e == 1:
                        dve.wait_ge(weights_loaded, 48)
                        here = weight_mem[:, FLOAT_COLS:]
                        V.tensor_scalar(here, here.bitcast(I32), DEQUANT, None, ALU.mult).then_inc(weights_ready, 1)
                    if not (last_group and e == GH - 1):
                        prepare(head + 1, group + (e + 1) // GH, (e + 1) % GH)
                    if e == ROUNDS and not last_group:
                        bounds(group + 1)
                    finish(head, group, e)

            group_of_heads(0, False)
            with dve.Fori(1, GROUPS - 1) as group:
                group_of_heads(group, False)
            group_of_heads(GROUPS - 1, True)
            dve.wait_ge(weights_ready, 1)


SHIFT = {"l": CB, "0": 0, "1": 1, "a": CB + 1, "b": CB + 2}
ORDER = [("load_in", "0"), ("msg", "a"), ("load_msg", "l"), ("load_x2", "a"), ("up0", "b"), ("y", "a"), ("up1", "b"), ("up2", "b"), ("mix", "1"),
         ("up3", "b"), ("yT", "a"), ("up4", "b"), ("up5", "b"), ("rk", "1"), ("fc0", "a"), ("val", "1"), ("fc1", "a"), ("proj0", "a"),
         ("uT", "1"), ("proj1", "a"), ("qkv", "1"), ("in0", "0"), ("in1", "0"), ("down", "b"), ("in2", "0"), ("kv", "1"), ("nT", "a"), ("end", "b")]
STREAM = dict(ORDER)
PLACE = {stage: i for i, (stage, _) in enumerate(ORDER)}
LOOPS = [(0, 1, "0"), (1, 2, "01"), (2, CB + 1, "01"), (CB + 1, CB + 2, "01a"), (CB + 2, CB + 3, "01ab"), (CB + 3, NC, "01ab"), (NC, NC + 1, "1ab"), (NC + 1, NC + CB + 1, "ab"), (NC + CB + 1, NC + CB + 2, "b")]
SP_LOOPS = [(0, 1, "0"), (1, 2, "01"), (2, CB, "01"), (CB, CB + 1, "01l"), (CB + 1, CB + 2, "01la"), (CB + 2, CB + 3, "01lab"), (CB + 3, NC, "01lab"), (NC, NC + 1, "1lab"),
            (NC + 1, NC + CB, "lab"), (NC + CB, NC + CB + 1, "ab"), (NC + CB + 1, NC + CB + 2, "b")]


def run(eng, stages, loops=LOOPS):
    def once(it, first, end, streams):
        def counter(here):
            def chunks_past(there):
                shift = SHIFT[STREAM[there]]
                if first < shift:
                    return 0
                if first >= shift + NC:
                    return NC
                return it - shift + (PLACE[there] < PLACE[here])
            return chunks_past

        for stage, stream in ORDER:
            if stream in streams and stage in stages:
                stages[stage](it - SHIFT[stream], counter(stage))

    for first, end, streams in loops:
        if end - first == 1:
            once(first, first, end, streams)
        else:
            with eng.Fori(first, end) as it:
                once(it, first, end, streams)


def later_layers(nc, heads_in, x_in, W, ident, out):
    with ExitStack() as ctx:
        sb = lambda n, s, d=F32: ctx.enter_context(nc.sbuf_tensor(n, s, d))
        dram = lambda n: nc.dram_tensor(n, [NC, P, K4 * C], F32, kind="Internal").ap()
        sems = {}

        def sem(n):
            if n not in sems:
                sems[n] = ctx.enter_context(nc.semaphore(n))
            return sems[n]

        x2_dram, n2_dram, q_dram = dram("x2_dram"), dram("n2_dram"), dram("q_dram")

        tok = lambda n: sb(n, [P, K4, C])
        chan = lambda n: sb(n, [P, KC, N])
        flat = lambda t: t[:, :, :].rearrange("p a b -> p (a b)")
        attn = sb("attn", [P, H, K4, D])
        x0, x1, t1, n1, f, x2, r_gate = (tok(n) for n in ("x0", "x1", "t1", "n1", "f", "x2", "r_gate"))
        n1T = sb("n1T", [P, KC, N + 1])
        xr, xk, k_act, uT, q = (chan(n) for n in ("xr", "xk", "k_act", "uT", "q"))
        k_relu = chan("k_relu")
        q_exp, k_exp = xr, r_gate
        k_feat = tok("k_feat")
        v_ones = sb("v_ones", [P, K4, KC, KVW])
        kv_sums = sb("kv_sums", [P, B, KC * KVW])
        kv_diag = sb("kv_diag", [P, KC, MSGW])
        q_in = chan("q_in")
        n2_in, x3, x3_b2, t2, x2_in, x4, x4_kept, y_out = (tok(n) for n in ("n2_in", "x3", "x3_b2", "t2", "x2_in", "x4", "x4_kept", "y_out"))
        o = f
        yT, n4T = chan("yT"), chan("n4T")
        denom = sb("denom", [P, K4, KC, HG])
        hT = sb("hT", [P, M1, N])
        gate = sb("gate", [P, 2, N])
        gated = sb("gated", [P, M2, N])
        norms = ("attn", "x1", "f", "x2", "x3", "o", "x4", "ffn")
        stats = {l: sb(f"stats_{l}", [P, K4, 6]) for l in norms}
        mv = {l: sb(f"mv_{l}", [P, K4, 2]) for l in norms}
        ve = {l: sb(f"ve_{l}", [P, K4]) for l in norms}
        rstd = {l: sb(f"rstd_{l}", [P, K4]) for l in norms}
        ve_n2, rstd_n2 = sb("ve_n2", [P, K4]), sb("rstd_n2", [P, K4])
        keep = sb("keep", [P, NC + 1])
        neghalf = sb("neghalf_k4", [P, K4])
        one_minus_mu = sb("one_minus_mu", [P, 2, KC])
        ps = ctx.enter_context(nc.psum_tensor("layers_ps", [P, 8, BANK], F32))
        banks = lambda a, n: ps[:, a:a + n, :]
        wide = lambda a, n: ps[:, a:a + n, :].rearrange("p a n -> p (a n)")
        blocks = lambda a: ps[:, a:a + 2, :].rearrange("p a (b n) -> p (a b) n", b=2)
        MSG_BANKS = (2, 3, 6, 7)
        up_bank = lambda m: (4, 2)[m % 2]

        block = ctx.enter_context(nc.Block())

        @block.sync
        def _(sp):
            heads_v = heads_in.rearrange("(b h) p (q n) -> b q p h n", b=B, q=CB)
            x_v = x_in.rearrange("b (q k p) c -> (b q) p k c", q=CB, p=P)
            out_v = out.rearrange("b (q k p) c -> (b q) p k c", q=CB, p=P)
            slab = lambda d, c: d[bass.ds(c, 1)].rearrange("a p n -> p (a n)")

            def load_in(c, past):
                sp.wait_ge(sem("attn_used"), c)
                sp.dma_start(attn[:, :, :, :].rearrange("p h k d -> p h (k d)"),
                             heads_v[bass.ds(c // CB, 1), bass.ds(c % CB, 1)].rearrange("a b p h n -> p (a b h) n")).then_inc(sem("attn_loaded"), 16)
                sp.wait_ge(sem("x1_done"), c)
                sp.dma_start(x0[:, :, :], x_v[bass.ds(c, 1)].rearrange("a p k c -> p (a k) c")).then_inc(sem("x0_loaded"), 16)

            def load_msg(c, past):
                sp.wait_ge(sem("msg_mm"), c * K4)
                sp.wait_ge(sem("q_stored"), c * 16 + 16)
                sp.dma_start(flat(q_in), slab(q_dram, c)).then_inc(sem("q_loaded"), 16)
                sp.wait_ge(sem("x3_done"), c)
                sp.wait_ge(sem("n2_stored"), c * 16 + 16)
                sp.dma_start(flat(n2_in), slab(n2_dram, c)).then_inc(sem("n2_loaded"), 16)

            def load_x2(c, past):
                sp.wait_ge(sem("x4_done"), c)
                sp.wait_ge(sem("x2_stored"), c * 16 + 16)
                sp.dma_start(flat(x2_in), slab(x2_dram, c)).then_inc(sem("x2_loaded"), 16)

            def store_x2_n2(c, past):
                sp.wait_ge(sem("x2_done"), c + 1)
                sp.dma_start(slab(x2_dram, c), flat(x2)).then_inc(sem("x2_stored"), 16)
                sp.wait_ge(sem("n2_done"), c + 1)
                sp.dma_start(slab(n2_dram, c), flat(n1)).then_inc(sem("n2_stored"), 16)

            def store_q(c, past):
                sp.wait_ge(sem("q_done"), c + 1)
                sp.dma_start(slab(q_dram, c), flat(q)).then_inc(sem("q_stored"), 16)

            def store_out(c, past):
                sp.wait_ge(sem("y_done"), c + 1)
                sp.dma_start(out_v[bass.ds(c, 1)].rearrange("a p k c -> p (a k) c"), y_out[:, :, :]).then_inc(sem("stored"), 16)

            run(sp, {"load_in": load_in, "load_msg": load_msg, "load_x2": load_x2, "uT": store_x2_n2, "kv": store_q, "end": store_out}, SP_LOOPS)
            for name in ("stored", "x2_stored", "n2_stored", "q_stored"):
                sp.wait_ge(sem(name), 16 * NC)

        @block.gpsimd
        def _(pool):
            pool.memset(neghalf[:, :], -0.5).then_inc(sem("pool_ready"), 1)
            pool.wait_ge(sem("pool_ready"), 1)

            def inverse_std(l):
                def f(c, past):
                    pool.wait_ge(sem("ve_" + l), c + 1)
                    pool.tensor_tensor(rstd[l][:, :], ve[l][:, :], neghalf[:, :], ALU.pow).then_inc(sem("rstd_" + l), 1)
                return f

            def val(c, past):
                inverse_std("f")(c, past)
                inverse_std("x2")(c, past)
                pool.wait_ge(sem("ve_n2"), c + 1)
                pool.tensor_tensor(rstd_n2[:, :], ve_n2[:, :], neghalf[:, :], ALU.pow).then_inc(sem("rstd_n2"), 1)

            def msg(c, past):
                inverse_std("x3")(c, past)
                pool.wait_ge(sem("o_done"), c)
                pool.tensor_tensor(x3_b2[:, :, :], x3[:, :, :], W["b2"].unsqueeze(1).broadcast_to([P, K4, C]), ALU.add).then_inc(sem("x3_b2_done"), 1)

            def proj1(c, past):
                inverse_std("o")(c, past)
                inverse_std("x4")(c, past)

            run(pool, {"in0": inverse_std("attn"), "in1": inverse_std("x1"), "val": val, "msg": msg, "proj1": proj1, "end": inverse_std("ffn")})

        @block.tensor
        def _(pe):
            def turn(src, done):
                for k in range(K4):
                    for h in range(KC):
                        last = nc.tensor.transpose(ps[:, h, k * P:(k + 1) * P], src[:, k, h * P:(h + 1) * P], ident[:, :])
                last.then_inc(sem(done), 1)

            def chan_out(dst, w, i, x, kk=KC):
                for k in range(kk):
                    last = nc.tensor.matmul(dst, w[:, k, i * P:(i + 1) * P], x[:, k, :], start=(k == 0), stop=(k == kk - 1))
                return last

            def tok_out(dst, x, blk, w, kk=KC):
                for k in range(kk):
                    last = nc.tensor.matmul(dst, x[:, k, blk * P:(blk + 1) * P], w[:, k, :], start=(k == 0), stop=(k == kk - 1))
                return last

            def mix(c, past):
                pe.wait_ge(sem("n1_done"), c + 1)
                pe.wait_ge(sem("q_done"), c)
                pe.wait_ge(sem("n4T_done"), past("nT"))
                turn(n1, "mix_mm")

            def rk(c, past):
                pe.wait_ge(sem("mixed"), c + 1)
                pe.wait_ge(sem("kv_done"), c)
                pe.wait_ge(sem("msg_read"), past("msg"))
                pe.wait_ge(sem("gated_done"), past("up5") * M2)
                for i in range(KC):
                    last = chan_out(ps[:, 2 + i, :], W["wk"], i, xk)
                last.then_inc(sem("k_mm"), 1)
                pe.wait_ge(sem("v_read"), c)
                pe.wait_ge(sem("ffn_read"), past("end"))
                for k in range(K4):
                    last = tok_out(blocks(4)[:, k, :], xr, k, W["wr"])
                last.then_inc(sem("r_mm"), 1)

            def val(c, past):
                pe.wait_ge(sem("k_act_done"), c + 1)
                for k in range(K4):
                    last = tok_out(blocks(2)[:, k, :], k_act, k, W["wv"])
                last.then_inc(sem("val_mm"), 1)

            def turn_u(c, past):
                pe.wait_ge(sem("u_done"), c + 1)
                pe.wait_ge(sem("yT_done"), past("yT"))
                turn(t1, "uT_mm")

            def qkv(c, past):
                pe.wait_ge(sem("uT_done"), c + 1)
                for i, name in enumerate(("k2_mm", "v2_mm")):
                    for k in range(K4):
                        last = tok_out(blocks(2 + 2 * i)[:, k, :], uT, k, W["akv"][:, :, i * C:(i + 1) * C])
                    last.then_inc(sem(name), 1)
                for i in range(KC):
                    last = chan_out(ps[:, i, :], W["aq"], i, uT)
                last.then_inc(sem("q_mm"), 1)

            def kv(c, past):
                pe.wait_ge(sem("k_feat_done"), c + 1)
                pe.wait_ge(sem("v_read"), c + 1)
                for g in range(KC):
                    for k in range(K4):
                        last = nc.tensor.matmul(ps[:, 2, g * KVW:(g + 1) * KVW], k_feat[:, k, g * P:(g + 1) * P], v_ones[:, k, g, :],
                                                start=(k == 0), stop=(k == K4 - 1))
                last.then_inc(sem("kv_mm"), 1)

            def msg(c, past):
                pe.wait_ge(sem("q_loaded"), c * 16 + 16)
                pe.wait_ge(sem("kv_diag_done"), c + 1)
                pe.wait_ge(sem("kv_done"), past("kv"))
                pe.wait_ge(sem("k_feat_done"), past("qkv"))
                pe.wait_ge(sem("gated_done"), past("up5") * M2)
                pe.wait_ge(sem("o_done"), c)
                for k in range(K4):
                    for g in range(KC):
                        last = nc.tensor.matmul(ps[:, MSG_BANKS[k], g * MSGW:(g + 1) * MSGW], q_in[:, g, k * P:(k + 1) * P], kv_diag[:, g, :], start=True, stop=True)
                    last.then_inc(sem("msg_mm"), 1)

            def turn_y(c, past):
                pe.wait_ge(sem("y_in_done"), c + 1)
                pe.wait_ge(sem("n1T_done"), past("mix"))
                pe.wait_ge(sem("n4T_done"), c)
                turn(t2, "yT_mm")

            def fc(half):
                def f(c, past):
                    if half == 0:
                        pe.wait_ge(sem("yT_done"), c + 1)
                        pe.wait_ge(sem("msg_read"), c + 1)
                    for i in range(half * M1 // 2, (half + 1) * M1 // 2):
                        if i >= 2:
                            pe.wait_ge(sem("gelu_done"), c * M1 + i - 1)
                        chan_out(ps[:, 6 + i % 2, :], W["w1"], i, yT).then_inc(sem("fc_mm"), 1)
                return f

            def proj(half):
                def f(c, past):
                    pe.wait_ge(sem("gelu_done"), c * M1 + M1)
                    for k in (2 * half, 2 * half + 1):
                        last = tok_out(blocks(6)[:, k, :], hT, k, W["w2"], M1)
                    last.then_inc(sem("proj_mm"), 1)
                return f

            def turn_n4(c, past):
                pe.wait_ge(sem("n4_done"), c + 1)
                pe.wait_ge(sem("q_done"), past("qkv"))
                turn(t2, "nT_mm")

            def up(m):
                def f(c, past):
                    if m == 0:
                        pe.wait_ge(sem("n4T_done"), c + 1)
                        pe.wait_ge(sem("ffn_read"), c)
                        pe.wait_ge(sem("v_read"), past("qkv"))
                    elif m == 1:
                        pe.wait_ge(sem("msg_read"), past("msg"))
                    else:
                        pe.wait_ge(sem("gated_done"), c * M2 + m - 1)
                    a = up_bank(m)
                    chan_out(ps[:, a, :], W["wg"], m, n4T).then_inc(sem("gate_mm"), 1)
                    chan_out(ps[:, a + 1, :], W["wu"], m, n4T).then_inc(sem("up_mm"), 1)
                return f

            def down(c, past):
                pe.wait_ge(sem("gated_done"), c * M2 + M2)
                pe.wait_ge(sem("v_read"), past("qkv"))
                for k in range(K4):
                    last = tok_out(blocks(4)[:, k, :], gated, k, W["wd"], M2)
                last.then_inc(sem("down_mm"), 1)

            run(pe, {"mix": mix, "rk": rk, "val": val, "uT": turn_u, "qkv": qkv, "kv": kv, "msg": msg, "yT": turn_y, "fc0": fc(0), "fc1": fc(1),
                     "proj0": proj(0), "proj1": proj(1), "nT": turn_n4, "down": down, **{f"up{m}": up(m) for m in range(M2)}})

        @block.scalar
        def _(act):
            A = nc.scalar.activation

            def mix(c, past):
                act.wait_ge(sem("mix_mm"), c + 1)
                act.wait_ge(sem("carried"), c + 1)
                A(n1T[:, :, 1:N + 1], banks(0, 2), ACT.Copy).then_inc(sem("n1T_done"), 1)

            def rk(c, past):
                act.wait_ge(sem("k_mm"), c + 1)
                act.wait_ge(sem("k_act_done"), c)
                A(k_relu[:, :, :], banks(2, 2), ACT.Relu).then_inc(sem("k_read"), 1)
                act.wait_ge(sem("r_mm"), c + 1)
                act.wait_ge(sem("k_feat_done"), c)
                A(flat(r_gate), wide(4, 2), ACT.Sigmoid).then_inc(sem("r_read"), 1)

            def turn_u(c, past):
                act.wait_ge(sem("uT_mm"), c + 1)
                act.wait_ge(sem("q_mm"), c)
                A(uT[:, :, :], banks(0, 2), ACT.Copy).then_inc(sem("uT_done"), 1)

            def qkv(c, past):
                act.wait_ge(sem("v2_mm"), c + 1)
                act.wait_ge(sem("kv_mm"), c)
                A(v_ones[:, :, :, 0:P], blocks(4).rearrange("p k (g n) -> p k g n", g=KC), ACT.Copy).then_inc(sem("v_read"), 1)
                act.wait_ge(sem("k_low"), c + 1)
                A(k_exp[:, :, :], k_exp[:, :, :], ACT.Exp).then_inc(sem("k_exp_done"), 1)
                act.wait_ge(sem("q_low"), c + 1)
                A(q_exp[:, :, :], q_exp[:, :, :], ACT.Exp).then_inc(sem("q_exp_done"), 1)

            def turn_y(c, past):
                act.wait_ge(sem("yT_mm"), c + 1)
                act.wait_ge(sem("fc_mm"), c * M1)
                A(yT[:, :, :], banks(0, 2), ACT.Copy).then_inc(sem("yT_done"), 1)

            def fc(half):
                def f(c, past):
                    if half == 0:
                        act.wait_ge(sem("proj_mm"), c * 2)
                    for i in range(half * M1 // 2, (half + 1) * M1 // 2):
                        act.wait_ge(sem("fc_mm"), c * M1 + i + 1)
                        A(hT[:, i, :], ps[:, 6 + i % 2, :], ACT.Gelu, bias=W["b1"][:, 0, i:i + 1]).then_inc(sem("gelu_done"), 1)
                return f

            def turn_n4(c, past):
                act.wait_ge(sem("nT_mm"), c + 1)
                act.wait_ge(sem("up_mm"), c * M2)
                A(n4T[:, :, :], banks(0, 2), ACT.Copy).then_inc(sem("n4T_done"), 1)

            def up(m):
                def f(c, past):
                    if m == 0:
                        act.wait_ge(sem("x4_done"), c + 1)
                        act.wait_ge(sem("y_done"), c)
                        A(x4_kept[:, :, :], x4[:, :, :], ACT.Copy).then_inc(sem("x4_kept"), 1)
                    act.wait_ge(sem("gate_mm"), c * M2 + m + 1)
                    act.wait_ge(sem("gated_done"), c * M2 + max(m - 1, 0))
                    A(gate[:, m % 2, :], ps[:, up_bank(m), :], ACT.Silu).then_inc(sem("silu_done"), 1)
                return f

            run(act, {"mix": mix, "rk": rk, "uT": turn_u, "qkv": qkv, "yT": turn_y, "fc0": fc(0), "fc1": fc(1), "nT": turn_n4,
                      **{f"up{m}": up(m) for m in range(M2)}})

        @block.vector
        def _(dve):
            V = nc.vector
            setup = Chain(dve, sem("setup"))
            setup.done(V.memset(n1T[:, :, :], 0.0))
            setup.done(V.memset(kv_sums[:, :, :], 0.0))
            setup.done(V.memset(kv_diag[:, :, :], 0.0))
            setup.done(V.memset(keep[:, :], 1.0))
            setup.done(V.memset(v_ones[:, :, :, P:P + 1], 1.0))
            setup.done(V.memset(v_ones[:, :, :, P + 1:P + 2], 0.0))
            for i, mu in enumerate(("mu_r", "mu_k")):
                setup.done(V.tensor_scalar(one_minus_mu[:, i, :], W[mu][:, 0, :], -1.0, 1.0, ALU.mult, ALU.add))
            setup.wait()
            setup.link(V.memset(keep[:, 0:NC:CB], 0.0))
            V.memset(keep[:, NC:NC + 1], 0.0).then_inc(sem("carried"), 1)

            def norm_stats(l, src, c):
                ch = Chain(dve, sem("stats_" + l), c * 2)
                for k in range(K4):
                    ins = V.bn_stats(stats[l][:, k, :], src(k))
                ch.link(ins)
                dve.sem_inc(sem("waited"), 1)
                for k in range(K4):
                    ins = V.bn_aggr(mv[l][:, k, :], stats[l][:, k, :])
                ch.link(ins)
                V.tensor_scalar(ve[l][:, :], mv[l][:, :, 1], EPS, None, ALU.add).then_inc(sem("ve_" + l), 1)

            def norm_apply(l, dst, src, c):
                dve.wait_ge(sem("rstd_" + l), c + 1)
                for k in range(K4):
                    ins = V.tensor_scalar(dst(k), src(k), mv[l][:, k, 0:1], rstd[l][:, k:k + 1], ALU.subtract, ALU.mult)
                return ins

            blk = lambda t: (lambda k: t[:, k, :])
            attn_blk = lambda k: attn[:, :, k, :]

            def in0(c, past):
                dve.wait_ge(sem("attn_loaded"), c * 16 + 16)
                norm_stats("attn", attn_blk, c)

            def in1(c, past):
                dve.wait_ge(sem("uT_mm"), c)
                norm_apply("attn", lambda k: t1[:, k, :].rearrange("p (h d) -> p h d", h=H), attn_blk, c).then_inc(sem("attn_used"), 1)
                dve.wait_ge(sem("attn_used"), c + 1)
                dve.wait_ge(sem("x0_loaded"), c * 16 + 16)
                V.tensor_tensor(x1[:, :, :], x0[:, :, :], t1[:, :, :], ALU.add).then_inc(sem("x1_done"), 1)
                dve.wait_ge(sem("x1_done"), c + 1)
                norm_stats("x1", blk(x1), c)

            def in2(c, past):
                dve.wait_ge(sem("n2_stored"), c * 16)
                norm_apply("x1", blk(n1), blk(x1), c).then_inc(sem("n1_done"), 1)

            def mix(c, past):
                ch = Chain(dve, sem("mix_step"), c * 2 * KC)
                dve.wait_ge(sem("n1T_done"), c + 1)
                dve.wait_ge(sem("r_mm"), c)
                dve.wait_ge(sem("q_done"), c)
                pairs = ((xk, "mu_k", 1), (xr, "mu_r", 0))
                for dst, mu, i in pairs:
                    for h in range(KC):
                        ch.done(V.tensor_scalar(dst[:, h, :], n1T[:, h, 0:N], one_minus_mu[:, i, h:h + 1], None, ALU.mult))
                ch.wait()
                for dst, mu, i in pairs:
                    for h in range(KC):
                        ins = V.scalar_tensor_tensor(dst[:, h, :], n1T[:, h, 1:N + 1], W[mu][:, 0, h:h + 1], dst[:, h, :], ALU.mult, ALU.add)
                ins.then_inc(sem("mixed"), 1)
                dve.wait_ge(sem("mixed"), c + 1)
                V.tensor_scalar(n1T[:, :, 0:1], n1T[:, :, N:N + 1], keep[:, bass.ds(c + 1, 1)], None, ALU.mult).then_inc(sem("carried"), 1)

            def rk(c, past):
                dve.wait_ge(sem("k_read"), c + 1)
                dve.wait_ge(sem("val_mm"), c)
                V.tensor_tensor(k_act[:, :, :], k_relu[:, :, :], k_relu[:, :, :], ALU.mult).then_inc(sem("k_act_done"), 1)

            def val(c, past):
                ch = Chain(dve, sem("val_step"), c * 4)
                dve.wait_ge(sem("val_mm"), c + 1)
                dve.wait_ge(sem("r_read"), c + 1)
                V.tensor_tensor(flat(f), wide(2, 2), flat(r_gate), ALU.mult).then_inc(sem("f_done"), 1)
                dve.wait_ge(sem("f_done"), c + 1)
                norm_stats("f", blk(f), c)
                ch.link(norm_apply("f", blk(t1), blk(f), c))
                dve.wait_ge(sem("x2_stored"), c * 16)
                V.tensor_tensor(x2[:, :, :], x1[:, :, :], t1[:, :, :], ALU.add).then_inc(sem("x2_done"), 1)
                dve.wait_ge(sem("x2_done"), c + 1)
                norm_stats("x2", blk(x2), c)
                norm_apply("x2", blk(n1), blk(x2), c).then_inc(sem("n2_done"), 1)
                ch.link(V.tensor_tensor(ve_n2[:, :], rstd["x2"][:, :], rstd["x2"][:, :], ALU.mult))
                ch.link(V.tensor_tensor(ve_n2[:, :], ve_n2[:, :], mv["x2"][:, :, 1], ALU.mult))
                V.tensor_scalar(ve_n2[:, :], ve_n2[:, :], EPS, None, ALU.add).then_inc(sem("ve_n2"), 1)
                dve.wait_ge(sem("n2_done"), c + 1)
                dve.wait_ge(sem("rstd_n2"), c + 1)
                for k in range(K4):
                    ins = V.scalar_tensor_tensor(t1[:, k, :], n1[:, k, :], rstd_n2[:, k:k + 1], W["g1"], ALU.mult, ALU.mult)
                ch.link(ins)
                V.tensor_tensor(t1[:, :, :], t1[:, :, :], W["be1"].unsqueeze(1).broadcast_to([P, K4, C]), ALU.add).then_inc(sem("u_done"), 1)

            def qkv(c, past):
                dve.wait_ge(sem("k2_mm"), c + 1)
                V.tensor_scalar(flat(k_exp), wide(2, 2), 0.0, None, ALU.min).then_inc(sem("k_low"), 1)
                dve.wait_ge(sem("q_mm"), c + 1)
                V.tensor_scalar(flat(q_exp), wide(0, 2), 0.0, None, ALU.min).then_inc(sem("q_low"), 1)
                dve.wait_ge(sem("k_exp_done"), c + 1)
                V.scalar_tensor_tensor(flat(k_feat), wide(2, 2), 0.0, flat(k_exp), ALU.max, ALU.add).then_inc(sem("k_feat_done"), 1)
                dve.wait_ge(sem("q_exp_done"), c + 1)
                dve.wait_ge(sem("q_stored"), c * 16)
                V.scalar_tensor_tensor(flat(q), wide(0, 2), 0.0, flat(q_exp), ALU.max, ALU.add).then_inc(sem("q_done"), 1)

            def kv(c, past):
                dve.wait_ge(sem("kv_mm"), c + 1)
                slot = kv_sums[:, bass.ds(c // CB, 1), :].rearrange("p a n -> p (a n)")
                V.scalar_tensor_tensor(slot, slot, keep[:, bass.ds(c, 1)], ps[:, 2, 0:KC * KVW], ALU.mult, ALU.add).then_inc(sem("kv_done"), 1)
                dve.wait_ge(sem("kv_done"), c + 1)

            def msg(c, past):
                ch = Chain(dve, sem("msg_step"), c * K4)
                dve.wait_ge(sem("msg_mm"), c * K4)
                for h in range(HG):
                    rows = slice(h * DG, (h + 1) * DG)
                    src = kv_sums[rows, bass.ds(c // CB, 1), :].rearrange("p a (g n) -> p (a g) n", g=KC)
                    V.tensor_copy(kv_diag[rows, :, h * DG:(h + 1) * DG], src[:, :, h * DG:(h + 1) * DG])
                    ins = V.tensor_copy(kv_diag[rows, :, HG * DG + h:HG * DG + h + 1], src[:, :, P:P + 1])
                ins.then_inc(sem("kv_diag_done"), 1)
                dve.wait_ge(sem("msg_mm"), c * K4 + K4)
                for k in range(0, K4, 2):
                    both = ps[:, MSG_BANKS[k]:MSG_BANKS[k] + 2, 0:KC * MSGW].rearrange("p k (g n) -> p k g n", g=KC)
                    ch.link(V.tensor_scalar(denom[:, k:k + 2, :, :], both[:, :, :, HG * DG:MSGW], EPS_ATTN, None, ALU.add))
                    ch.link(V.reciprocal(denom[:, k:k + 2, :, :], denom[:, k:k + 2, :, :]))
                    for i in range(2):
                        ins = V.tensor_tensor(t2[:, k + i, :].rearrange("p (g h d) -> p g h d", g=KC, h=HG),
                                              both[:, i, :, 0:HG * DG].rearrange("p g (h d) -> p g h d", h=HG),
                                              denom[:, k + i, :, :].unsqueeze(3).broadcast_to([P, KC, HG, DG]), ALU.mult)
                ins.then_inc(sem("msg_read"), 1)
                dve.wait_ge(sem("msg_read"), c + 1)
                dve.wait_ge(sem("n2_loaded"), c * 16 + 16)
                dve.wait_ge(sem("x3_b2_done"), c)
                V.tensor_tensor(x3[:, :, :], n2_in[:, :, :], t2[:, :, :], ALU.add).then_inc(sem("x3_done"), 1)
                dve.wait_ge(sem("x3_done"), c + 1)
                norm_stats("x3", blk(x3), c)

            def y_in(c, past):
                ch = Chain(dve, sem("y_step"), c)
                dve.wait_ge(sem("rstd_x3"), c + 1)
                for k in range(K4):
                    ins = V.scalar_tensor_tensor(t2[:, k, :], x3[:, k, :], mv["x3"][:, k, 0:1], W["g2"], ALU.subtract, ALU.mult)
                ch.link(ins)
                for k in range(K4):
                    ins = V.scalar_tensor_tensor(t2[:, k, :], t2[:, k, :], rstd["x3"][:, k:k + 1], W["be2"], ALU.mult, ALU.add)
                ins.then_inc(sem("y_in_done"), 1)

            def proj1(c, past):
                ch = Chain(dve, sem("proj_step"), c)
                dve.wait_ge(sem("proj_mm"), c * 2 + 2)
                dve.wait_ge(sem("x3_b2_done"), c + 1)
                V.tensor_tensor(flat(o), wide(6, 2), flat(x3_b2), ALU.add).then_inc(sem("o_done"), 1)
                dve.wait_ge(sem("o_done"), c + 1)
                norm_stats("o", blk(o), c)
                dve.wait_ge(sem("yT_mm"), c + 1)
                ch.link(norm_apply("o", blk(t2), blk(o), c))
                dve.wait_ge(sem("x2_loaded"), c * 16 + 16)
                dve.wait_ge(sem("x4_kept"), c)
                V.tensor_tensor(x4[:, :, :], x2_in[:, :, :], t2[:, :, :], ALU.add).then_inc(sem("x4_done"), 1)
                dve.wait_ge(sem("x4_done"), c + 1)
                norm_stats("x4", blk(x4), c)
                norm_apply("x4", blk(t2), blk(x4), c).then_inc(sem("n4_done"), 1)

            def up(m):
                def f(c, past):
                    dve.wait_ge(sem("silu_done"), c * M2 + m + 1)
                    dve.wait_ge(sem("up_mm"), c * M2 + m + 1)
                    if m == 0:
                        dve.wait_ge(sem("down_mm"), c)
                    V.tensor_tensor(gated[:, m, :], ps[:, up_bank(m) + 1, :], gate[:, m % 2, :], ALU.mult).then_inc(sem("gated_done"), 1)
                return f

            def end(c, past):
                dve.wait_ge(sem("down_mm"), c + 1)
                ffn_blk = lambda k: blocks(4)[:, k, :]
                norm_stats("ffn", ffn_blk, c)
                dve.wait_ge(sem("stored"), c * 16)
                norm_apply("ffn", blk(y_out), ffn_blk, c).then_inc(sem("ffn_read"), 1)
                dve.wait_ge(sem("ffn_read"), c + 1)
                dve.wait_ge(sem("x4_kept"), c + 1)
                V.tensor_tensor(y_out[:, :, :], y_out[:, :, :], x4_kept[:, :, :], ALU.add).then_inc(sem("y_done"), 1)

            run(dve, {"in0": in0, "in1": in1, "in2": in2, "mix": mix, "rk": rk, "val": val, "qkv": qkv, "kv": kv, "msg": msg, "y": y_in, "proj1": proj1,
                      "end": end, **{f"up{m}": up(m) for m in range(M2)}})


def transformer(nc, x, rot, ent, floats, ints, rows, out):
    with ExitStack() as ctx:
        sb = lambda n, s: ctx.enter_context(nc.sbuf_tensor(n, s, F32))
        weight_mem = sb("weight_mem", [P, FLOAT_COLS + INT_COLS])
        row_mem = sb("row_mem", [P, len(ROWS), C])
        ident = sb("ident", [P, P])
        heads_dram = nc.dram_tensor("heads_dram", [NHD, P, BB * D], F32, kind="Internal").ap()
        W, at = {}, 0
        for name, k, n in FLOAT_WEIGHTS + INT_WEIGHTS:
            W[name] = weight_mem[:, at:at + k * n].rearrange("p (k n) -> p k n", k=k)
            at += k * n
        for i, name in enumerate(ROWS):
            W[name] = row_mem[:, i, :]
        softmax_attention(nc, x, rot, ent, floats, ints, rows, weight_mem, row_mem, ident, heads_dram)
        later_layers(nc, heads_dram, x, W, ident, out)


def kernel(**inputs):
    import numpy as np
    import concourse.bacc as bacc
    from concourse.bass_utils import run_bass_kernel_spmd

    def on_partitions(w):
        k = w.shape[0] // P
        return w.reshape(k, P, -1).transpose(1, 0, 2).reshape(P, -1)

    a = {name: np.asarray(v) for name, v in inputs.items()}
    vec = lambda name: a[name].reshape(-1, P).T
    mat = lambda *names: on_partitions(np.concatenate([a[n].T for n in names], axis=1))
    arrays = {
        "in_x_dram": a["L0_attn_inputs"],
        "in_rot_dram": a["L0_attn_rotation_params"],
        "in_ent_dram": a["L0_attn_entangle_params"],
        "in_floats_dram": np.concatenate([mat("L0_ffn_W_r"), mat("L0_ffn_W_k"), mat("L0_ffn_W_v"), mat("L1_attn_wq"), mat("L1_attn_wk", "L1_attn_wv"),
                                          mat("L1_attn_w1"), mat("L1_attn_w2"), vec("L0_ffn_mu_r"), vec("L0_ffn_mu_k"), vec("L1_attn_b1")], axis=1),
        "in_ints_dram": np.concatenate([mat("L1_ffn_w_gate"), mat("L1_ffn_w_up"), mat("L1_ffn_w_down")], axis=1),
        "in_rows_dram": np.concatenate([a["L1_attn_" + n] for n in ROWS]),
    }
    arrays = {n: np.ascontiguousarray(v) for n, v in arrays.items()}
    nc = bacc.Bacc("TRN2", target_bir_lowering=False, num_devices=1)
    args = [nc.dram_tensor(n, v.shape, mybir.dt.from_np(v.dtype), kind="ExternalInput").ap() for n, v in arrays.items()]
    out = nc.dram_tensor("out_0_dram", (B, T, C), F32, kind="ExternalOutput").ap()
    transformer(nc, *args, out)
    r = run_bass_kernel_spmd(nc, [arrays], core_ids=[0])
    return r.results[0]["out_0_dram"]
```

```python
import concourse.bass as bass
from concourse import mybir
from concourse.alu_op_type import AluOpType as ALU
from contextlib import ExitStack

F32, BF16, FP16, I32 = mybir.dt.float32, mybir.dt.bfloat16, mybir.dt.float16, mybir.dt.int32
ACT = mybir.ActivationFunctionType
AX = mybir.AxisListType

P = 128
B, T, C = 4, 2048, 256
EPS = 1e-5

H, D = 16, 16
NHD = B * H
BB = T // P
NB = B * BB
BANK = 512
QC = T // BANK
GH = P // D
GROUPS = NHD // GH
HALVES = 2 * BB
SLOTS = 3
AHEAD = 3
ROUNDS = QC
ROUND_AT, GENERAL_AT = 4, 8
PARTS = 3
PRODUCTS = 6
BIAS = PRODUCTS * D
ROWS_QK = BIAS + PARTS
SAFE = 75.0
PROBS = 4

N = 512
NC = B * T // N
CB = T // N
K4 = N // P
KC = C // P
F1, F2 = 1024, 768
M1, M2 = F1 // P, F2 // P
HG, DG = 4, 32
KVW = HG * DG + 2
MSGW = HG * DG + HG
EPS_ATTN = 1e-6
DEQUANT = 1.0 / 127.0
NARROW = 127.0
NORM_SCALE, HIDDEN_SCALE = 2048.0, 0.5

FLOAT_WEIGHTS = (("wr", KC, C), ("wk", KC, C), ("wv", KC, C), ("aq", KC, C), ("akv", KC, 2 * C), ("w1", KC, F1), ("w2", M1, C),
                 ("mu_r", 1, KC), ("mu_k", 1, KC), ("b1", 1, M1))
INT_WEIGHTS = (("wg", KC, F2), ("wu", KC, F2), ("wd", M2, C))
ROWS = ("b2", "g1", "be1", "g2", "be2")
FLOAT_COLS = sum(k * n for _, k, n in FLOAT_WEIGHTS)
INT_COLS = sum(k * n for _, k, n in INT_WEIGHTS)


class Chain:

    def __init__(self, eng, sem, base=0):
        self.eng, self.sem, self.base, self.n = eng, sem, base, 0

    def done(self, ins):
        ins.then_inc(self.sem, 1)
        self.n += 1

    def wait(self):
        self.eng.wait_ge(self.sem, self.base + self.n)

    def link(self, ins):
        self.done(ins)
        self.wait()


def slot_of(at):
    at %= GH * HALVES
    return 1 if at == GH * HALVES - 1 else at % SLOTS


def last_use(at):
    return max(g for g in range(at) if slot_of(g) == slot_of(at))


def softmax_attention(nc, x_in, rot, ent, floats, ints, rows, weight_mem, row_mem, narrow, ident, heads_out):
    with ExitStack() as ctx:
        sb = lambda n, s, d=F32: ctx.enter_context(nc.sbuf_tensor(n, s, d))
        sem = lambda n: ctx.enter_context(nc.semaphore(n))

        xs = sb("xs", [P, B * BB, C])
        result = sb("result", [P, 2, BB, D])
        identb = sb("identb", [P, P], BF16)
        neghalf = sb("neghalf", [P, BB])
        rot_row, ent_row = sb("rot_row", [P, C]), sb("ent_row", [P, C])
        rot_col, ent_col = sb("rot_col", [P, KC]), sb("ent_col", [P, KC])
        q_factor, k_factor = sb("q_factor", [P, GROUPS]), sb("k_factor", [P, GROUPS])
        stats, mv, ve, rstd = sb("stats", [P, BB, 6]), sb("mv", [P, BB, 2]), sb("ve", [P, BB]), sb("rstd", [P, BB])
        weighted = sb("weighted", [P, GH, BB, D])
        bound, widest = sb("bound", [P, GH, BB]), sb("widest", [P, 2, GH])
        flags = sb("flags", [P, NHD], I32)
        widest_weight = sb("widest_weight", [P, 2])
        probs = sb("probs", [P, PROBS, T])
        staged = sb("staged", [P, QC, P])
        qk = sb("qk", [P, 2, BANK])
        parts = [sb(f"parts{i}", [P, 2 * PARTS, BANK], BF16) for i in range(2)]
        qT = [sb(f"qT{i}", [P, T], BF16) for i in range(2)]
        kT = [sb(f"kT{i}", [P, T], BF16) for i in range(2)]
        vals = [sb(f"vals{i}", [P, BB, 32]) for i in range(2)]
        sums = sb("sums", [P, BANK])
        recip = sb("recip", [P, QC, QC])
        chunk_max, neg_max = sb("chunk_max", [P, BB, QC]), sb("neg_max", [P, BB, 2])
        max_split = sb("max_split", [P, BB, P], BF16)

        split_dram = nc.dram_tensor("split_dram", [GROUPS, 2 * PARTS, P, T], BF16, kind="Internal").ap()

        ps = ctx.enter_context(nc.psum_tensor("ps", [P, 8, BANK], F32))
        SCORES = [ps[:, 2 * s:2 * s + 2, :].rearrange("p a n -> p (a n)") for s in range(SLOTS)]
        ACC = ps[:, 6, :]
        TURN = ps[:, 7, :]
        TURNB = TURN.bitcast(BF16)

        rot_loaded, weights_loaded, weights_ready, widest_weight_ready = sem("rot_loaded"), sem("weights_loaded"), sem("weights_ready"), sem("widest_weight_ready")
        x_loaded = [sem(f"x_loaded{b}") for b in range(B)]
        pool_init, consts, setup_step = sem("pool_init"), sem("consts"), sem("setup_step")
        var_ready, rstd_ready, normed, norm_step = sem("var_ready"), sem("rstd_ready"), sem("normed"), sem("norm_step")
        round_staged, round_full, round_read, split_step, parts_ready = (sem(n) for n in ("round_staged", "round_full", "round_read", "split_step", "parts_ready"))
        split_stored = [sem(f"split_stored{i}") for i in range(2)]
        bound_step, bound_ready, widest_ready, flags_ready = sem("bound_step"), sem("bound_ready"), sem("widest_ready"), sem("flags_ready")
        qk_loaded = [sem(f"qk_loaded{i}") for i in range(2)]
        bias_clear, vals_ready, operands_ready = sem("bias_clear"), sem("vals_ready"), sem("operands_ready")
        scores_ready, exps_done, probs_free = sem("scores_ready"), sem("exps_done"), sem("probs_free")
        acc_free, sums_ready, result_full, recip_ready, result_read = (sem(n) for n in ("acc_free", "sums_ready", "result_full", "recip_ready", "result_read"))
        max_full, max_free, max_ready, max_step = sem("max_full"), sem("max_free"), sem("max_ready"), sem("max_step")
        heads_stored = [sem(f"heads_stored{i}") for i in range(2)]
        waited = sem("waited")

        MAX_USES = BB * QC + 2
        MAX_STEPS = 5
        SPLIT_STEPS = 4
        LOADS = 6 * 16

        block = ctx.enter_context(nc.Block())

        @block.sync
        def _(sp):
            for dst, src in ((rot_row, rot), (ent_row, ent)):
                sp.dma_start(dst[:, :], src.rearrange("h d -> (h d)").partition_broadcast(P)).then_inc(rot_loaded, 16)
            for dst, src in ((rot_col, rot), (ent_col, ent)):
                for half in range(KC):
                    sp.dma_start(dst[:, half:half + 1], src[half * GH:(half + 1) * GH, :].rearrange("h d -> (h d)").unsqueeze(1)).then_inc(rot_loaded, 16)

            def load_x(b):
                sp.dma_start(xs[:, b * BB:(b + 1) * BB, :], x_in[b].rearrange("(k p) c -> p k c", p=P)).then_inc(x_loaded[b], 16)

            def store_round(group, r):
                sp.wait_ge(parts_ready, group * ROUNDS + r + 1)
                sp.dma_start(split_dram[bass.ds(group, 1), :, :, r * BANK:(r + 1) * BANK].rearrange("g s p t -> p (g s) t"),
                             parts[r % 2][:, :, :]).then_inc(split_stored[r % 2], 16)

            def load_operands(head, group, e):
                buf = e % 2
                if e == 0:
                    for stored in split_stored:
                        sp.wait_ge(stored, (group + 1) * (ROUNDS // 2 * 16))
                        sp.sem_inc(waited, 1)
                if not (isinstance(head, int) and head < 2):
                    sp.wait_ge(scores_ready, (head - 1) * HALVES)
                src = split_dram[bass.ds(group, 1), :, e * D:(e + 1) * D, :].rearrange("g s p t -> (g s) p t")
                at = 0
                for i in range(PARTS):
                    n = PARTS - i
                    q_src = src[i:i + 1].broadcast_to([n, D, T])
                    sp.dma_start(qT[buf][at:at + n * D, :], q_src).then_inc(qk_loaded[buf], 16)
                    sp.dma_start(kT[buf][at:at + n * D, :], src[PARTS:PARTS + n]).then_inc(qk_loaded[buf], 16)
                    at += n * D

            def store_result(head, buf):
                sp.wait_ge(result_read, head + 2)
                sp.dma_start(heads_out[bass.ds(head, 1)].rearrange("a p n -> p (a n)"),
                             result[:, buf, :, :].rearrange("p k d -> p (k d)")).then_inc(heads_stored[buf], 16)

            for b in range(B):
                load_x(b)
            for r in range(ROUNDS):
                store_round(0, r)
            load_operands(0, 0, 0)
            sp.dma_start(weight_mem[:, 0:FLOAT_COLS], floats).then_inc(weights_loaded, 16)
            sp.dma_start(weight_mem[:, FLOAT_COLS:].bitcast(I32), ints).then_inc(weights_loaded, 16)
            sp.dma_start(row_mem[:, :, :].rearrange("p a c -> p (a c)"), rows.partition_broadcast(P)).then_inc(weights_loaded, 16)

            def group_of_heads(group, last):
                for e in range(GH):
                    head = group * GH + e
                    if e + 1 < GH:
                        load_operands(head + 1, group, e + 1)
                    elif not last:
                        load_operands(head + 1, group + 1, 0)
                    if not (isinstance(head, int) and head == 0):
                        store_result(head - 1, (e + 1) % 2)
                    if e < ROUNDS and not last:
                        store_round(group + 1, e)

            group_of_heads(0, False)
            with sp.Fori(1, GROUPS - 1) as group:
                group_of_heads(group, False)
            group_of_heads(GROUPS - 1, True)
            store_result(NHD - 1, (GH - 1) % 2)
            for stored in heads_stored:
                sp.wait_ge(stored, 16 * NHD // 2)

        @block.gpsimd
        def _(pool):
            pool.memset(neghalf[:, :], -0.5).then_inc(pool_init, 1)
            for m in (ident, identb):
                pool.memset(m[:, :], 0.0).then_inc(pool_init, 1)
            pool.wait_ge(pool_init, 3)
            for m in (ident, identb):
                pool.affine_select(out=m[:, :], in_=m[:, :], compare_op=ALU.not_equal, fill=1.0, base=0,
                                   pattern=[[-1, P]], channel_multiplier=1).then_inc(consts, 1)

            def inverse_std(b):
                pool.wait_ge(var_ready, b + 1)
                pool.tensor_tensor(rstd[:, :], ve[:, :], neghalf[:, :], ALU.pow).then_inc(rstd_ready, 1)

            def widest_of(group):
                pool.wait_ge(bound_ready, group + 1)
                pool.partition_all_reduce(widest[:, 1, :], widest[:, 0, :], P, bass.bass_isa.ReduceOp.max).then_inc(widest_ready, 1)

            inverse_std(0)
            widest_of(0)
            widest_of(1)
            for b in range(1, B):
                inverse_std(b)
            for group in range(2, GROUPS):
                widest_of(group)
            pool.wait_ge(weights_ready, 2)
            pool.partition_all_reduce(widest_weight[:, 1:2], widest_weight[:, 0:1], P, bass.bass_isa.ReduceOp.max).then_inc(widest_weight_ready, 1)

        @block.tensor
        def _(pe):
            pe.wait_ge(consts, 2)
            pe.sem_inc(probs_free, PROBS)
            pe.sem_inc(acc_free, 1)
            pe.sem_inc(max_free, 1)
            pe.sem_inc(result_read, 1)

            def turn_round(group, r):
                pe.wait_ge(round_staged, group * ROUNDS + r + 1)
                for k in range(QC):
                    last = nc.tensor.transpose(TURN[:, k * P:(k + 1) * P], staged[:, k, :], ident[:, :])
                last.then_inc(round_full, 1)

            def half_scores(i, slot, buf):
                j, half = i // 2, i % 2
                for n in range(2):
                    q0 = half * T // 2 + n * BANK
                    last = nc.tensor.matmul(SCORES[slot][:, n * BANK:(n + 1) * BANK], kT[buf][0:ROWS_QK, j * P:(j + 1) * P],
                                            qT[buf][0:ROWS_QK, q0:q0 + BANK], start=True, stop=True)
                last.then_inc(scores_ready, 1)

            def general_scores(head, group, e):
                buf = e % 2
                if e == 0:
                    pe.wait_ge(flags_ready, group + 1)
                pe.sem_inc(waited, 1)
                general = pe.value_load(flags[0:1, bass.ds(head, 1)], min_val=0, max_val=1)
                with pe.If(general > 0):
                    pe.wait_ge(qk_loaded[buf], (group * (GH // 2) + e // 2 + 1) * LOADS)
                    pe.wait_ge(bias_clear, head + 1)
                    pe.sem_inc(waited, 1)
                    with pe.Fori(0, BB) as k:
                        for c in range(QC):
                            pe.wait_ge(max_free, head * MAX_USES + k * QC + c + 1)
                            nc.tensor.matmul(TURN, qT[buf][0:ROWS_QK, bass.ds(k * P, P)], kT[buf][0:ROWS_QK, c * BANK:(c + 1) * BANK],
                                             start=True, stop=True).then_inc(max_full, 1)
                    pe.wait_ge(max_ready, head + 1)
                    for r in range(2):
                        pe.wait_ge(max_free, head * MAX_USES + BB * QC + r + 1)
                        for k in range(BB // 2):
                            last = nc.tensor.transpose(TURNB[:, k * P:(k + 1) * P], max_split[:, r * BB // 2 + k, :], identb[:, :])
                        last.then_inc(max_full, 1)
                    pe.wait_ge(max_free, (head + 1) * MAX_USES + 1)
                with pe.Else():
                    pe.sem_inc(max_full, MAX_USES)

            def operands(head, group, e):
                pe.wait_ge(operands_ready, head + 1)
                pe.wait_ge(qk_loaded[e % 2], (group * (GH // 2) + e // 2 + 1) * LOADS)

            for r in range(ROUNDS):
                if r > 0:
                    pe.wait_ge(round_read, r)
                turn_round(0, r)
            pe.wait_ge(round_read, ROUNDS)
            general_scores(0, 0, 0)
            operands(0, 0, 0)
            for i in range(2 * AHEAD):
                if i >= SLOTS:
                    pe.wait_ge(exps_done, i - SLOTS + 1)
                half_scores(i, slot_of(i), 0)

            def group_of_heads(group, last_group):
                first = group * GH * HALVES
                for e in range(GH):
                    head, buf, last = group * GH + e, e % 2, last_group and e == GH - 1
                    nxt, nxt_group, nxt_e = head + 1, group + (e + 1) // GH, (e + 1) % GH
                    for j in range(BB):
                        pe.wait_ge(exps_done, head * HALVES + 2 * j + 2)
                        if j == 0:
                            pe.wait_ge(acc_free, head + 1)
                        for c in range(QC):
                            mm = nc.tensor.matmul(ACC[32 * c:32 * c + 32, :], vals[buf][:, j, :], probs[:, j % PROBS, c * BANK:(c + 1) * BANK],
                                                  start=(j == 0), stop=(j == BB - 1), tile_position=(0, 32 * c))
                        mm.then_inc(probs_free, 1)
                        if j == ROUND_AT and e < ROUNDS and not last_group:
                            pe.wait_ge(result_read, head + 1)
                            turn_round(group + 1, e)
                        if j == GENERAL_AT and not last:
                            rounds = group * ROUNDS + ROUNDS + (0 if last_group else min(e + 1, ROUNDS))
                            pe.wait_ge(round_read, rounds)
                            pe.wait_ge(result_read, head + 1)
                            general_scores(nxt, nxt_group, nxt_e)
                        if j + AHEAD == BB and not last:
                            operands(nxt, nxt_group, nxt_e)
                        for half in range(2):
                            i = 2 * (j + AHEAD) + half
                            if i >= HALVES and last:
                                continue
                            at = e * HALVES + i
                            pe.wait_ge(exps_done, first + last_use(at) + 1)
                            half_scores(i % HALVES, slot_of(at), buf if i < HALVES else 1 - buf)
                    pe.wait_ge(sums_ready, head + 1)
                    if last:
                        pe.wait_ge(result_read, head + 1)
                    for t in range(QC):
                        mm = nc.tensor.transpose(TURN[:, t * P:(t + 1) * P], sums[:, t * P:(t + 1) * P], ident[:, :])
                    mm.then_inc(result_full, 1)

            with pe.Fori(0, GROUPS - 1) as group:
                group_of_heads(group, False)
            group_of_heads(GROUPS - 1, True)

        @block.scalar
        def _(act):
            with act.Fori(0, GROUPS) as group:
                for at in range(GH * HALVES):
                    j, half = at // 2, at % 2
                    if half == 0:
                        act.wait_ge(probs_free, group * GH * BB + j + 1)
                    act.wait_ge(scores_ready, group * GH * HALVES + at + 1)
                    nc.scalar.activation(probs[:, j % PROBS, half * T // 2:(half + 1) * T // 2], SCORES[slot_of(at)], ACT.Exp).then_inc(exps_done, 1)

        @block.vector
        def _(dve):
            V = nc.vector
            setup = Chain(dve, setup_step)
            setup.done(V.memset(max_split[:, :, :], 0.0))
            for t in kT:
                setup.done(V.memset(t[BIAS:BIAS + PARTS, :], 1.0))
            for t in vals:
                setup.done(V.memset(t[:, :, :], 0.0))
            setup.wait()
            for t in vals:
                setup.done(V.memset(t[:, :, D:D + 1], 1.0))
            dve.wait_ge(rot_loaded, 16 * (2 + 2 * KC))
            for half in range(KC):
                setup.done(V.tensor_scalar(q_factor[:, half:GROUPS:KC], rot_col[:, half:half + 1].broadcast_to([P, B]), D ** -0.5, None, ALU.mult))
                setup.done(V.tensor_copy(k_factor[:, half:GROUPS:KC], ent_col[:, half:half + 1].broadcast_to([P, B])))
            setup.done(V.scalar_tensor_tensor(rot_row[:, :], rot_row[:, :], D ** -0.5, ent_row[:, :], ALU.mult, ALU.mult))
            setup.wait()

            def norm(b):
                ch = Chain(dve, norm_step, b * 2)
                x = lambda k: xs[:, b * BB + k, :]
                dve.wait_ge(x_loaded[b], 16)
                for k in range(BB):
                    ins = V.bn_stats(stats[:, k, :], x(k))
                ch.link(ins)
                for k in range(BB):
                    ins = V.bn_aggr(mv[:, k, :], stats[:, k, :])
                ch.link(ins)
                V.tensor_scalar(ve[:, :], mv[:, :, 1], EPS, None, ALU.add).then_inc(var_ready, 1)
                dve.wait_ge(rstd_ready, b + 1)
                for k in range(BB):
                    ins = V.tensor_scalar(x(k), x(k), mv[:, k, 0:1], rstd[:, k:k + 1], ALU.subtract, ALU.mult)
                ins.then_inc(normed, 1)
                dve.wait_ge(normed, b + 1)

            def split_round(group, r):
                ch = Chain(dve, split_step, (group * ROUNDS + r) * SPLIT_STEPS)
                cut = lambda i: parts[r % 2][:, i:2 * PARTS:PARTS, :]
                V.tensor_copy(staged[:, :, :], xs[:, bass.ds(group // KC * BB + r * QC, QC), bass.ds(group % KC * P, P)]).then_inc(round_staged, 1)
                dve.wait_ge(round_full, group * ROUNDS + r + 1)
                if not (isinstance(group, int) and group * ROUNDS + r < 2):
                    dve.wait_ge(split_stored[r % 2], (group * (ROUNDS // 2) + r // 2) * 16)
                V.tensor_scalar(qk[:, 0, :], TURN, q_factor[:, bass.ds(group, 1)], None, ALU.mult)
                V.tensor_scalar(qk[:, 1, :], TURN, k_factor[:, bass.ds(group, 1)], None, ALU.mult).then_inc(round_read, 1)
                dve.wait_ge(round_read, group * ROUNDS + r + 1)
                ch.link(V.tensor_copy(cut(0), qk[:, :, :]))
                ch.link(V.tensor_tensor(qk[:, :, :], qk[:, :, :], cut(0), ALU.subtract))
                ch.link(V.tensor_copy(cut(1), qk[:, :, :]))
                ch.link(V.tensor_tensor(cut(2), qk[:, :, :], cut(1), ALU.subtract))
                dve.sem_inc(parts_ready, 1)

            def bounds(group):
                ch = Chain(dve, bound_step, group * 4)
                x = xs[:, bass.ds(group // KC * BB, BB), bass.ds(group % KC * P, P)].rearrange("p k (h d) -> p h k d", h=GH)
                w = weights_of_group(group)
                ch.link(V.tensor_tensor(weighted[:, :, :, :], x, x, ALU.mult))
                ch.link(V.tensor_tensor(weighted[:, :, :, :], weighted[:, :, :, :], w, ALU.mult))
                ch.link(V.tensor_reduce(bound[:, :, :], weighted[:, :, :, :], AX.X, ALU.add, apply_absolute_value=True))
                V.tensor_reduce(widest[:, 0, :], bound[:, :, :], AX.X, ALU.max).then_inc(bound_ready, 1)
                dve.wait_ge(widest_ready, group + 1)
                ch.link(V.tensor_scalar(flags[:, bass.ds(group * GH, GH)], widest[:, 1, :], SAFE, None, ALU.is_gt))
                dve.sem_inc(flags_ready, 1)

            def weights_of_group(group):
                half = group % KC
                w = rot_row[:, half * GH * D:(half + 1) * GH * D] if isinstance(half, int) else rot_row[:, bass.ds(half * GH * D, GH * D)]
                return w.rearrange("p (h d) -> p h d", h=GH).unsqueeze(2).broadcast_to([P, GH, BB, D])

            def prepare(head, group, e):
                buf = e % 2
                if not (isinstance(head, int) and head < 2):
                    dve.wait_ge(scores_ready, (head - 1) * HALVES)
                V.memset(qT[buf][BIAS:BIAS + PARTS, :], 0.0).then_inc(bias_clear, 1)
                V.tensor_copy(vals[buf][:, :, 0:D], xs[:, bass.ds(group // KC * BB, BB), bass.ds(group % KC * P + e * D, D)]).then_inc(vals_ready, 1)
                general = dve.value_load(flags[0:1, bass.ds(head, 1)], min_val=0, max_val=1)
                with dve.If(general > 0):
                    with dve.Fori(0, BB) as k:
                        for c in range(QC):
                            dve.wait_ge(max_full, head * MAX_USES + k * QC + c + 1)
                            V.tensor_reduce(chunk_max[:, bass.ds(k, 1), c], TURN, AX.X, ALU.max).then_inc(max_free, 1)
                    dve.wait_ge(max_free, head * MAX_USES + BB * QC + 1)
                    ch = Chain(dve, max_step, head * MAX_STEPS)
                    rest, rest2, cut = neg_max[:, :, 0], neg_max[:, :, 1], max_split[:, :, BIAS:BIAS + PARTS]
                    ch.link(V.tensor_reduce(rest, chunk_max[:, :, :], AX.X, ALU.max, negate=True))
                    ch.link(V.tensor_copy(cut[:, :, 0], rest))
                    ch.link(V.tensor_tensor(rest2, rest, cut[:, :, 0], ALU.subtract))
                    ch.link(V.tensor_copy(cut[:, :, 1], rest2))
                    ch.link(V.tensor_tensor(cut[:, :, 2], rest2, cut[:, :, 1], ALU.subtract))
                    dve.sem_inc(max_ready, 1)
                    dve.wait_ge(bias_clear, head + 1)
                    for r in range(2):
                        dve.wait_ge(max_full, head * MAX_USES + BB * QC + r + 1)
                        V.tensor_copy(qT[buf][BIAS:BIAS + PARTS, r * T // 2:(r + 1) * T // 2], TURNB[BIAS:BIAS + PARTS, :]).then_inc(max_free, 1)
                    dve.wait_ge(max_free, (head + 1) * MAX_USES + 1)
                    dve.sem_inc(waited, 1)
                with dve.Else():
                    dve.sem_inc(max_free, MAX_USES)
                    dve.sem_inc(max_ready, 1)
                    dve.sem_inc(max_step, MAX_STEPS)
                dve.wait_ge(bias_clear, head + 1)
                dve.wait_ge(vals_ready, head + 1)
                dve.sem_inc(operands_ready, 1)

            def finish(head, group, e):
                dve.wait_ge(probs_free, head * BB + BB + PROBS)
                V.tensor_copy(sums[:, :], ACC).then_inc(sums_ready, 1)
                dve.wait_ge(sums_ready, head + 1)
                dve.sem_inc(acc_free, 1)
                dve.wait_ge(result_full, head + 1)
                turned = TURN.rearrange("p (t c d) -> p t c d", t=QC, c=QC)
                V.reciprocal(recip[:, :, :], turned[:, :, :, D]).then_inc(recip_ready, 1)
                dve.wait_ge(recip_ready, head + 1)
                dst = result[:, e % 2, :, :].rearrange("p (c t) d -> p t c d", c=QC)
                if not (isinstance(head, int) and head < 2):
                    dve.wait_ge(heads_stored[e % 2], (group * (GH // 2) + e // 2) * 16)
                V.tensor_tensor(dst, turned[:, :, :, 0:D], recip[:, :, :].unsqueeze(3).broadcast_to([P, QC, QC, D]), ALU.mult).then_inc(result_read, 1)

            norm(0)
            for r in range(ROUNDS):
                split_round(0, r)
            bounds(0)
            prepare(0, 0, 0)

            def group_of_heads(group, last_group):
                for e in range(GH):
                    head = group * GH + e
                    if e < ROUNDS and not last_group:
                        split_round(group + 1, e)
                    if isinstance(group, int) and group == 0 and ROUNDS < e < ROUNDS + B:
                        norm(e - ROUNDS)
                    if last_group and e == 1:
                        dve.wait_ge(weights_loaded, 48)
                        here = weight_mem[:, FLOAT_COLS:]
                        V.tensor_copy(here, here.bitcast(I32)).then_inc(weights_ready, 1)
                        dve.wait_ge(weights_ready, 1)
                        V.tensor_reduce(widest_weight[:, 0:1], here, AX.X, ALU.max, apply_absolute_value=True).then_inc(weights_ready, 1)
                    if last_group and e == 2:
                        dve.wait_ge(widest_weight_ready, 1)
                        V.tensor_scalar(narrow[:, :], widest_weight[:, 1:2], NARROW, None, ALU.is_le).then_inc(weights_ready, 1)
                    if not (last_group and e == GH - 1):
                        prepare(head + 1, group + (e + 1) // GH, (e + 1) % GH)
                    if e == ROUNDS and not last_group:
                        bounds(group + 1)
                    finish(head, group, e)

            group_of_heads(0, False)
            with dve.Fori(1, GROUPS - 1) as group:
                group_of_heads(group, False)
            group_of_heads(GROUPS - 1, True)
            dve.wait_ge(weights_ready, 3)


SHIFT = {"0": 0, "1": 1, "2": 2, "l": CB + 1, "m": CB + 2, "a": CB + 3, "b": CB + 4, "c": CB + 5}
STAGES = {"0": "load_in in0 in1 in2", "1": "mix mix_r mix_k val f x2 n2 u", "2": "uT k k_low k_feat v q q_low q_feat kv", "l": "load_msg diag", "m": "msg y yT",
          "a": "load_x2 b2 fc0 fc1 proj0 proj1 proj2 proj3 o",
          "b": "x4 n4 nT n4_low keep up0 up1 up2 up3 up4 up5 high0 high1 high2 high3 high4 high5 low0 low1 low2 low3 low4 low5 down0 down1 down2 down3",
          "c": "ffn out"}
STREAM = {stage: stream for stream, stages in STAGES.items() for stage in stages.split()}
PE_ORDER = "mix fc0 uT fc1 nT mix_r mix_k val up0 up1 up2 up3 msg proj0 up4 up5 proj1 proj2 proj3 v k down0 yT down1 q down2 kv down3".split()
ACT_ORDER = "mix fc0 uT fc1 keep nT mix_r mix_k up0 up1 high0 high1 up2 up3 high2 high3 up4 up5 high4 high5 v k yT q".split()
DVE_ORDER = "x4 b2 mix ffn n4 out n4_low in0 f up0 up1 low0 x2 low1 up2 up3 low2 n2 low3 msg up4 u low4 in1 up5 low5 y o k_low k_feat in2 q_low q_feat kv diag".split()
SP_ORDER = "load_in load_msg load_x2 x2 n2 q_feat out".split()
PLACE = {stage: i for i, stage in enumerate(PE_ORDER)}


def loops():
    cuts = sorted({shift + n for shift in SHIFT.values() for n in (0, 1, NC)})
    return [(a, b, [s for s, shift in SHIFT.items() if shift <= a < shift + NC]) for a, b in zip(cuts, cuts[1:])]


def run(eng, order, stages):
    def once(it, first, streams):
        def counter(here):
            def chunks_past(there):
                shift = SHIFT[STREAM[there]]
                if first < shift:
                    return 0
                if first >= shift + NC:
                    return NC
                return it - shift + chunks_past.before(there)
            chunks_past.before = lambda there: PLACE[there] < PLACE[here]
            return chunks_past

        for stage in order:
            if STREAM[stage] in streams:
                stages[stage](it - SHIFT[STREAM[stage]], counter(stage))

    for first, end, streams in loops():
        if end - first == 1:
            once(first, first, streams)
        else:
            with eng.Fori(first, end) as it:
                once(it, first, streams)


def later_layers(nc, heads_in, x_in, W, W16, int_weights, narrow, ident, out):
    with ExitStack() as ctx:
        sb = lambda n, s, d=F32: ctx.enter_context(nc.sbuf_tensor(n, s, d))
        dram = lambda n: nc.dram_tensor(n, [NC, P, K4 * C], F32, kind="Internal").ap()
        sems = {}

        def sem(n):
            if n not in sems:
                sems[n] = ctx.enter_context(nc.semaphore(n))
            return sems[n]

        x2_dram, n2_dram, q_dram = dram("x2_dram"), dram("n2_dram"), dram("q_dram")

        tok = lambda n: sb(n, [P, K4, C])
        chan = lambda n: sb(n, [P, KC, N])
        flat = lambda t: t[:, :, :].rearrange("p a b -> p (a b)")
        attn = sb("attn", [P, H, K4, D])
        x0, x1, n1, f, x2, r_gate, u = (tok(n) for n in ("x0", "x1", "n1", "f", "x2", "r_gate", "u"))
        n1T = sb("n1T", [P, KC, N + 1])
        xr, xk, k_act, uT, q = (chan(n) for n in ("xr", "xk", "k_act", "uT", "q"))
        k_feat = tok("k_feat")
        v_ones = sb("v_ones", [P, K4, KC, KVW])
        kv_sums = sb("kv_sums", [P, B, KC * KVW])
        kv_diag = sb("kv_diag", [P, KC, MSGW])
        q_in = chan("q_in")
        n2_in, x3, y, o, x2_in, x4, n4, x4_kept, y_out = (tok(n) for n in ("n2_in", "x3", "y", "o", "x2_in", "x4", "n4", "x4_kept", "y_out"))
        yT, n4T = chan("yT"), chan("n4T")
        denom = sb("denom", [P, K4, KC, HG])
        hT = sb("hT", [P, M1, N])
        gate = sb("gate", [P, 2, N])
        gated = sb("gated", [P, M2, N])
        n4T16 = n4T[:, :, :].rearrange("p a n -> p (a n)").bitcast(FP16).rearrange("p (s k n) -> p s k n", s=2, k=KC)
        gated16 = gated[:, :, :].rearrange("p a n -> p (a n)").bitcast(FP16).rearrange("p (s k n) -> p s k n", s=2, k=M2)
        hT16 = hT[:, :, :].rearrange("p a n -> p (a n)").bitcast(FP16)[:, 0:INT_COLS]
        norms = ("attn", "x1", "f", "x2", "x3", "o", "x4", "ffn")
        stats = {l: sb(f"stats_{l}", [P, K4, 6]) for l in norms}
        mv = {l: sb(f"mv_{l}", [P, K4, 2]) for l in norms}
        ve = {l: sb(f"ve_{l}", [P, K4]) for l in norms}
        rstd = {l: sb(f"rstd_{l}", [P, K4]) for l in norms}
        ve_n2, rstd_n2 = sb("ve_n2", [P, K4]), sb("rstd_n2", [P, K4])
        keep = sb("keep", [P, NC + 1])
        neghalf = sb("neghalf_k4", [P, K4])
        one_minus_mu = sb("one_minus_mu", [P, 2, KC])
        ps = ctx.enter_context(nc.psum_tensor("layers_ps", [P, 8, BANK], F32))
        banks = lambda a, n: ps[:, a:a + n, :]
        wide = lambda a, n: ps[:, a:a + n, :].rearrange("p a n -> p (a n)")
        blocks = lambda a: ps[:, a:a + 2, :].rearrange("p a (b n) -> p (a b) n", b=2)
        MSG_BANKS = (2, 3, 4, 5)
        up_bank = lambda m: (4, 2)[m % 2]

        block = ctx.enter_context(nc.Block())

        @block.sync
        def _(sp):
            heads_v = heads_in.rearrange("(b h) p (q n) -> b q p h n", b=B, q=CB)
            x_v = x_in.rearrange("b (q k p) c -> (b q) p k c", q=CB, p=P)
            out_v = out.rearrange("b (q k p) c -> (b q) p k c", q=CB, p=P)
            slab = lambda d, c: d[bass.ds(c, 1)].rearrange("a p n -> p (a n)")

            def load_in(c, past):
                sp.wait_ge(sem("x1_done"), c)
                sp.dma_start(attn[:, :, :, :].rearrange("p h k d -> p h (k d)"),
                             heads_v[bass.ds(c // CB, 1), bass.ds(c % CB, 1)].rearrange("a b p h n -> p (a b h) n")).then_inc(sem("attn_loaded"), 16)
                sp.dma_start(x0[:, :, :], x_v[bass.ds(c, 1)].rearrange("a p k c -> p (a k) c")).then_inc(sem("x0_loaded"), 16)

            def load_msg(c, past):
                sp.wait_ge(sem("msg_mm"), c * K4)
                sp.wait_ge(sem("q_stored"), c * 16 + 16)
                sp.dma_start(flat(q_in), slab(q_dram, c)).then_inc(sem("q_loaded"), 16)
                sp.wait_ge(sem("x3_done"), c)
                sp.wait_ge(sem("n2_stored"), c * 16 + 16)
                sp.dma_start(flat(n2_in), slab(n2_dram, c)).then_inc(sem("n2_loaded"), 16)

            def load_x2(c, past):
                sp.wait_ge(sem("x4_done"), c)
                sp.wait_ge(sem("x2_stored"), c * 16 + 16)
                sp.dma_start(flat(x2_in), slab(x2_dram, c)).then_inc(sem("x2_loaded"), 16)

            def store_x2(c, past):
                sp.wait_ge(sem("x2_done"), c + 1)
                sp.dma_start(slab(x2_dram, c), flat(x2)).then_inc(sem("x2_stored"), 16)

            def store_n2(c, past):
                sp.wait_ge(sem("n2_done"), c + 1)
                sp.dma_start(slab(n2_dram, c), flat(n1)).then_inc(sem("n2_stored"), 16)

            def store_q(c, past):
                sp.wait_ge(sem("q_done"), c + 1)
                sp.dma_start(slab(q_dram, c), flat(q)).then_inc(sem("q_stored"), 16)

            def store_out(c, past):
                sp.wait_ge(sem("y_done"), c + 1)
                sp.dma_start(out_v[bass.ds(c, 1)].rearrange("a p k c -> p (a k) c"), y_out[:, :, :]).then_inc(sem("stored"), 16)

            run(sp, SP_ORDER, {"load_in": load_in, "load_msg": load_msg, "load_x2": load_x2, "x2": store_x2, "n2": store_n2, "q_feat": store_q, "out": store_out})
            for name in ("stored", "x2_stored", "n2_stored", "q_stored"):
                sp.wait_ge(sem(name), 16 * NC)

        @block.gpsimd
        def _(pool):
            pool.memset(neghalf[:, :], -0.5).then_inc(sem("pool_ready"), 1)
            pool.wait_ge(sem("pool_ready"), 1)

            def inverse_std(l):
                def f(c, past):
                    pool.wait_ge(sem("ve_" + l), c + 1)
                    pool.tensor_tensor(rstd[l][:, :], ve[l][:, :], neghalf[:, :], ALU.pow).then_inc(sem("rstd_" + l), 1)
                return f

            def n2(c, past):
                pool.wait_ge(sem("ve_n2"), c + 1)
                pool.tensor_tensor(rstd_n2[:, :], ve_n2[:, :], neghalf[:, :], ALU.pow).then_inc(sem("rstd_n2"), 1)

            def add_b2(c, past):
                pool.wait_ge(sem("x3_done"), c + 1)
                pool.wait_ge(sem("o_normed"), c)
                pool.tensor_tensor(o[:, :, :], x3[:, :, :], W["b2"].unsqueeze(1).broadcast_to([P, K4, C]), ALU.add).then_inc(sem("x3_b2_done"), 1)

            stages = {"in0": inverse_std("attn"), "in1": inverse_std("x1"), "f": inverse_std("f"), "x2": inverse_std("x2"), "n2": n2, "msg": inverse_std("x3"), "b2": add_b2,
                      "o": inverse_std("o"), "x4": inverse_std("x4"), "ffn": inverse_std("ffn")}
            run(pool, [stage for stage in DVE_ORDER if stage in stages], stages)

        @block.tensor
        def _(pe):
            def turn(src, done):
                for k in range(K4):
                    for h in range(KC):
                        last = nc.tensor.transpose(ps[:, h, k * P:(k + 1) * P], src[:, k, h * P:(h + 1) * P], ident[:, :])
                last.then_inc(sem(done), 1)

            def chan_out(dst, w, i, x, kk=KC):
                for k in range(kk):
                    last = nc.tensor.matmul(dst, w[:, k, i * P:(i + 1) * P], x[:, k, :], start=(k == 0), stop=(k == kk - 1))
                return last

            def tok_out(dst, x, blk, w, kk=KC):
                for k in range(kk):
                    last = nc.tensor.matmul(dst, x[:, k, blk * P:(blk + 1) * P], w[:, k, :], start=(k == 0), stop=(k == kk - 1))
                return last

            def freed(name, n):
                if not (isinstance(n, int) and n == 0):
                    pe.wait_ge(sem(name), n)

            def freed_up(past, odd):
                last = max(range(odd, M2, 2), key=lambda m: (past.before(f"up{m}"), m))
                n = past(f"up{last}")
                if not (isinstance(n, int) and n == 0):
                    pe.wait_ge(sem("up_read"), n * M2 - (M2 - 1 - last))

            def free_01(past):
                freed("n1T_done", past("mix"))
                freed("yT_done", past("yT"))
                freed("uT_done", past("uT"))
                freed("q_done", past("q"))
                freed("n4T_done", past("nT"))

            def free_23(past):
                freed("k_read", past("mix_k"))
                freed("f_done", past("val"))
                freed("k_feat_done", past("k"))
                freed("kv_done", past("kv"))
                freed("msg_read", past("msg"))
                freed_up(past, 1)

            def free_45(past):
                freed("r_read", past("mix_r"))
                freed("v_read", past("v"))
                freed("msg_read", past("msg"))
                freed_up(past, 0)
                freed("ffn_read", past("down0"))

            def free_67(past):
                freed("o_done", past("proj3"))

            def mix(c, past):
                pe.wait_ge(sem("n1_done"), c + 1)
                free_01(past)
                turn(n1, "mix_mm")

            def mix_r(c, past):
                pe.wait_ge(sem("mixed"), c + 1)
                free_45(past)
                for k in range(K4):
                    last = tok_out(blocks(4)[:, k, :], xr, k, W["wr"])
                last.then_inc(sem("r_mm"), 1)

            def mix_k(c, past):
                pe.wait_ge(sem("mixed"), c + 1)
                free_23(past)
                for i in range(KC):
                    last = chan_out(ps[:, 2 + i, :], W["wk"], i, xk)
                last.then_inc(sem("k_mm"), 1)

            def val(c, past):
                pe.wait_ge(sem("k_act_done"), c + 1)
                free_23(past)
                for k in range(K4):
                    last = tok_out(blocks(2)[:, k, :], k_act, k, W["wv"])
                last.then_inc(sem("val_mm"), 1)

            def turn_u(c, past):
                pe.wait_ge(sem("u_done"), c + 1)
                free_01(past)
                turn(u, "uT_mm")

            def attn_k(c, past):
                pe.wait_ge(sem("uT_done"), c + 1)
                free_23(past)
                for k in range(K4):
                    last = tok_out(blocks(2)[:, k, :], uT, k, W["akv"][:, :, 0:C])
                last.then_inc(sem("k2_mm"), 1)

            def attn_v(c, past):
                pe.wait_ge(sem("uT_done"), c + 1)
                free_45(past)
                for k in range(K4):
                    last = tok_out(blocks(4)[:, k, :], uT, k, W["akv"][:, :, C:2 * C])
                last.then_inc(sem("v2_mm"), 1)

            def attn_q(c, past):
                pe.wait_ge(sem("uT_done"), c + 1)
                free_01(past)
                for i in range(KC):
                    last = chan_out(ps[:, i, :], W["aq"], i, uT)
                last.then_inc(sem("q_mm"), 1)

            def kv(c, past):
                pe.wait_ge(sem("v_read"), c + 1)
                free_23(past)
                for g in range(KC):
                    for k in range(K4):
                        last = nc.tensor.matmul(ps[:, 2, g * KVW:(g + 1) * KVW], k_feat[:, k, g * P:(g + 1) * P], v_ones[:, k, g, :],
                                                start=(k == 0), stop=(k == K4 - 1))
                last.then_inc(sem("kv_mm"), 1)

            def msg(c, past):
                pe.wait_ge(sem("q_loaded"), c * 16 + 16)
                pe.wait_ge(sem("kv_diag_done"), c + 1)
                free_23(past)
                free_45(past)
                for k in range(K4):
                    for g in range(KC):
                        last = nc.tensor.matmul(ps[:, MSG_BANKS[k], g * MSGW:(g + 1) * MSGW], q_in[:, g, k * P:(k + 1) * P], kv_diag[:, g, :], start=True, stop=True)
                    last.then_inc(sem("msg_mm"), 1)

            def turn_y(c, past):
                pe.wait_ge(sem("y_in_done"), c + 1)
                free_01(past)
                turn(y, "yT_mm")

            def fc(half):
                def f(c, past):
                    if half == 0:
                        pe.wait_ge(sem("yT_done"), c + 1)
                        free_67(past)
                    for i in range(half * M1 // 2, (half + 1) * M1 // 2):
                        if i >= 2:
                            pe.wait_ge(sem("gelu_done"), c * M1 + i - 1)
                        chan_out(ps[:, 6 + i % 2, :], W["w1"], i, yT).then_inc(sem("fc_mm"), 1)
                return f

            def proj(k):
                def f(c, past):
                    pe.wait_ge(sem("gelu_done"), c * M1 + M1)
                    tok_out(blocks(6)[:, k, :], hT, k, W["w2"], M1).then_inc(sem("proj_mm"), 1)
                return f

            def turn_n4(c, past):
                pe.wait_ge(sem("n4_done"), c + 1)
                free_01(past)
                turn(n4, "nT_mm")

            def up(m, exact16):
                def f(c, past):
                    if m == 0:
                        pe.wait_ge(sem("n4T_done"), c + 1)
                    free_23(past) if m % 2 else free_45(past)
                    a = up_bank(m)
                    for i, (w, done) in enumerate((("wg", "gate_mm"), ("wu", "up_mm"))):
                        if exact16:
                            for p in range(2):
                                for k in range(KC):
                                    last = nc.tensor.matmul(ps[:, a + i, :], W16[w][:, k, m * P:(m + 1) * P], n4T16[:, p, k, :],
                                                            start=(p == k == 0), stop=(p == 1 and k == KC - 1))
                        else:
                            last = chan_out(ps[:, a + i, :], W[w], m, n4T)
                        last.then_inc(sem(done), 1)
                return f

            def down(blk, exact16):
                def f(c, past):
                    if blk == 0:
                        pe.wait_ge(sem("gated_done" if exact16 else "up_read"), c * M2 + M2)
                        free_45(past)
                    dst = blocks(4)[:, blk, :]
                    if exact16:
                        for p in range(2):
                            for k in range(M2):
                                last = nc.tensor.matmul(dst, gated16[:, p, k, blk * P:(blk + 1) * P], W16["wd"][:, k, :],
                                                        start=(p == k == 0), stop=(p == 1 and k == M2 - 1))
                    else:
                        last = tok_out(dst, gated, blk, W["wd"], M2)
                    last.then_inc(sem("down_mm"), 1)
                return f

            def program(exact16):
                run(pe, PE_ORDER, {"mix": mix, "mix_r": mix_r, "mix_k": mix_k, "val": val, "uT": turn_u, "k": attn_k, "v": attn_v, "q": attn_q, "kv": kv, "msg": msg,
                                   "yT": turn_y, "fc0": fc(0), "fc1": fc(1), **{f"proj{k}": proj(k) for k in range(K4)}, "nT": turn_n4,
                                   **{f"down{k}": down(k, exact16) for k in range(K4)}, **{f"up{m}": up(m, exact16) for m in range(M2)}})

            is_narrow = pe.value_load(narrow[0:1, 0:1], min_val=0, max_val=1)
            with pe.If(is_narrow > 0):
                pe.wait_ge(sem("w16_ready"), 2)
                program(True)
            with pe.Else():
                program(False)

        @block.scalar
        def _(act):
            A = nc.scalar.activation

            def mix(c, past):
                act.wait_ge(sem("mix_mm"), c + 1)
                act.wait_ge(sem("carried"), c + 1)
                A(n1T[:, :, 1:N + 1], banks(0, 2), ACT.Copy).then_inc(sem("n1T_done"), 1)

            def mix_r(c, past):
                act.wait_ge(sem("r_mm"), c + 1)
                act.wait_ge(sem("f_done"), c)
                A(flat(r_gate), wide(4, 2), ACT.Sigmoid).then_inc(sem("r_read"), 1)

            def mix_k(c, past):
                act.wait_ge(sem("k_mm"), c + 1)
                act.wait_ge(sem("val_mm"), c)
                A(k_act[:, :, :], banks(2, 2), ACT.Relu).then_inc(sem("k_read"), 1)
                act.wait_ge(sem("k_read"), c + 1)
                A(k_act[:, :, :], k_act[:, :, :], ACT.Square).then_inc(sem("k_act_done"), 1)

            def turn_u(c, past):
                act.wait_ge(sem("uT_mm"), c + 1)
                act.wait_ge(sem("q_mm"), c)
                A(uT[:, :, :], banks(0, 2), ACT.Copy).then_inc(sem("uT_done"), 1)

            def attn_v(c, past):
                act.wait_ge(sem("v2_mm"), c + 1)
                act.wait_ge(sem("kv_mm"), c)
                A(v_ones[:, :, :, 0:P], blocks(4).rearrange("p k (g n) -> p k g n", g=KC), ACT.Copy).then_inc(sem("v_read"), 1)

            def k_exp(c, past):
                act.wait_ge(sem("k_low"), c + 1)
                A(k_feat[:, :, :], k_feat[:, :, :], ACT.Exp).then_inc(sem("k_exp_done"), 1)

            def q_exp(c, past):
                act.wait_ge(sem("q_low"), c + 1)
                A(q[:, :, :], q[:, :, :], ACT.Exp).then_inc(sem("q_exp_done"), 1)

            def turn_y(c, past):
                act.wait_ge(sem("yT_mm"), c + 1)
                act.wait_ge(sem("fc_mm"), c * M1)
                A(yT[:, :, :], banks(0, 2), ACT.Copy).then_inc(sem("yT_done"), 1)

            def fc(half):
                def f(c, past):
                    if half == 0:
                        act.wait_ge(sem("proj_mm"), c * K4)
                    for i in range(half * M1 // 2, (half + 1) * M1 // 2):
                        act.wait_ge(sem("fc_mm"), c * M1 + i + 1)
                        A(hT[:, i, :], ps[:, 6 + i % 2, :], ACT.Gelu, bias=W["b1"][:, 0, i:i + 1]).then_inc(sem("gelu_done"), 1)
                return f

            def turn_n4(exact16):
                def f(c, past):
                    act.wait_ge(sem("nT_mm"), c + 1)
                    act.wait_ge(sem("up_mm"), c * M2)
                    if exact16:
                        A(n4T16[:, 0, :, :], banks(0, 2), ACT.Copy, scale=NORM_SCALE).then_inc(sem("n4_high"), 1)
                    else:
                        A(n4T[:, :, :], banks(0, 2), ACT.Copy).then_inc(sem("n4T_done"), 1)
                return f

            def keep_x4(c, past):
                act.wait_ge(sem("x4_done"), c + 1)
                act.wait_ge(sem("y_done"), c)
                A(x4_kept[:, :, :], x4[:, :, :], ACT.Copy).then_inc(sem("x4_kept"), 1)

            def up(m, exact16):
                def f(c, past):
                    act.wait_ge(sem("gate_mm"), c * M2 + m + 1)
                    act.wait_ge(sem("gated_done" if exact16 else "up_read"), c * M2 + max(m - 1, 0))
                    A(gate[:, m % 2, :], ps[:, up_bank(m), :], ACT.Silu, scale=DEQUANT / NORM_SCALE if exact16 else DEQUANT).then_inc(sem("silu_done"), 1)
                return f

            def high(m):
                def f(c, past):
                    act.wait_ge(sem("up_read"), c * M2 + m + 1)
                    if m == 0:
                        act.wait_ge(sem("down_mm"), c * K4)
                    A(gated16[:, 0, m, :], gate[:, m % 2, :], ACT.Copy).then_inc(sem("gated_high"), 1)
                return f

            def program(exact16):
                stages = {"mix": mix, "mix_r": mix_r, "mix_k": mix_k, "uT": turn_u, "v": attn_v, "k": k_exp, "q": q_exp, "keep": keep_x4, "yT": turn_y,
                          "fc0": fc(0), "fc1": fc(1), "nT": turn_n4(exact16), **{f"up{m}": up(m, exact16) for m in range(M2)},
                          **{f"high{m}": high(m) for m in range(M2)}}
                run(act, [stage for stage in ACT_ORDER if exact16 or not stage.startswith("high")], stages)

            is_narrow = act.value_load(narrow[0:1, 0:1], min_val=0, max_val=1)
            with act.If(is_narrow > 0):
                A(hT16, int_weights, ACT.Copy).then_inc(sem("w16_ready"), 1)
                act.wait_ge(sem("w16_ready"), 1)
                A(W16["all"], hT16, ACT.Copy).then_inc(sem("w16_ready"), 1)
                act.wait_ge(sem("w16_ready"), 2)
                program(True)
            with act.Else():
                program(False)

        @block.vector
        def _(dve):
            V = nc.vector
            setup = Chain(dve, sem("setup"))
            setup.done(V.memset(n1T[:, :, :], 0.0))
            setup.done(V.memset(kv_sums[:, :, :], 0.0))
            setup.done(V.memset(kv_diag[:, :, :], 0.0))
            setup.done(V.memset(keep[:, :], 1.0))
            setup.done(V.memset(v_ones[:, :, :, P:P + 1], 1.0))
            setup.done(V.memset(v_ones[:, :, :, P + 1:P + 2], 0.0))
            for i, mu in enumerate(("mu_r", "mu_k")):
                setup.done(V.tensor_scalar(one_minus_mu[:, i, :], W[mu][:, 0, :], -1.0, 1.0, ALU.mult, ALU.add))
            setup.wait()
            setup.link(V.memset(keep[:, 0:NC:CB], 0.0))
            V.memset(keep[:, NC:NC + 1], 0.0).then_inc(sem("carried"), 1)

            def norm_stats(l, src, c, eps=EPS):
                ch = Chain(dve, sem("stats_" + l), c * 2)
                for k in range(K4):
                    ins = V.bn_stats(stats[l][:, k, :], src(k))
                ch.link(ins)
                dve.sem_inc(sem("waited"), 1)
                for k in range(K4):
                    ins = V.bn_aggr(mv[l][:, k, :], stats[l][:, k, :])
                ch.link(ins)
                V.tensor_scalar(ve[l][:, :], mv[l][:, :, 1], eps, None, ALU.add).then_inc(sem("ve_" + l), 1)

            def norm_apply(l, dst, src, c):
                dve.wait_ge(sem("rstd_" + l), c + 1)
                for k in range(K4):
                    ins = V.tensor_scalar(dst(k), src(k), mv[l][:, k, 0:1], rstd[l][:, k:k + 1], ALU.subtract, ALU.mult)
                return ins

            blk = lambda t: (lambda k: t[:, k, :])
            attn_blk = lambda k: attn[:, :, k, :]

            def in0(c, past):
                dve.wait_ge(sem("attn_loaded"), c * 16 + 16)
                norm_stats("attn", attn_blk, c)

            def in1(c, past):
                norm_apply("attn", attn_blk, attn_blk, c).then_inc(sem("attn_normed"), 1)
                dve.wait_ge(sem("attn_normed"), c + 1)
                dve.wait_ge(sem("x0_loaded"), c * 16 + 16)
                V.tensor_tensor(x1[:, :, :].rearrange("p k (h d) -> p k h d", h=H), x0[:, :, :].rearrange("p k (h d) -> p k h d", h=H),
                                attn[:, :, :, :].rearrange("p h k d -> p k h d"), ALU.add).then_inc(sem("x1_done"), 1)
                dve.wait_ge(sem("x1_done"), c + 1)
                norm_stats("x1", blk(x1), c)

            def in2(c, past):
                dve.wait_ge(sem("n2_stored"), c * 16)
                norm_apply("x1", blk(n1), blk(x1), c).then_inc(sem("n1_done"), 1)

            def mix(c, past):
                ch = Chain(dve, sem("mix_step"), c * 2 * KC)
                dve.wait_ge(sem("n1T_done"), c + 1)
                dve.wait_ge(sem("r_mm"), c)
                pairs = ((xk, "mu_k", 1), (xr, "mu_r", 0))
                for dst, mu, i in pairs:
                    for h in range(KC):
                        ch.done(V.tensor_scalar(dst[:, h, :], n1T[:, h, 0:N], one_minus_mu[:, i, h:h + 1], None, ALU.mult))
                ch.wait()
                for dst, mu, i in pairs:
                    for h in range(KC):
                        ins = V.scalar_tensor_tensor(dst[:, h, :], n1T[:, h, 1:N + 1], W[mu][:, 0, h:h + 1], dst[:, h, :], ALU.mult, ALU.add)
                ins.then_inc(sem("mixed"), 1)
                dve.wait_ge(sem("mixed"), c + 1)
                V.tensor_scalar(n1T[:, :, 0:1], n1T[:, :, N:N + 1], keep[:, bass.ds(c + 1, 1)], None, ALU.mult).then_inc(sem("carried"), 1)

            def f_layer(c, past):
                dve.wait_ge(sem("val_mm"), c + 1)
                dve.wait_ge(sem("r_read"), c + 1)
                V.tensor_tensor(flat(f), wide(2, 2), flat(r_gate), ALU.mult).then_inc(sem("f_done"), 1)
                dve.wait_ge(sem("f_done"), c + 1)
                norm_stats("f", blk(f), c)

            def x2_layer(c, past):
                ch = Chain(dve, sem("x2_step"), c)
                dve.wait_ge(sem("x2_stored"), c * 16)
                ch.link(norm_apply("f", blk(x2), blk(f), c))
                V.tensor_tensor(x2[:, :, :], x1[:, :, :], x2[:, :, :], ALU.add).then_inc(sem("x2_done"), 1)
                dve.wait_ge(sem("x2_done"), c + 1)
                norm_stats("x2", blk(x2), c)

            def n2_layer(c, past):
                ch = Chain(dve, sem("n2_step"), c * 2)
                norm_apply("x2", blk(n1), blk(x2), c).then_inc(sem("n2_done"), 1)
                ch.link(V.tensor_tensor(ve_n2[:, :], rstd["x2"][:, :], rstd["x2"][:, :], ALU.mult))
                ch.link(V.tensor_tensor(ve_n2[:, :], ve_n2[:, :], mv["x2"][:, :, 1], ALU.mult))
                V.tensor_scalar(ve_n2[:, :], ve_n2[:, :], EPS, None, ALU.add).then_inc(sem("ve_n2"), 1)

            def u_layer(c, past):
                ch = Chain(dve, sem("u_step"), c)
                dve.wait_ge(sem("n2_done"), c + 1)
                dve.wait_ge(sem("rstd_n2"), c + 1)
                dve.wait_ge(sem("uT_mm"), c)
                for k in range(K4):
                    ins = V.scalar_tensor_tensor(u[:, k, :], n1[:, k, :], rstd_n2[:, k:k + 1], W["g1"], ALU.mult, ALU.mult)
                ch.link(ins)
                V.tensor_tensor(u[:, :, :], u[:, :, :], W["be1"].unsqueeze(1).broadcast_to([P, K4, C]), ALU.add).then_inc(sem("u_done"), 1)

            def k_low(c, past):
                dve.wait_ge(sem("k2_mm"), c + 1)
                dve.wait_ge(sem("kv_mm"), c)
                V.tensor_scalar(flat(k_feat), wide(2, 2), 0.0, None, ALU.min).then_inc(sem("k_low"), 1)

            def k_features(c, past):
                dve.wait_ge(sem("k_exp_done"), c + 1)
                V.scalar_tensor_tensor(flat(k_feat), wide(2, 2), 0.0, flat(k_feat), ALU.max, ALU.add).then_inc(sem("k_feat_done"), 1)

            def q_low(c, past):
                dve.wait_ge(sem("q_mm"), c + 1)
                dve.wait_ge(sem("q_stored"), c * 16)
                V.tensor_scalar(flat(q), wide(0, 2), 0.0, None, ALU.min).then_inc(sem("q_low"), 1)

            def q_features(c, past):
                dve.wait_ge(sem("q_exp_done"), c + 1)
                V.scalar_tensor_tensor(flat(q), wide(0, 2), 0.0, flat(q), ALU.max, ALU.add).then_inc(sem("q_done"), 1)

            def kv(c, past):
                dve.wait_ge(sem("kv_mm"), c + 1)
                slot = kv_sums[:, bass.ds(c // CB, 1), :].rearrange("p a n -> p (a n)")
                V.scalar_tensor_tensor(slot, slot, keep[:, bass.ds(c, 1)], ps[:, 2, 0:KC * KVW], ALU.mult, ALU.add).then_inc(sem("kv_done"), 1)
                dve.wait_ge(sem("kv_done"), c + 1)

            def diag(c, past):
                dve.wait_ge(sem("msg_mm"), c * K4)
                for h in range(HG):
                    rows = slice(h * DG, (h + 1) * DG)
                    src = kv_sums[rows, bass.ds(c // CB, 1), :].rearrange("p a (g n) -> p (a g) n", g=KC)
                    V.tensor_copy(kv_diag[rows, :, h * DG:(h + 1) * DG], src[:, :, h * DG:(h + 1) * DG])
                    ins = V.tensor_copy(kv_diag[rows, :, HG * DG + h:HG * DG + h + 1], src[:, :, P:P + 1])
                ins.then_inc(sem("kv_diag_done"), 1)

            def msg(c, past):
                ch = Chain(dve, sem("msg_step"), c * K4)
                dve.wait_ge(sem("msg_mm"), c * K4 + K4)
                dve.wait_ge(sem("x3_b2_done"), c)
                for k in range(0, K4, 2):
                    both = ps[:, MSG_BANKS[k]:MSG_BANKS[k] + 2, 0:KC * MSGW].rearrange("p k (g n) -> p k g n", g=KC)
                    ch.link(V.tensor_scalar(denom[:, k:k + 2, :, :], both[:, :, :, HG * DG:MSGW], EPS_ATTN, None, ALU.add))
                    ch.link(V.reciprocal(denom[:, k:k + 2, :, :], denom[:, k:k + 2, :, :]))
                    for i in range(2):
                        ins = V.tensor_tensor(x3[:, k + i, :].rearrange("p (g h d) -> p g h d", g=KC, h=HG),
                                              both[:, i, :, 0:HG * DG].rearrange("p g (h d) -> p g h d", h=HG),
                                              denom[:, k + i, :, :].unsqueeze(3).broadcast_to([P, KC, HG, DG]), ALU.mult)
                ins.then_inc(sem("msg_read"), 1)
                dve.wait_ge(sem("msg_read"), c + 1)
                dve.wait_ge(sem("n2_loaded"), c * 16 + 16)
                V.tensor_tensor(x3[:, :, :], n2_in[:, :, :], x3[:, :, :], ALU.add).then_inc(sem("x3_done"), 1)
                dve.wait_ge(sem("x3_done"), c + 1)
                norm_stats("x3", blk(x3), c)

            def y_in(c, past):
                ch = Chain(dve, sem("y_step"), c)
                dve.wait_ge(sem("rstd_x3"), c + 1)
                dve.wait_ge(sem("yT_mm"), c)
                for k in range(K4):
                    ins = V.scalar_tensor_tensor(y[:, k, :], x3[:, k, :], mv["x3"][:, k, 0:1], W["g2"], ALU.subtract, ALU.mult)
                ch.link(ins)
                for k in range(K4):
                    ins = V.scalar_tensor_tensor(y[:, k, :], y[:, k, :], rstd["x3"][:, k:k + 1], W["be2"], ALU.mult, ALU.add)
                ins.then_inc(sem("y_in_done"), 1)

            def o_layer(c, past):
                dve.wait_ge(sem("proj_mm"), c * K4 + K4)
                dve.wait_ge(sem("x3_b2_done"), c + 1)
                V.tensor_tensor(flat(o), wide(6, 2), flat(o), ALU.add).then_inc(sem("o_done"), 1)
                dve.wait_ge(sem("o_done"), c + 1)
                norm_stats("o", blk(o), c)

            def x4_layer(c, past):
                dve.wait_ge(sem("x4_kept"), c)
                norm_apply("o", blk(x4), blk(o), c).then_inc(sem("o_normed"), 1)
                dve.wait_ge(sem("o_normed"), c + 1)
                dve.wait_ge(sem("x2_loaded"), c * 16 + 16)
                V.tensor_tensor(x4[:, :, :], x2_in[:, :, :], x4[:, :, :], ALU.add).then_inc(sem("x4_done"), 1)
                dve.wait_ge(sem("x4_done"), c + 1)
                norm_stats("x4", blk(x4), c)

            def n4_layer(c, past):
                dve.wait_ge(sem("nT_mm"), c)
                norm_apply("x4", blk(n4), blk(x4), c).then_inc(sem("n4_done"), 1)

            def n4_low(c, past):
                dve.wait_ge(sem("n4_high"), c + 1)
                V.scalar_tensor_tensor(n4T16[:, 1, :, :].rearrange("p a n -> p (a n)"), wide(0, 2), NORM_SCALE, n4T16[:, 0, :, :].rearrange("p a n -> p (a n)"),
                                       ALU.mult, ALU.subtract).then_inc(sem("n4T_done"), 1)

            def up(m, exact16):
                def f(c, past):
                    dve.wait_ge(sem("silu_done"), c * M2 + m + 1)
                    dve.wait_ge(sem("up_mm"), c * M2 + m + 1)
                    if m == 0:
                        dve.wait_ge(sem("down_mm"), c * K4)
                    dst = gate[:, m % 2, :] if exact16 else gated[:, m, :]
                    V.scalar_tensor_tensor(dst, ps[:, up_bank(m) + 1, :], DEQUANT / NORM_SCALE * HIDDEN_SCALE if exact16 else DEQUANT, gate[:, m % 2, :],
                                           ALU.mult, ALU.mult).then_inc(sem("up_read"), 1)
                return f

            def low(m):
                def f(c, past):
                    dve.wait_ge(sem("gated_high"), c * M2 + m + 1)
                    V.tensor_tensor(gated16[:, 1, m, :], gate[:, m % 2, :], gated16[:, 0, m, :], ALU.subtract).then_inc(sem("gated_done"), 1)
                return f

            ffn_blk = lambda k: blocks(4)[:, k, :]

            def ffn_stats(exact16):
                def f(c, past):
                    dve.wait_ge(sem("down_mm"), c * K4 + K4)
                    norm_stats("ffn", ffn_blk, c, EPS / (DEQUANT / (HIDDEN_SCALE if exact16 else 1.0)) ** 2)
                return f

            def finish(c, past):
                dve.wait_ge(sem("stored"), c * 16)
                norm_apply("ffn", blk(y_out), ffn_blk, c).then_inc(sem("ffn_read"), 1)
                dve.wait_ge(sem("ffn_read"), c + 1)
                dve.wait_ge(sem("x4_kept"), c + 1)
                V.tensor_tensor(y_out[:, :, :], y_out[:, :, :], x4_kept[:, :, :], ALU.add).then_inc(sem("y_done"), 1)

            def program(exact16):
                stages = {"in0": in0, "in1": in1, "in2": in2, "mix": mix, "f": f_layer, "x2": x2_layer, "n2": n2_layer, "u": u_layer,
                          "k_low": k_low, "k_feat": k_features, "q_low": q_low, "q_feat": q_features, "kv": kv, "diag": diag, "msg": msg, "y": y_in,
                          "o": o_layer, "x4": x4_layer, "n4": n4_layer, "ffn": ffn_stats(exact16), "out": finish,
                          **{f"up{m}": up(m, exact16) for m in range(M2)}}
                if exact16:
                    stages |= {"n4_low": n4_low, **{f"low{m}": low(m) for m in range(M2)}}
                run(dve, [stage for stage in DVE_ORDER if stage in stages], stages)

            is_narrow = dve.value_load(narrow[0:1, 0:1], min_val=0, max_val=1)
            with dve.If(is_narrow > 0):
                program(True)
            with dve.Else():
                program(False)


def transformer(nc, x, rot, ent, floats, ints, rows, out):
    with ExitStack() as ctx:
        sb = lambda n, s: ctx.enter_context(nc.sbuf_tensor(n, s, F32))
        weight_mem = sb("weight_mem", [P, FLOAT_COLS + INT_COLS])
        row_mem = sb("row_mem", [P, len(ROWS), C])
        ident = sb("ident", [P, P])
        narrow = ctx.enter_context(nc.sbuf_tensor("narrow", [P, 1], I32))
        heads_dram = nc.dram_tensor("heads_dram", [NHD, P, BB * D], F32, kind="Internal").ap()
        W, at = {}, 0
        for name, k, n in FLOAT_WEIGHTS + INT_WEIGHTS:
            W[name] = weight_mem[:, at:at + k * n].rearrange("p (k n) -> p k n", k=k)
            at += k * n
        for i, name in enumerate(ROWS):
            W[name] = row_mem[:, i, :]
        int_weights = weight_mem[:, FLOAT_COLS:]
        W16, at = {"all": int_weights.bitcast(FP16)[:, 0:INT_COLS]}, 0
        for name, k, n in INT_WEIGHTS:
            W16[name] = W16["all"][:, at:at + k * n].rearrange("p (k n) -> p k n", k=k)
            at += k * n
        softmax_attention(nc, x, rot, ent, floats, ints, rows, weight_mem, row_mem, narrow, ident, heads_dram)
        later_layers(nc, heads_dram, x, W, W16, int_weights, narrow, ident, out)


def kernel(**inputs):
    import numpy as np
    import concourse.bacc as bacc
    from concourse.bass_utils import run_bass_kernel_spmd

    def on_partitions(w):
        k = w.shape[0] // P
        return w.reshape(k, P, -1).transpose(1, 0, 2).reshape(P, -1)

    a = {name: np.asarray(v) for name, v in inputs.items()}
    vec = lambda name: a[name].reshape(-1, P).T
    mat = lambda *names: on_partitions(np.concatenate([a[n].T for n in names], axis=1))
    arrays = {
        "in_x_dram": a["L0_attn_inputs"],
        "in_rot_dram": a["L0_attn_rotation_params"],
        "in_ent_dram": a["L0_attn_entangle_params"],
        "in_floats_dram": np.concatenate([mat("L0_ffn_W_r"), mat("L0_ffn_W_k"), mat("L0_ffn_W_v"), mat("L1_attn_wq"), mat("L1_attn_wk", "L1_attn_wv"),
                                          mat("L1_attn_w1"), mat("L1_attn_w2"), vec("L0_ffn_mu_r"), vec("L0_ffn_mu_k"), vec("L1_attn_b1")], axis=1),
        "in_ints_dram": np.concatenate([mat("L1_ffn_w_gate"), mat("L1_ffn_w_up"), mat("L1_ffn_w_down")], axis=1),
        "in_rows_dram": np.concatenate([a["L1_attn_" + n] for n in ROWS]),
    }
    arrays = {n: np.ascontiguousarray(v) for n, v in arrays.items()}
    nc = bacc.Bacc("TRN2", target_bir_lowering=False, num_devices=1)
    args = [nc.dram_tensor(n, v.shape, mybir.dt.from_np(v.dtype), kind="ExternalInput").ap() for n, v in arrays.items()]
    out = nc.dram_tensor("out_0_dram", (B, T, C), F32, kind="ExternalOutput").ap()
    transformer(nc, *args, out)
    r = run_bass_kernel_spmd(nc, [arrays], core_ids=[0])
    return r.results[0]["out_0_dram"]
```
